# Optimizing a Trainium2 kernel written in Bass

```python
import numpy as np
import jax
import jax.numpy as jnp

def _softmax(x, axis=-1):
    return jax.nn.softmax(x, axis=axis)

def _gelu(x):
    return jax.nn.gelu(x, approximate=True)

def _silu(x):
    return jax.nn.silu(x)

def _sigmoid(x):
    return jax.nn.sigmoid(x)

def _layernorm(x, axis=-1, eps=1e-05):
    m = jnp.mean(x, axis=axis, keepdims=True)
    v = jnp.var(x, axis=axis, keepdims=True)
    return (x - m) / jnp.sqrt(v + eps)

def _scatter_add(tgt, idx, src, axis=0):
    return tgt.at[idx].add(src)

def _segment_sum(src, seg, n):
    return jax.ops.segment_sum(src, seg, n)
kernel_name = 'mk_gnn_resnorm_d4_gnn_r32_527dfa'

def setup_inputs(seed: int=0):
    np.random.seed(seed)
    _w = jnp.asarray

    def _rec_inputs():
        import jax
        import jax.numpy as jnp
        _gk = jax.random.key(seed)
        x = -0.0003713 + 1 * jax.random.normal(jax.random.fold_in(_gk, 1), (3125, 128), jnp.float32)
        _s = jax.random.randint(jax.random.fold_in(_gk, 2), (25000,), 0, 3125, jnp.int32)
        _d = jax.random.randint(jax.random.fold_in(_gk, 3), (25000,), 0, 3125, jnp.int32)
        _loop = jnp.arange(3125, dtype=jnp.int32)
        src = jnp.concatenate([_s, _d, _loop])
        dst = jnp.concatenate([_d, _s, _loop])
        _o = jnp.argsort(dst, stable=True)
        src = src[_o]
        dst = dst[_o]
        edge_type_2 = jax.random.randint(jax.random.fold_in(_gk, 13), (53125,), 0, 2, jnp.int32)
        edge_type_4 = jax.random.randint(jax.random.fold_in(_gk, 14), (53125,), 0, 4, jnp.int32)
        edge_type_8 = jax.random.randint(jax.random.fold_in(_gk, 15), (53125,), 0, 8, jnp.int32)
        return (x, src, dst, edge_type_2, edge_type_4, edge_type_8)
    x, src, dst, edge_type_2, edge_type_4, edge_type_8 = _rec_inputs()

    def _L0_gnn_setup():
        import jax, jax.numpy as jnp
        import numpy as np
        N = 3125
        E = 18750
        NFEAT = 128
        NHID = 128
        BN_EPS = 1e-05

        def _spectral_normalize(W, n_iter=30):
            u = jnp.full((W.shape[0],), 1.0 / np.sqrt(W.shape[0]), W.dtype)

            def body(_, u):
                v = W.T @ u
                v = v / (jnp.linalg.norm(v) + 1e-12)
                u = W @ v
                u = u / (jnp.linalg.norm(u) + 1e-12)
                return u
            u = jax.lax.fori_loop(0, n_iter, body, u)
            v = W.T @ u
            v = v / (jnp.linalg.norm(v) + 1e-12)
            u = jax.lax.stop_gradient(u)
            v = jax.lax.stop_gradient(v)
            sigma = u @ (W @ v)
            return W / sigma
        key = jax.random.key(seed)
        ks = jax.random.split(key, 8)
        x = jax.random.normal(ks[0], (N, NFEAT), dtype=jnp.float32)
        edge_index = jax.random.randint(ks[1], (2, E), 0, N, dtype=jnp.int32)
        W1 = jax.random.normal(ks[2], (NHID, NFEAT), dtype=jnp.float32) * 0.05
        b1 = jax.random.normal(ks[3], (NHID,), dtype=jnp.float32) * 0.05
        gamma = jnp.ones((NHID,), dtype=jnp.float32)
        beta = jnp.zeros((NHID,), dtype=jnp.float32)
        W2 = jax.random.normal(ks[4], (NHID, NHID), dtype=jnp.float32) * 0.05
        b2 = jax.random.normal(ks[5], (NHID,), dtype=jnp.float32) * 0.05
        return {'x': x, 'edge_index': edge_index, 'W1': W1, 'b1': b1, 'gamma': gamma, 'beta': beta, 'W2': W2, 'b2': b2}
    _L0_gnn_all = _L0_gnn_setup()
    _L0_gnn_in = {k: v for k, v in _L0_gnn_all.items() if k in ('W1', 'b1', 'gamma', 'beta', 'W2', 'b2')}
    del _L0_gnn_all

    def _L1_gnn_setup():
        import jax, jax.numpy as jnp
        import numpy as np
        IN_DIM = 128
        OUT_DIM = 128
        N_NODES = 10000
        N_EDGES = 20000
        key = jax.random.key(seed)
        ks = jax.random.split(key, 9)
        X = jax.random.normal(ks[0], (N_NODES, IN_DIM), dtype=jnp.float32)
        edge_index = jax.random.randint(ks[1], (2, N_EDGES), 0, N_NODES, dtype=jnp.int64)
        edge_types = jax.random.randint(ks[2], (N_EDGES,), 0, 2, dtype=jnp.int64)
        s = 1.0 / np.sqrt(IN_DIM)
        W_data = jax.random.uniform(ks[3], (OUT_DIM, IN_DIM), minval=-s, maxval=s, dtype=jnp.float32)
        b_data = jax.random.uniform(ks[4], (OUT_DIM,), minval=-s, maxval=s, dtype=jnp.float32)
        W_control = jax.random.uniform(ks[5], (OUT_DIM, IN_DIM), minval=-s, maxval=s, dtype=jnp.float32)
        b_control = jax.random.uniform(ks[6], (OUT_DIM,), minval=-s, maxval=s, dtype=jnp.float32)
        W_self = jax.random.uniform(ks[7], (OUT_DIM, IN_DIM), minval=-s, maxval=s, dtype=jnp.float32)
        b_self = jax.random.uniform(ks[8], (OUT_DIM,), minval=-s, maxval=s, dtype=jnp.float32)
        return {'X': X, 'edge_index': edge_index, 'edge_types': edge_types, 'W_data': W_data, 'b_data': b_data, 'W_control': W_control, 'b_control': b_control, 'W_self': W_self, 'b_self': b_self}
    _L1_gnn_all = _L1_gnn_setup()
    _L1_gnn_in = {k: v for k, v in _L1_gnn_all.items() if k in ('W_data', 'b_data', 'W_control', 'b_control', 'W_self', 'b_self')}
    del _L1_gnn_all

    def _L2_gnn_setup():
        import jax, jax.numpy as jnp
        import numpy as np
        N_NODES = 50000
        N_EDGES = 18750
        IN_F = 128
        OUT_F = 128
        N_REL = 4
        SLOPE = 0.2

        def _gat_relation(x, src, dst, rel_mask, W, b, a_src, a_dst, n):
            h = x @ W
            s_score = h @ a_src
            d_score = h @ a_dst
            e_logit = jax.nn.leaky_relu(s_score[src] + d_score[dst], SLOPE)
            e_logit = jnp.where(rel_mask, e_logit, -jnp.inf)
            sl_logit = jax.nn.leaky_relu(s_score + d_score, SLOPE)
            seg = jnp.concatenate([dst, jnp.arange(n, dtype=dst.dtype)])
            logits = jnp.concatenate([e_logit, sl_logit])
            m = jax.ops.segment_max(logits, seg, num_segments=n)
            p = jnp.exp(logits - m[seg])
            denom = jax.ops.segment_sum(p, seg, num_segments=n)
            feats = jnp.concatenate([h[src], h], axis=0)
            num = jax.ops.segment_sum(p[:, None] * feats, seg, num_segments=n)
            return num / denom[:, None] + b
        key = jax.random.key(seed)
        ks = jax.random.split(key, 10)
        x = jax.random.normal(ks[0], (N_NODES, IN_F), dtype=jnp.float32)
        edge_index = jax.random.randint(ks[1], (2, N_EDGES), 0, N_NODES, dtype=jnp.int64)
        edge_type = jax.random.randint(ks[2], (N_EDGES,), 0, N_REL, dtype=jnp.int64)
        s = 1.0 / np.sqrt(IN_F)
        W_self = jax.random.uniform(ks[3], (IN_F, OUT_F), jnp.float32, -s, s)
        b_self = jax.random.uniform(ks[4], (OUT_F,), jnp.float32, -s, s)
        W_rel = jax.random.normal(ks[5], (N_REL, IN_F, OUT_F), dtype=jnp.float32) * s
        b_rel = jnp.zeros((N_REL, OUT_F), dtype=jnp.float32)
        att_src = jax.random.normal(ks[6], (N_REL, OUT_F), dtype=jnp.float32) * s
        att_dst = jax.random.normal(ks[7], (N_REL, OUT_F), dtype=jnp.float32) * s
        return {'x': x, 'edge_index': edge_index, 'edge_type': edge_type, 'W_self': W_self, 'b_self': b_self, 'W_rel': W_rel, 'b_rel': b_rel, 'att_src': att_src, 'att_dst': att_dst}
    _L2_gnn_all = _L2_gnn_setup()
    _L2_gnn_in = {k: v for k, v in _L2_gnn_all.items() if k in ('W_self', 'b_self', 'W_rel', 'b_rel', 'att_src', 'att_dst')}
    del _L2_gnn_all

    def _L3_gnn_setup():
        import jax, jax.numpy as jnp
        import numpy as np
        N_NODES = 3125
        N_EDGES = 18750
        IN_FEAT = 128
        OUT_FEAT = 128
        NUM_RELS = 8
        NUM_BASES = 4
        key = jax.random.key(seed)
        ks = jax.random.split(key, 8)
        h = jax.random.normal(ks[0], (N_NODES, IN_FEAT), dtype=jnp.float32)
        weight = jax.random.normal(ks[1], (NUM_BASES, IN_FEAT, OUT_FEAT), dtype=jnp.float32) * (1.0 / np.sqrt(IN_FEAT))
        w_comp = jax.random.normal(ks[2], (NUM_RELS, NUM_BASES), dtype=jnp.float32) * (1.0 / np.sqrt(NUM_BASES))
        root_weight = jax.random.normal(ks[3], (IN_FEAT, OUT_FEAT), dtype=jnp.float32) * (1.0 / np.sqrt(IN_FEAT))
        bias = jnp.zeros((OUT_FEAT,), dtype=jnp.float32)
        src = jax.random.randint(ks[4], (N_EDGES,), 0, N_NODES, dtype=jnp.int32)
        dst = jax.random.randint(ks[5], (N_EDGES,), 0, N_NODES, dtype=jnp.int32)
        rel_type = jax.random.randint(ks[6], (N_EDGES,), 0, NUM_RELS, dtype=jnp.int32)
        return {'h': h, 'weight': weight, 'w_comp': w_comp, 'root_weight': root_weight, 'bias': bias, 'src': src, 'dst': dst, 'rel_type': rel_type}
    _L3_gnn_all = _L3_gnn_setup()
    _L3_gnn_in = {k: v for k, v in _L3_gnn_all.items() if k in ('weight', 'w_comp', 'root_weight', 'bias')}
    del _L3_gnn_all
    return {'x': x, 'src': src, 'dst': dst, 'edge_type_2': edge_type_2, 'edge_type_4': edge_type_4, 'edge_type_8': edge_type_8, 'L0_gnn_W1': _L0_gnn_in['W1'], 'L0_gnn_b1': _L0_gnn_in['b1'], 'L0_gnn_gamma': _L0_gnn_in['gamma'], 'L0_gnn_beta': _L0_gnn_in['beta'], 'L0_gnn_W2': _L0_gnn_in['W2'], 'L0_gnn_b2': _L0_gnn_in['b2'], 'L1_gnn_W_data': _L1_gnn_in['W_data'], 'L1_gnn_b_data': _L1_gnn_in['b_data'], 'L1_gnn_W_control': _L1_gnn_in['W_control'], 'L1_gnn_b_control': _L1_gnn_in['b_control'], 'L1_gnn_W_self': _L1_gnn_in['W_self'], 'L1_gnn_b_self': _L1_gnn_in['b_self'], 'L2_gnn_W_self': _L2_gnn_in['W_self'], 'L2_gnn_b_self': _L2_gnn_in['b_self'], 'L2_gnn_W_rel': _L2_gnn_in['W_rel'], 'L2_gnn_b_rel': _L2_gnn_in['b_rel'], 'L2_gnn_att_src': _L2_gnn_in['att_src'], 'L2_gnn_att_dst': _L2_gnn_in['att_dst'], 'L3_gnn_weight': _L3_gnn_in['weight'], 'L3_gnn_w_comp': _L3_gnn_in['w_comp'], 'L3_gnn_root_weight': _L3_gnn_in['root_weight'], 'L3_gnn_bias': _L3_gnn_in['bias']}

def reference(x, src, dst, edge_type_2, edge_type_4, edge_type_8, L0_gnn_W1, L0_gnn_b1, L0_gnn_gamma, L0_gnn_beta, L0_gnn_W2, L0_gnn_b2, L1_gnn_W_data, L1_gnn_b_data, L1_gnn_W_control, L1_gnn_b_control, L1_gnn_W_self, L1_gnn_b_self, L2_gnn_W_self, L2_gnn_b_self, L2_gnn_W_rel, L2_gnn_b_rel, L2_gnn_att_src, L2_gnn_att_dst, L3_gnn_weight, L3_gnn_w_comp, L3_gnn_root_weight, L3_gnn_bias):
    import jax
    import jax.numpy as jnp

    def _L0_gnn_ref(x, edge_index, W1, b1, gamma, beta, W2, b2):
        import jax, jax.numpy as jnp
        import numpy as np
        N = 3125
        E = 18750
        NFEAT = 128
        NHID = 128
        BN_EPS = 1e-05

        def _spectral_normalize(W, n_iter=30):
            u = jnp.full((W.shape[0],), 1.0 / np.sqrt(W.shape[0]), W.dtype)

            def body(_, u):
                v = W.T @ u
                v = v / (jnp.linalg.norm(v) + 1e-12)
                u = W @ v
                u = u / (jnp.linalg.norm(u) + 1e-12)
                return u
            u = jax.lax.fori_loop(0, n_iter, body, u)
            v = W.T @ u
            v = v / (jnp.linalg.norm(v) + 1e-12)
            u = jax.lax.stop_gradient(u)
            v = jax.lax.stop_gradient(v)
            sigma = u @ (W @ v)
            return W / sigma
        src, dst = (edge_index[0], edge_index[1])
        agg = jax.ops.segment_sum(x[src], dst, num_segments=N)
        h = agg + x
        h = h @ _spectral_normalize(W1).T + b1
        h = jax.nn.relu(h)
        mean = h.mean(axis=0)
        var = h.var(axis=0)
        h = (h - mean) / jnp.sqrt(var + BN_EPS) * gamma + beta
        h = h @ _spectral_normalize(W2).T + b2
        return h

    def _L1_gnn_ref(X, edge_index, edge_types, W_data, b_data, W_control, b_control, W_self, b_self):
        import jax, jax.numpy as jnp
        import numpy as np
        IN_DIM = 128
        OUT_DIM = 128
        N_NODES = 10000
        N_EDGES = 20000
        src, dst = (edge_index[0], edge_index[1])
        Xs = X[src]
        m_data = Xs @ W_data.T + b_data
        m_ctrl = Xs @ W_control.T + b_control
        msg = jnp.where((edge_types == 0)[:, None], m_data, m_ctrl)
        agg = jax.ops.segment_sum(msg, dst, num_segments=X.shape[0])
        out = agg + (X @ W_self.T + b_self)
        return jax.nn.relu(out)

    def _L2_gnn_ref(x, edge_index, edge_type, W_self, b_self, W_rel, b_rel, att_src, att_dst):
        import jax, jax.numpy as jnp
        import numpy as np
        N_NODES = 50000
        N_EDGES = 18750
        IN_F = 128
        OUT_F = 128
        N_REL = 4
        SLOPE = 0.2

        def _gat_relation(x, src, dst, rel_mask, W, b, a_src, a_dst, n):
            h = x @ W
            s_score = h @ a_src
            d_score = h @ a_dst
            e_logit = jax.nn.leaky_relu(s_score[src] + d_score[dst], SLOPE)
            e_logit = jnp.where(rel_mask, e_logit, -jnp.inf)
            sl_logit = jax.nn.leaky_relu(s_score + d_score, SLOPE)
            seg = jnp.concatenate([dst, jnp.arange(n, dtype=dst.dtype)])
            logits = jnp.concatenate([e_logit, sl_logit])
            m = jax.ops.segment_max(logits, seg, num_segments=n)
            p = jnp.exp(logits - m[seg])
            denom = jax.ops.segment_sum(p, seg, num_segments=n)
            feats = jnp.concatenate([h[src], h], axis=0)
            num = jax.ops.segment_sum(p[:, None] * feats, seg, num_segments=n)
            return num / denom[:, None] + b
        n = x.shape[0]
        src, dst = (edge_index[0], edge_index[1])
        out = x @ W_self + b_self
        for r in range(N_REL):
            out = out + _gat_relation(x, src, dst, edge_type == r, W_rel[r], b_rel[r], att_src[r], att_dst[r], n)
        return out

    def _L3_gnn_ref(h, weight, w_comp, root_weight, bias, src, dst, rel_type):
        import jax, jax.numpy as jnp
        import numpy as np
        N_NODES = 3125
        N_EDGES = 18750
        IN_FEAT = 128
        OUT_FEAT = 128
        NUM_RELS = 8
        NUM_BASES = 4
        B, I, O = weight.shape
        R = w_comp.shape[0]
        W = (w_comp @ weight.reshape(B, I * O)).reshape(R, I, O)
        proj = jnp.einsum('ni,rio->nro', h, W)
        msg = proj[src, rel_type]
        agg = jax.ops.segment_sum(msg, dst, num_segments=h.shape[0])
        out = h @ root_weight + agg + bias
        return jax.nn.relu(out)
    edge_index = jnp.stack([src, dst])
    x = _layernorm(x + _L0_gnn_ref(x, edge_index, L0_gnn_W1, L0_gnn_b1, L0_gnn_gamma, L0_gnn_beta, L0_gnn_W2, L0_gnn_b2), axis=-1)
    x = _layernorm(x + _L1_gnn_ref(x, edge_index, edge_type_2, L1_gnn_W_data, L1_gnn_b_data, L1_gnn_W_control, L1_gnn_b_control, L1_gnn_W_self, L1_gnn_b_self), axis=-1)
    x = _layernorm(x + _L2_gnn_ref(x, edge_index, edge_type_4, L2_gnn_W_self, L2_gnn_b_self, L2_gnn_W_rel, L2_gnn_b_rel, L2_gnn_att_src, L2_gnn_att_dst), axis=-1)
    x = _layernorm(x + _L3_gnn_ref(x, L3_gnn_weight, L3_gnn_w_comp, L3_gnn_root_weight, L3_gnn_bias, src, dst, edge_type_8), axis=-1)
    return x

_drawn_inputs = setup_inputs


def setup_inputs(seed=0):
    import zlib

    import numpy as np

    out = dict(_drawn_inputs(seed))
    spreads = {'L0_gnn_gamma': (1.0, 0.2),
     'L0_gnn_beta': (0.0, 0.1),
     'L2_gnn_b_rel': (0.0, 0.1),
     'L3_gnn_bias': (0.0, 0.331)}
    factors = {'L0_gnn_b1': 6.791}
    for name, (base, spread) in spreads.items():
        noise = np.random.default_rng([zlib.crc32(name.encode()), seed]).standard_normal(out[name].shape)
        drawn = base * np.exp(spread * noise) if base else spread * noise
        out[name] = jnp.asarray(drawn.astype(out[name].dtype))
    for name, factor in factors.items():
        out[name] = (out[name] * factor).astype(out[name].dtype)
    return out
```

```python
from contextlib import ExitStack

import concourse.bass as bass
from concourse import mybir

ALU = mybir.AluOpType
ACT = mybir.ActivationFunctionType
F32 = mybir.dt.float32
BF16 = mybir.dt.bfloat16
I32 = mybir.dt.int32
AX = mybir.AxisListType.X

P = 128
EPS = 1e-05
TINY = 1e-12
SLOPE = 0.2
POWER_STEPS = 30


class Chain:

    def __init__(self, eng, sem, steps=None):
        self.eng, self.sem, self.steps, self.base, self.k = eng, sem, steps, 0, 0

    def begin(self, round_number):
        assert self.steps is not None and self.k in (0, self.steps), (self.k, self.steps)
        self.base, self.k = round_number * self.steps, 0

    def did(self, instruction):
        self.k += 1
        instruction.then_inc(self.sem, 1)

    def wait(self):
        self.eng.wait_ge(self.sem, self.base + self.k)

    def link(self, instruction):
        self.did(instruction)
        self.wait()


def build_gnn(nc, a, out, upto=3):
    N, F = a["x"].shape
    E = a["src"].shape[0]
    R1, R2, R3, NBASE = 2, a["L2_gnn_W_rel"].shape[0], a["L3_gnn_w_comp"].shape[0], a["L3_gnn_weight"].shape[0]
    assert F == P
    NB = -(-N // P)
    NPAD = NB * P
    LAST = N - (NB - 1) * P
    TB = E // N
    LEAD = TB // 2
    SLOTS = NB * TB
    ROWS = -(-E // P)
    REST = E - (ROWS - 1) * P
    assert LEAD + ROWS <= SLOTS
    NCH = 4
    RC = ROWS // NCH
    assert RC * NCH == ROWS and RC <= P
    RING = NB + 1 + (NB + 1) % 2
    SHIFTS = RING // 2
    PAIR = 2 * P
    SPAN = RING * P
    ACCT = 2 * RING
    NOBODY = 1 << 20
    GW = F + 4
    BATCH = 5
    NBATCH = NB // BATCH
    assert NBATCH * BATCH == NB and NB % 2 == 1
    SW = R2 * 3 + 4

    t1 = nc.dram_tensor("table1", (R1 * NPAD, F), F32).ap()
    t2 = nc.dram_tensor("table2", (R2 * NPAD, GW), F32).ap()
    t3 = nc.dram_tensor("table3", (R3 * NPAD, F), F32).ap()
    kept = nc.dram_tensor("kept_rows", (NB, P, TB * GW), F32).ap()

    with ExitStack() as ctx:
        def sb(name, shape, dt=F32):
            return ctx.enter_context(nc.sbuf_tensor(name, shape, dt))

        def sem(name):
            return ctx.enter_context(nc.semaphore(name))

        psum = ctx.enter_context(nc.psum_tensor("psum", [P, 8, 512], F32))
        bank = [psum[:, i, :] for i in range(8)]

        X = sb("X", [P, NB, F])
        S = sb("S", [P, NB, F])
        acc = sb("acc", [P, ACCT * P])
        featT = acc[:, P:P + NPAD]
        ring = sb("ring", [P, 2, TB, GW])
        onehot = sb("onehot", [P, TB, PAIR])
        idx_stage = sb("idx_stage", [P, 2, TB], I32)
        key_stage = sb("key_stage", [P, TB])
        key_wrap = sb("key_wrap", [P, TB])
        iota = sb("iota", [P, PAIR])
        prow = sb("prow", [P, 1])
        ident = sb("ident", [P, P])
        ones = sb("ones", [P, P])
        block_base = sb("block_base", [P, NB])
        edge_rows = ring[0:RC].rearrange("p h k g -> p (h k g)")[:, 0:5 * NCH * P].bitcast(I32).rearrange(
            "p (a q e) -> p a q e", a=5, q=NCH)
        edge_rows_f = onehot[0:RC].rearrange("p t n -> p (t n)")[:, 0:5 * NCH * P].rearrange(
            "p (a q e) -> p a q e", a=5, q=NCH)
        tab = sb("tab", [P, 5, SLOTS])
        idx = sb("idx", [P, 4, SLOTS], I32)
        key0 = sb("key0", [P, NB, TB])
        key_w = sb("key_w", [P, NB, TB])
        in_pair = sb("in_pair", [P, 1])
        count = sb("count", [1, 2])
        shifts = sb("shifts", [1, 1], I32)
        wraw = sb("wraw", [P, 7 + R2 + NBASE, F])
        wT = sb("wT", [P, 5 + R2, F])
        small = sb("small", [3 + 2 * R2, F])
        smallT = sb("smallT", [P, 3 + 2 * R2])
        rows_b = sb("rows_b", [P, 6 + R2, F])
        wcomp = sb("wcomp", [P, R3 * NBASE])
        wcat2 = sb("wcat2", [P, F + 2 * R2])
        wcat3 = sb("wcat3", [P, R3, F])
        tb = sb("tb", [P, BATCH, R3 * F])
        XT = tb[:, :, :].rearrange("p a b -> p (a b)")[:, 0:NPAD]
        stg = sb("stg", [P, BATCH, F])
        y = sb("y", [P, BATCH, F])
        xn = sb("xn", [P, BATCH, F])
        xt = sb("xt", [P, BATCH, F])
        st6 = sb("st6", [P, BATCH, 6])
        mv = sb("mv", [P, BATCH, 2])
        rstd = sb("rstd", [P, BATCH])
        eps = sb("eps", [P, 1])
        u = sb("u", [P, 2])
        v = sb("v", [P, 2])
        raw = sb("raw", [P, 2])
        sq = sb("sq", [P, 2])
        nrm = sb("nrm", [P, 2])
        inv_sigma = sb("inv_sigma", [P, 2])
        NCHK = -(-N // 512)
        bn6 = sb("bn6", [P, NCHK, 6])
        bnmv = sb("bnmv", [P, 2])
        bn_scale = sb("bn_scale", [P, 1])
        bn_shift = sb("bn_shift", [P, 1])

        pads_set = sem("pads_set")
        edges_in = sem("edges_in")
        x_in = sem("x_in")
        weights_in = sem("weights_in")
        iota_set = sem("iota_set")
        v_prep = sem("v_prep")
        edges_f = sem("edges_f")
        edge_tr = sem("edge_tr")
        edge_ev = sem("edge_ev")
        ident_set = sem("ident_set")
        idx_ready = sem("idx_ready")
        match_summed = sem("match_summed")
        match_total = sem("match_total")
        shifts_ready = sem("shifts_ready")
        w_tr = sem("w_tr")
        w_ev = sem("w_ev")
        x_tr = sem("x_tr")
        x_ev = sem("x_ev")
        wa_done = sem("wa_done")
        weights_ready = sem("weights_ready")
        pw_pe = sem("pw_pe")
        pw_act = sem("pw_act")
        pw_v = sem("pw_v")
        out_stored = sem("out_stored")
        dve_turn = sem("dve_turn")

        def blocks(eng, body):
            with eng.Fori(0, NB // 2) as m:
                body(2 * m, 0, m)
                body(2 * m + 1, 1, m)
            body(NB - 1, 0, NB // 2)

        USES = [NB - NB // 2, NB // 2]
        staged = [sem(f"staged{h}") for h in range(2)]
        gathered = [sem(f"gathered{h}") for h in range(2)]
        pool_go = sem("pool_go")

        class Pass:
            def __init__(self, n, table, idx_row, width):
                self.n, self.table, self.idx_row, self.width = n, table, idx_row, width
                self.staged, self.gathered, self.go = staged, gathered, pool_go
                self.hot = sem(f"hot{n}")
                self.summed = sem(f"summed{n}")
                self.acc_done = sem(f"acc_done{n}")
                if n != 2:
                    self.key_staged = sem(f"key_staged{n}")
                    self.key_shift = sem(f"key_shift{n}")
                    self.acc_zero = sem(f"acc_zero{n}")
                if n:
                    self.ready = sem(f"table_ready{n}")

            def staged_by(self, h, m):
                return m + (1 + self.n * USES[h])

            def gathered_by(self, h, m):
                return (m + (1 + self.n * USES[h])) * (16 * TB)

        passes = [Pass(0, a["x"], 0, F), Pass(1, t1, 1, F), Pass(2, t2, 2, GW), Pass(3, t3, 3, F)]

        def stage_indices(eng, ps, S_, free):
            def stage(n, h):
                nc.scalar.copy(idx_stage[:, h, :], idx[:, ps.idx_row, bass.ds(n * TB, TB)]).then_inc(ps.staged[h], 1)
            eng.wait_ge(idx_ready, 1)
            stage(0, 0)
            stage(1, 1)
            with eng.Fori(0, NB // 2 - 1) as m:
                for h in range(2):
                    free(2 * m + h, h, m)
                    stage(2 * m + 2 + h, h)
            free(NB - 3, 0, NB // 2 - 1)
            stage(NB - 1, 0)

        def gather_pass(pool, ps):
            def block(n, h, m):
                pool.wait_ge(ps.staged[h], ps.staged_by(h, m))
                pool.sem_inc(ps.go, 1)
                for k in range(TB):
                    pool.indirect_dma_start(
                        ring[:, h, k, 0:ps.width], None, ps.table,
                        bass.IndirectOffsetOnAxis(ap=idx_stage[:, h, k:k + 1], axis=0)).then_inc(ps.gathered[h], 16)
            blocks(pool, block)

        def sum_pass_pe(pe, ps, S_):
            def block(n, h, m):
                first = pe.snap(n * S_)
                with pe.Fori(0, S_) as s:
                    pe.wait_ge(ps.gathered[h], ps.gathered_by(h, m))
                    pe.wait_ge(ps.hot, first + s + 1)
                    pe.wait_ge(ps.acc_done, first + s)
                    for k in range(TB):
                        mm = nc.tensor.matmul(bank[0][:, 0:PAIR], ring[:, h, k, 0:F], onehot[:, k, :],
                                              start=(k == 0), stop=(k == TB - 1))
                    mm.then_inc(ps.summed, 1)
            blocks(pe, block)


        def onehots(hot, scalar2=None):
            for k in range(TB):
                w = None if scalar2 is None else scalar2[:, k:k + 1]
                made = nc.vector.tensor_scalar(hot[:, k, :], iota[:, :], key_stage[:, k:k + 1], w,
                                               ALU.is_equal, ALU.bypass if w is None else ALU.mult)
            return made

        def next_pair(dve, chain):
            chain.link(nc.vector.tensor_scalar(key_wrap[:, :], key_stage[:, :], float(PAIR), float(SPAN), ALU.is_lt, ALU.mult))
            chain.did(nc.vector.scalar_tensor_tensor(key_stage[:, :], key_stage[:, :], float(-PAIR), key_wrap[:, :], ALU.add, ALU.add))

        def sum_pass_dve(dve, ps, S_):
            nc.vector.memset(acc[:, :], 0.0).then_inc(ps.acc_zero, 1)
            dve.wait_ge(ps.acc_zero, 1)
            keys = Chain(dve, ps.key_shift, 2)

            def block(n, h, m):
                first = dve.snap(n * S_)
                dve.wait_ge(ps.key_shift, first * 2)
                nc.vector.tensor_copy(key_stage[:, :], row(key0, n)).then_inc(ps.key_staged, 1)
                with dve.Fori(0, S_) as s:
                    dve.wait_ge(ps.key_staged, n + 1)
                    keys.begin(first + s)
                    keys.wait()
                    onehots(onehot).then_inc(ps.hot, 1)
                    next_pair(dve, keys)
                    dve.wait_ge(ps.summed, first + s + 1)
                    dve.wait_ge(ps.acc_done, first + s)
                    sums = acc[:, bass.ds((n + 2 * s) * P, PAIR)]
                    nc.vector.tensor_tensor(sums, sums, bank[0][:, 0:PAIR], ALU.add).then_inc(ps.acc_done, 1)
            blocks(dve, block)

        def row(t, n):
            return t[:, bass.ds(n, 1), :].rearrange("p a k -> p (a k)")

        class Tail:
            def __init__(self, l):
                self.l = l
                self.uses = 2 if l == 2 else 1
                self.next = passes[l + 1] if l < 3 else None
                self.lhs = sem(f"lhs{l}")
                self.own = sem(f"own{l}")
                self.y_read = sem(f"y_read{l}")
                self.stats = sem(f"stats{l}")
                self.rooted = sem(f"rooted{l}")
                self.normed = sem(f"normed{l}")
                if l < 3:
                    self.x_kept = sem(f"x_kept{l}")
                    self.turned = sem(f"turned{l}")
                    self.turned_ev = sem(f"turned_ev{l}")
                    self.tabled = sem(f"tabled{l}")
                if l < 2:
                    self.ev_dve = sem(f"ev_dve{l}")
                if l in (1, 2):
                    self.ev_act = sem(f"ev_act{l}")
                self.chain = sem(f"tail_chain{l}")
                self.folded = sem(f"folded{l}")
                if l == 2:
                    self.h_in = sem(f"h_in{l}")

        tails = [Tail(l) for l in range(upto + 1)]
        psA = psum[:, 0:2, :].rearrange("p a b -> p (a b)")[:, 0:BATCH * F].rearrange("p (j f) -> p j f", f=F)
        psT = psum[:, 2:4, :].rearrange("p a b -> p (a b)")[:, 0:BATCH * F].rearrange("p (j f) -> p j f", f=F)
        SETS = [[4, 5], [6, 7]]
        h_self = ring[:, :, :, :].rearrange("p a b c -> p (a b c)")[:, 0:BATCH * R2 * GW].rearrange(
            "p (j r g) -> p j r g", j=BATCH, r=R2)

        def tile_batch(t, b):
            return t[:, bass.ds(b * BATCH, BATCH), :]

        def fold(dve, ps, tl, S_):
            dve.wait_ge(ps.acc_done, NB * S_)
            nc.vector.tensor_tensor(featT, featT, acc[:, (RING + 1) * P:(RING + 1) * P + NPAD], ALU.add).then_inc(tl.folded, 1)

        def tail_act(act, tl):
            l = tl.l
            act.wait_ge(tl.folded, 1)
            with act.Fori(0, NBATCH) as b:
                act.wait_ge(tl.own, b * tl.uses)
                src_ = featT[:, bass.ds(b * (BATCH * P), BATCH * P)]
                dst_ = stg[:, :, :].rearrange("p j f -> p (j f)")
                if l == 0:
                    nc.scalar.activation(dst_, src_, ACT.Identity, bias=bn_shift[:, :], scale=bn_scale[:, :]).then_inc(tl.lhs, 1)
                else:
                    nc.scalar.copy(dst_, src_).then_inc(tl.lhs, 1)
                act.wait_ge(tl.stats, b + 1)
                nc.scalar.activation(rstd[:, :], mv[:, :, 1], ACT.Sqrt, bias=eps[:, :]).then_inc(tl.rooted, 1)
                if l == 3:
                    return
                act.wait_ge(tl.normed, b + 1)
                nc.scalar.copy(tile_batch(X, b), xn[:, :, :]).then_inc(tl.x_kept, 1)
                act.wait_ge(tl.turned, b + 1)
                act.wait_ge(tl.tabled, b * BATCH)
                nc.scalar.copy(xt[:, :, :], psT).then_inc(tl.turned_ev, 1)
                if l == 0:
                    return
                act.wait_ge(tl.next.ready, b * (BATCH * 16))
                for j in range(BATCH):
                    act.wait_ge(tl.tabled, b * BATCH + (j + 1))
                    s0 = SETS[j % 2]
                    if l == 1:
                        tv = tb[:, j, 0:R2 * GW].rearrange("p (r g) -> p r g", r=R2)
                        nc.scalar.copy(tv[:, :, 0:F], bank[s0[0]].rearrange("p (r f) -> p r f", r=R2)).then_inc(tl.ev_act, 1)
                    else:
                        half = R3 // 2 * F
                        nc.scalar.copy(tb[:, j, 0:half], bank[s0[0]])
                        nc.scalar.copy(tb[:, j, half:2 * half], bank[s0[1]]).then_inc(tl.ev_act, 1)

        def tail_pe(pe, tl):
            l = tl.l
            with pe.Fori(0, NBATCH) as b:
                pe.wait_ge(tl.lhs, b + 1)
                pe.wait_ge(tl.y_read, b * tl.uses)
                for j in range(BATCH):
                    mm = nc.tensor.matmul(psA[:, j, :], stg[:, j, :], (wT[:, 1, :] if l == 0 else ident[:, :]), start=True, stop=True)
                mm.then_inc(tl.own, 1)
                if l == 3:
                    return
                pe.wait_ge(tl.normed, b + 1)
                pe.wait_ge(tl.turned_ev, b)
                for j in range(BATCH):
                    mm = nc.tensor.transpose(psT[:, j, :], xn[:, j, :], ident[:, :])
                mm.then_inc(tl.turned, 1)
                pe.wait_ge(tl.turned_ev, b + 1)
                if l == 2:
                    pe.wait_ge(tl.y_read, b * 2 + 1)
                    for j in range(BATCH):
                        mm = nc.tensor.matmul(psA[:, j, :], xt[:, j, :], wraw[:, 6, :], start=True, stop=True)
                    mm.then_inc(tl.own, 1)
                for j in range(BATCH):
                    before = b * BATCH + (j - 1 if j >= 2 else 0)
                    if l < 2:
                        pe.wait_ge(tl.ev_dve, before)
                    if l > 0:
                        pe.wait_ge(tl.ev_act, before)
                    s0 = SETS[j % 2]
                    x_j = xt[:, j, :]
                    if l == 0:
                        mm = nc.tensor.matmul(bank[s0[0]][:, 0:3 * F], x_j, wT[:, 2:5, :].rearrange("p a f -> p (a f)"), start=True, stop=True)
                    elif l == 1:
                        nc.tensor.matmul(bank[s0[0]], x_j, wraw[:, 7:7 + R2, :].rearrange("p a f -> p (a f)"), start=True, stop=True)
                        mm = nc.tensor.matmul(bank[s0[1]][:, 0:F + 2 * R2], x_j, wcat2[:, :], start=True, stop=True)
                    else:
                        for c in range(2):
                            mm = nc.tensor.matmul(bank[s0[c]], x_j, wcat3[:, 4 * c:4 * c + 4, :].rearrange("p a f -> p (a f)"), start=True, stop=True)
                    mm.then_inc(tl.tabled, 1)

        def tail_dve(dve, tl):
            l = tl.l
            steps = {0: 2, 1: 3, 2: 2 + 1 + R2, 3: 3}[l]
            chain = Chain(dve, tl.chain, steps)
            if l > 0:
                if l < 3:
                    dve.wait_ge(tails[l - 1].ev_dve, NB)
                else:
                    dve.wait_ge(tails[2].y_read, NBATCH * 2)
                dve.wait_ge(tails[l - 1].x_kept, NBATCH)
            else:
                dve.wait_ge(x_ev, -(-NB // 4) + 1)
            if l == 1:
                dve.wait_ge(passes[1].ready, NB * 16)
                for j in range(BATCH):
                    nc.vector.memset(tb[:, j, 0:R2 * GW].rearrange("p (r g) -> p r g", r=R2)[:, :, F + 1:GW], 0.0)
            with dve.Fori(0, NBATCH) as b:
                chain.begin(b)
                dve.wait_ge(tl.own, b * tl.uses + 1)
                dve.wait_ge(tl.normed, b)
                if l == 0:
                    nc.vector.tensor_tensor(y[:, :, :], psA, tile_batch(X, b), ALU.add).then_inc(tl.y_read, 1)
                    dve.wait_ge(tl.y_read, b * tl.uses + 1)
                elif l in (1, 3):
                    nc.vector.tensor_tensor(y[:, :, :], psA, tile_batch(S, b), ALU.add).then_inc(tl.y_read, 1)
                    dve.wait_ge(tl.y_read, b * tl.uses + 1)
                    chain.link(nc.vector.scalar_tensor_tensor(y[:, :, :], y[:, :, :], 0.0, tile_batch(X, b), ALU.max, ALU.add))
                else:
                    nc.vector.tensor_tensor(y[:, :, :], psA, tile_batch(S, b), ALU.add).then_inc(tl.y_read, 1)
                    dve.wait_ge(tl.y_read, b * tl.uses + 1)
                    chain.link(nc.vector.tensor_tensor(y[:, :, :], y[:, :, :], tile_batch(X, b), ALU.add))
                    nc.vector.tensor_copy(al_stage[:, :, :], tile_batch(alpha_self, b)).then_inc(al_staged, 1)
                    dve.wait_ge(al_staged, b + 1)
                    dve.wait_ge(tl.h_in, (b + 1) * (16 * BATCH))
                    for r in range(R2):
                        for j in range(BATCH):
                            last = nc.vector.scalar_tensor_tensor(y[:, j, :], h_self[:, j, r, 0:F], al_stage[:, j, r:r + 1], y[:, j, :], ALU.mult, ALU.add)
                        chain.link(last)
                for j in range(BATCH):
                    last = nc.vector.bn_stats(st6[:, j, :], y[:, j, :])
                chain.link(last)
                dve.sem_inc(dve_turn, 1)
                for j in range(BATCH):
                    last = nc.vector.bn_aggr(mv[:, j, :], st6[:, j, :])
                last.then_inc(tl.stats, 1)
                dve.wait_ge(tl.rooted, b + 1)
                chain.link(nc.vector.reciprocal(rstd[:, :], rstd[:, :]))
                if l < 3:
                    dve.wait_ge(tl.x_kept, b)
                    dve.wait_ge(tl.turned, b)
                else:
                    dve.wait_ge(out_stored, b * 16 * BATCH)
                for j in range(BATCH):
                    last = nc.vector.tensor_scalar(xn[:, j, :], y[:, j, :], mv[:, j, 0:1], rstd[:, j:j + 1], ALU.subtract, ALU.mult)
                last.then_inc(tl.normed, 1)
                if l == 3:
                    return
                if l == 2:
                    dve.wait_ge(tl.own, b * 2 + 2)
                    nc.vector.tensor_tensor(tile_batch(S, b), psA, rows_b[:, 5:6, :].to_broadcast([P, BATCH, F]), ALU.add).then_inc(tl.y_read, 1)
                    return
                for j in range(BATCH):
                    t = b * BATCH + j
                    dve.wait_ge(tl.tabled, t + 1)
                    if l == 0:
                        if j == 0:
                            dve.wait_ge(tl.next.ready, b * (BATCH * 16))
                        pst = bank[SETS[j % 2][0]]
                        nc.vector.tensor_tensor(tb[:, j, 0:2 * F], pst[:, 0:2 * F], rows_b[:, 1:3, :].rearrange("p a f -> p (a f)"), ALU.add)
                        nc.vector.tensor_tensor(row(S, t), pst[:, 2 * F:3 * F], rows_b[:, 3, :], ALU.add).then_inc(tl.ev_dve, 1)
                    elif l == 1:
                        pst = bank[SETS[j % 2][1]]
                        if j == 0:
                            dve.wait_ge(tl.next.ready, b * (BATCH * 16))
                        nc.vector.tensor_copy(row(scores, t), pst[:, F:F + 2 * R2])
                        nc.vector.tensor_copy(tb[:, j, 0:R2 * GW].rearrange("p (r g) -> p r g", r=R2)[:, :, F], pst[:, F:F + R2])
                        nc.vector.tensor_tensor(row(S, t), pst[:, 0:F], rows_b[:, 4, :], ALU.add).then_inc(tl.ev_dve, 1)

        def tail_sp(sp, tl):
            l = tl.l
            with sp.Fori(0, NBATCH) as b:
                if l == 2:
                    own_rows(sp, b)
                for j in range(BATCH):
                    t = b * BATCH + j
                    if l < 2:
                        sp.wait_ge(tl.ev_dve, t + 1)
                    if l > 0:
                        sp.wait_ge(tl.ev_act, t + 1)
                    if l == 0:
                        dst_ = t1.rearrange("(r n) f -> n r f", r=R1)[bass.ds(t * P, P), :, :]
                        src_ = tb[:, j, 0:R1 * F].rearrange("p (r f) -> p r f", r=R1)
                    elif l == 1:
                        dst_ = t2.rearrange("(r n) f -> n r f", r=R2)[bass.ds(t * P, P), :, :]
                        src_ = tb[:, j, 0:R2 * GW].rearrange("p (r f) -> p r f", r=R2)
                    else:
                        dst_ = t3.rearrange("(r n) f -> n r f", r=R3)[bass.ds(t * P, P), :, :]
                        src_ = tb[:, j, 0:R3 * F].rearrange("p (r f) -> p r f", r=R3)
                    sp.dma_start(dst_, src_).then_inc(tl.next.ready, 16)

        def store_out(sp, tl):
            with sp.Fori(0, NBATCH - 1) as b:
                sp.wait_ge(tl.normed, b + 1)
                for j in range(BATCH):
                    sp.dma_start(out[bass.ds((b * BATCH + j) * P, P), :], xn[:, j, :]).then_inc(out_stored, 16)
            sp.wait_ge(tl.normed, NBATCH)
            for j in range(BATCH):
                t = (NBATCH - 1) * BATCH + j
                here = min(P, N - t * P)
                sp.dma_start(out[t * P:t * P + here, :], xn[0:here, j, :]).then_inc(out_stored, 16)
            sp.wait_ge(out_stored, NB * 16)

        def prepare_dve(dve):
            ch = Chain(dve, v_prep)
            for i in range(5):
                nc.vector.memset(edge_rows[:, i, NCH - 1, :], NOBODY if i == 1 else 0)
                nc.vector.memset(tab[:, i, 0:LEAD], float(NOBODY) if i == 1 else 0.0)
                nc.vector.memset(tab[:, i, LEAD + ROWS:SLOTS], float(NOBODY) if i == 1 else 0.0)
            nc.vector.memset(X[:, NB - 1, :], 0.0).then_inc(pads_set, 1)
            nc.vector.memset(ones[:, :], 1.0)
            nc.vector.memset(eps[:, :], EPS)
            nc.vector.memset(u[:, :], float(P) ** -0.5)
            dve.wait_ge(iota_set, 3)
            nc.vector.tensor_scalar(ident[:, :], iota[:, 0:P], prow[:, :], None, ALU.is_equal).then_inc(ident_set, 1)
            dve.wait_ge(edges_in, 16 * 15)
            nc.vector.tensor_copy(edge_rows_f, edge_rows[:, :, :, :]).then_inc(edges_f, 1)
            for i in range(5):
                dve.wait_ge(edge_tr, i + 1)
                last = nc.vector.tensor_copy(tab[:, i, LEAD:LEAD + ROWS], bank[i][:, 0:ROWS])
            last.then_inc(edge_ev, 1)
            dve.wait_ge(edge_ev, 1)
            nc.vector.tensor_copy(idx[:, 0, :], tab[:, 0, :])
            for i in range(1, 4):
                last = nc.vector.scalar_tensor_tensor(idx[:, i, :], tab[:, 1 + i, :], float(NPAD), tab[:, 0, :], ALU.mult, ALU.add)
            last.then_inc(idx_ready, 1)
            base = block_base[:, :].rearrange("p (b o) -> p b o", o=1).to_broadcast([P, NB, TB])
            dst_f = tab[:, 1, :].rearrange("p (b k) -> p b k", k=TB)
            ch.link(nc.vector.tensor_tensor(key_w[:, :, :], dst_f, base, ALU.subtract))
            ch.link(nc.vector.tensor_scalar(key0[:, :, :], key_w[:, :, :], 0.0, float(SPAN), ALU.is_lt, ALU.mult))
            ch.link(nc.vector.tensor_tensor(key0[:, :, :], key0[:, :, :], key_w[:, :, :], ALU.add))
            ch.link(nc.vector.tensor_scalar(key_w[:, :, :], key0[:, :, :], float(PAIR), None, ALU.is_lt))
            nc.vector.tensor_reduce(in_pair[:, :], key_w[:, :, :].rearrange("p b k -> p (b k)"), AX, ALU.add).then_inc(match_summed, 1)
            dve.wait_ge(match_total, 1)
            ch.link(nc.vector.tensor_scalar(count[:, 0:1], bank[5][0:1, 0:1], float(E), float(1 - SHIFTS), ALU.is_equal, ALU.mult))
            nc.vector.tensor_scalar(shifts[:, :], count[:, 0:1], float(SHIFTS), None, ALU.add).then_inc(shifts_ready, 1)
            dve.wait_ge(weights_in, 16 * WEIGHT_LOADS)
            for g in range(3):
                dve.wait_ge(w_tr, g + 1)
                n = min(4, 5 + R2 - 4 * g)
                nc.vector.tensor_copy(wT[:, 4 * g:4 * g + n, :].rearrange("p a f -> p (a f)"), bank[5 + g][:, 0:n * P])
            dve.wait_ge(w_tr, 4)
            nc.vector.tensor_copy(smallT[:, :], bank[4][:, 0:3 + 2 * R2])
            nc.vector.tensor_copy(wcat2[:, 0:F], wraw[:, 5, :]).then_inc(w_ev, 1)
            for r in range(R2):
                ch.link(nc.vector.tensor_tensor(rows_b[:, 4, :], rows_b[:, 4, :], rows_b[:, 6 + r, :], ALU.add))
            for k in range(NBASE):
                for r in range(R3):
                    w = wcomp[:, r * NBASE + k:r * NBASE + k + 1]
                    base_k = wraw[:, 7 + R2 + k, :]
                    if k == 0:
                        last = nc.vector.tensor_scalar(wcat3[:, r, :], base_k, w, None, ALU.mult)
                    else:
                        last = nc.vector.scalar_tensor_tensor(wcat3[:, r, :], base_k, w, wcat3[:, r, :], ALU.mult, ALU.add)
                ch.link(last)
            dve.wait_ge(wa_done, 1)
            nc.vector.tensor_copy(wcat2[:, F:F + 2 * R2], bank[4][:, 64:64 + 2 * R2]).then_inc(weights_ready, 1)
            for g in range(-(-NB // 4)):
                dve.wait_ge(x_tr, g + 1)
                n = min(4, NB - 4 * g)
                nc.vector.tensor_copy(XT[:, 4 * g * P:(4 * g + n) * P], bank[1 + g % 2][:, 0:n * P]).then_inc(x_ev, 1)
            ch.wait()
            nc.vector.tensor_tensor(X[:, :, :], X[:, :, :], rows_b[:, 0:1, :].to_broadcast([P, NB, F]), ALU.add).then_inc(x_ev, 1)

        WEIGHT_LOADS = 7 + 2 + 3 + 2 + 6 + 1 + 1

        def prepare_pe(pe):
            pe.wait_ge(ident_set, 1)
            pe.wait_ge(edges_f, 1)
            for i in range(5):
                for q in range(NCH):
                    tr = nc.tensor.transpose(bank[i][:, q * RC:(q + 1) * RC], edge_rows_f[:, i, q, :], ident[0:RC, 0:RC])
                tr.then_inc(edge_tr, 1)
            pe.wait_ge(match_summed, 1)
            nc.tensor.matmul(bank[5][0:1, 0:1], in_pair[:, :], ones[:, 0:1], start=True, stop=True).then_inc(match_total, 1)
            pe.wait_ge(shifts_ready, 1)
            pe.wait_ge(weights_in, 16 * WEIGHT_LOADS)
            order = list(range(5)) + list(range(7, 7 + R2))
            for g in range(3):
                for i, w in enumerate(order[4 * g:4 * g + 4]):
                    tr = nc.tensor.transpose(bank[5 + g][:, i * P:(i + 1) * P], wraw[:, w, :], ident[:, :])
                tr.then_inc(w_tr, 1)
            nc.tensor.transpose(bank[4][:, 0:3 + 2 * R2], small[:, :], ident[0:3 + 2 * R2, 0:3 + 2 * R2]).then_inc(w_tr, 1)
            pe.wait_ge(w_ev, 1)
            for r in range(R2):
                mm = nc.tensor.matmul(bank[4][:, 64 + r:64 + r + R2 + 1:R2], wT[:, 5 + r, :], smallT[:, 3 + r:3 + r + R2 + 1:R2], start=True, stop=True)
            mm.then_inc(wa_done, 1)
            pe.wait_ge(x_in, 16 * NB)
            for g in range(-(-NB // 4)):
                if g >= 2:
                    pe.wait_ge(x_ev, g - 1)
                for i in range(min(4, NB - 4 * g)):
                    tr = nc.tensor.transpose(bank[1 + g % 2][:, i * P:(i + 1) * P], X[:, 4 * g + i, :], ident[:, :])
                tr.then_inc(x_tr, 1)

        PW = 5

        def half_pe(pe, weights, vec, n, k):
            pe.wait_ge(pw_v, (n + k) * PW)
            for c in range(2):
                mm = nc.tensor.matmul(bank[7][:, c:c + 1], weights[:, c, :], vec[:, c:c + 1], start=True, stop=True)
            mm.then_inc(pw_pe, 1)
            pe.wait_ge(pw_v, (n + k) * PW + 2)
            nc.tensor.matmul(bank[7][:, 2:4], ones[:, :], sq[:, :], start=True, stop=True).then_inc(pw_pe, 1)

        def half_act(act, n, k):
            act.wait_ge(pw_pe, (n + k) * 2 + 2)
            nc.scalar.activation(nrm[:, :], bank[7][:, 2:4], ACT.Sqrt).then_inc(pw_act, 1)

        def half_dve(dve, ch, dest, n, k):
            dve.wait_ge(pw_pe, (n + k) * 2 + 1)
            ch.link(nc.vector.tensor_copy(raw[:, :], bank[7][:, 0:2]))
            ch.did(nc.vector.tensor_tensor(sq[:, :], raw[:, :], raw[:, :], ALU.mult))
            dve.wait_ge(pw_act, (n + k) + 1)
            ch.link(nc.vector.tensor_scalar(nrm[:, :], nrm[:, :], TINY, None, ALU.add))
            ch.link(nc.vector.reciprocal(nrm[:, :], nrm[:, :]))
            ch.did(nc.vector.tensor_tensor(dest[:, :], raw[:, :], nrm[:, :], ALU.mult))

        def power_pe(pe):
            with pe.Fori(0, POWER_STEPS) as i:
                half_pe(pe, wraw, u, 2 * i, 0)
                half_pe(pe, wT, v, 2 * i, 1)
            n = 2 * POWER_STEPS
            half_pe(pe, wraw, u, n, 0)
            pe.wait_ge(pw_v, (n + 1) * PW)
            for c in range(2):
                mm = nc.tensor.matmul(bank[7][:, c:c + 1], wT[:, c, :], v[:, c:c + 1], start=True, stop=True)
            mm.then_inc(pw_pe, 1)
            pe.wait_ge(pw_v, (n + 1) * PW + 1)
            nc.tensor.matmul(bank[7][:, 2:4], ones[:, :], sq[:, :], start=True, stop=True).then_inc(pw_pe, 1)

        def power_act(act):
            with act.Fori(0, POWER_STEPS) as i:
                half_act(act, 2 * i, 0)
                half_act(act, 2 * i, 1)
            half_act(act, 2 * POWER_STEPS, 0)

        def power_dve(dve):
            ch = Chain(dve, pw_v, 2 * PW)
            with dve.Fori(0, POWER_STEPS) as i:
                ch.begin(i)
                half_dve(dve, ch, v, 2 * i, 0)
                half_dve(dve, ch, u, 2 * i, 1)
            ch.begin(POWER_STEPS)
            n = 2 * POWER_STEPS
            half_dve(dve, ch, v, n, 0)
            dve.wait_ge(pw_pe, (n + 1) * 2 + 1)
            ch.did(nc.vector.tensor_tensor(sq[:, :], bank[7][:, 0:2], u[:, :], ALU.mult))
            dve.wait_ge(pw_pe, (n + 1) * 2 + 2)
            ch.link(nc.vector.reciprocal(inv_sigma[:, :], bank[7][:, 2:4]))
            nc.vector.tensor_scalar(wT[:, 1, :], wT[:, 1, :], inv_sigma[:, 1:2], None, ALU.mult).then_inc(sigma_ready, 1)

        sigma_ready = sem("sigma_ready")
        gin_mm = sem("gin_mm")
        gin_relu = sem("gin_relu")
        gin_stats = sem("gin_stats")
        gin_root = sem("gin_root")
        gin_norm = sem("gin_norm")
        gin_ready = sem("gin_ready")
        x_added = sem("x_added")

        def chunks():
            return [(c, c * 512, min(512, NPAD - c * 512)) for c in range(-(-NPAD // 512))]

        def gin_pe(pe):
            pe.wait_ge(x_added, 1)
            for c, at, w in chunks():
                if c >= 2:
                    pe.wait_ge(gin_relu, c - 1)
                nc.tensor.matmul(bank[1 + c % 2][:, 0:w], wT[:, 0, :], featT[:, at:at + w], start=True, stop=True).then_inc(gin_mm, 1)

        def gin_act(act):
            act.wait_ge(sigma_ready, 1)
            for c, at, w in chunks():
                act.wait_ge(gin_mm, c + 1)
                nc.scalar.activation(featT[:, at:at + w], bank[1 + c % 2][:, 0:w], ACT.Relu, bias=smallT[:, 0:1], scale=inv_sigma[:, 0:1]).then_inc(gin_relu, 1)
            act.wait_ge(gin_stats, NCHK + 1)
            nc.scalar.activation(bn_scale[:, :], bnmv[:, 1:2], ACT.Sqrt, bias=eps[:, :]).then_inc(gin_root, 1)
            act.wait_ge(gin_ready, 1)

        def gin_dve(dve):
            dve.wait_ge(tails[0].folded, 1)
            nc.vector.tensor_tensor(featT, featT, XT, ALU.add).then_inc(x_added, 1)
            for c in range(NCHK):
                dve.wait_ge(gin_relu, c + 1)
                nc.vector.bn_stats(bn6[:, c, :], featT[:, 512 * c:min(512 * c + 512, N)]).then_inc(gin_stats, 1)
            dve.wait_ge(gin_stats, NCHK)
            nc.vector.bn_aggr(bnmv[:, :], bn6[:, :, :].rearrange("p a b -> p (a b)")).then_inc(gin_stats, 1)
            dve.wait_ge(gin_root, 1)
            ch = Chain(dve, gin_norm)
            ch.link(nc.vector.reciprocal(bn_scale[:, :], bn_scale[:, :]))
            ch.link(nc.vector.tensor_tensor(bn_scale[:, :], bn_scale[:, :], smallT[:, 1:2], ALU.mult))
            ch.link(nc.vector.tensor_tensor(bn_shift[:, :], bn_scale[:, :], bnmv[:, 0:1], ALU.mult))
            nc.vector.tensor_tensor(bn_shift[:, :], smallT[:, 2:3], bn_shift[:, :], ALU.subtract).then_inc(gin_ready, 1)

        scores = sb("scores", [P, NB, 2 * R2])
        alpha_self = sb("alpha_self", [P, NB, R2])
        al_stage = sb("al_stage", [P, BATCH, R2])
        al_staged = sem("al_staged")
        rel_mask = sb("rel_mask", [P, SLOTS, R2], BF16)
        pair_key = sb("pair_key", [P, NB, TB])
        ident16 = sb("ident16", [P, P], BF16)
        iota16 = sb("iota16", [P, PAIR], BF16)
        low_col = sb("low_col", [P, 1])
        low_one = sb("low_one", [1, 1])
        low = sb("low", [P, 1])
        s_edge = sb("s_edge", [P, NB, TB])
        p_edge = sb("p_edge", [P, NB, TB])
        v_stage = sb("v_stage", [P, TB])
        kk_stage = sb("kk_stage", [P, TB])
        mask_stage = sb("mask_stage", [P, TB, R2])
        group_max = sb("group_max", [P, TB])
        masked = sb("masked", [P, TB, R2])
        rest = sb("rest", [P, TB, R2])
        ops16 = sb("ops16", [P, TB, SW], BF16)
        hot16 = sb("hot16", [P, TB, PAIR], BF16)
        hotT = sb("hotT", [P, 2 * TB, P], BF16)
        out_u = sb("out_u", [P, 2, TB, SW])
        val_u = sb("val_u", [P, 2, TB, R2])
        max_u = sb("max_u", [P, 2, R2])
        U = sb("U", [P, ACCT, R2])
        D = sb("D", [P, ACCT, R2])
        node = [sb(f"node{i}", [P, NB, R2]) for i in range(4)]
        target = sb("target", [P, ACCT, 2 * R2])
        target_rest = sb("target_rest", [P, ACCT, 2 * R2])
        target16 = sb("target16", [P, ACCT, 3 * 2 * R2], BF16)
        share16 = sb("share16", [P, ACCT, 3 * R2], BF16)
        picked = sb("picked", [P, TB, 3, 2 * R2])
        pick_sum = sb("pick_sum", [P, TB, 2 * R2])
        dm_edge = sb("dm_edge", [P, TB, 2])
        logit = sb("logit", [P, TB])
        p_stage = sb("p_stage", [P, TB])
        p_acc = sb("p_acc", [P, TB])
        in_win = sb("in_win", [P, TB])
        den_u = sb("den_u", [P, 2, 3, R2])
        den_w = sb("den_w", [P, 2, R2])
        v_rows = acc[:, 0:TB * P].rearrange("p (k e) -> p k e", k=TB)
        v_equal = acc[:, TB * P:2 * TB * P].rearrange("p (k e) -> p k e", k=TB)
        turned16 = psum[:, 0:5, :].bitcast(BF16)

        n_prep = sem("n_prep")
        low_pe = sem("low_pe")
        low_set = sem("low_set")
        extracted = sem("extracted")
        kept_in = [sem(f"kept_in{h}") for h in range(2)]
        diag = sem("diag")
        eq_mm = sem("eq_mm")
        rows_read = sem("rows_read")
        eq_read = sem("eq_read")
        m_block = sem("m_block")
        m_round = sem("m_round")
        ops_ready = sem("ops_ready")
        maxed = sem("maxed")
        max_read = sem("max_read")
        max_done = sem("max_done")
        self_logit = sem("self_logit")
        self_exp = sem("self_exp")
        n_chain = sem("n_chain")
        hot_p = sem("hot_p")
        turned_p = sem("turned_p")
        turned_p_ev = sem("turned_p_ev")
        picked_p = sem("picked_p")
        p_block = sem("p_block")
        p_round = sem("p_round")
        logits = sem("logits")
        exped = sem("exped")
        p_ops = sem("p_ops")
        den_mm = sem("den_mm")
        den_done = sem("den_done")
        p_kept = sem("p_kept")
        reloaded = [sem(f"reloaded{h}") for h in range(2)]
        hot_q = sem("hot_q")
        turned_q = sem("turned_q")
        turned_q_ev = sem("turned_q_ev")
        picked_q = sem("picked_q")
        q_block = sem("q_block")
        q_round = sem("q_round")
        GROUPS = [(0, 6), (6, 12), (12, TB)]
        NG = len(GROUPS)
        A2 = passes[2]

        def eq_tile(g, k):
            at = k - GROUPS[g][0]
            return bank[3 * (g % 2) + at // 2][:, PAIR * (at % 2):PAIR * (at % 2) + PAIR]

        def thirds(ch, src_, hi, mid, lo, rest_):
            ch.link(nc.vector.tensor_copy(hi, src_))
            ch.link(nc.vector.tensor_tensor(rest_, src_, hi, ALU.subtract))
            ch.link(nc.vector.tensor_copy(mid, rest_))
            ch.link(nc.vector.tensor_tensor(lo, rest_, mid, ALU.subtract))

        def blocks_ahead(eng, body):
            with eng.Fori(0, NB // 2 - 1) as m:
                body(2 * m, 0, m, True)
                body(2 * m + 1, 1, m, True)
            body(NB - 3, 0, NB // 2 - 1, True)
            body(NB - 2, 1, NB // 2 - 1, False)
            body(NB - 1, 0, NB // 2, False)

        def keep_rows(sp):
            def block(n, h, m):
                sp.wait_ge(A2.gathered[h], A2.gathered_by(h, m))
                sp.dma_start(kept[bass.ds(n, 1), :, :].rearrange("o p c -> (o p) c"),
                             ring[:, h, :, :].rearrange("p k g -> p (k g)")).then_inc(kept_in[h], 16)
            blocks(sp, block)

        def reload_rows(sp):
            sp.wait_ge(kept_in[0], 16 * (NB // 2 + 1))
            sp.wait_ge(kept_in[1], 16 * (NB // 2))
            S_ = sp.value_load(shifts[0:1, 0:1], min_val=1, max_val=SHIFTS)

            def load(n, h):
                sp.dma_start(ring[:, h, :, :].rearrange("p k g -> p (k g)"),
                             kept[bass.ds(n, 1), :, :].rearrange("o p c -> (o p) c")).then_inc(reloaded[h], 16)
            sp.wait_ge(extracted, NB)
            load(0, 0)
            load(1, 1)
            with sp.Fori(0, NB // 2 - 1) as m:
                for h in range(2):
                    sp.wait_ge(A2.summed, (2 * m + (h + 1)) * S_)
                    load(2 * m + (2 + h), h)
            sp.wait_ge(A2.summed, (NB - 2) * S_)
            load(NB - 1, 0)

        def own_rows(sp, b):
            tl = tails[2]
            sp.wait_ge(tl.folded, 1)
            sp.wait_ge(tl.normed, b)
            for j in range(BATCH):
                sp.dma_start(h_self[:, j, :, :], t2.rearrange("(r n) f -> n r f", r=R2)[bass.ds((b * BATCH + j) * P, P), :, :]).then_inc(tl.h_in, 16)

        def attend_act(act, S_):
            def stage(n, h):
                nc.scalar.copy(idx_stage[:, h, :], idx[:, 2, bass.ds(n * TB, TB)]).then_inc(A2.staged[h], 1)
            act.wait_ge(tails[1].normed, NBATCH)
            stage(0, 0)
            stage(1, 1)

            def block(n, h, m, ahead):
                for g, (lo_, hi_) in enumerate(GROUPS):
                    act.wait_ge(eq_read, n * NG)
                    act.wait_ge(eq_mm, n * NG + (g + 1))
                    for k in range(lo_, hi_):
                        last = nc.scalar.copy(v_rows[:, k, :], eq_tile(g, k)[:, P:PAIR])
                    last.then_inc(rows_read, 1)
                if ahead:
                    act.wait_ge(kept_in[h], (m + 1) * 16)
                    act.wait_ge(extracted, n + 1)
                    stage(n + 2, h)
            blocks_ahead(act, block)
            act.wait_ge(self_logit, 1)
            nc.scalar.activation(node[3][:, :, :], node[3][:, :, :], ACT.Exp).then_inc(self_exp, 1)

            def turn_block(turned, ev, then):
                def block(n, h, m):
                    first = act.snap(n * S_)
                    with act.Fori(0, S_) as s:
                        c = first + s
                        act.wait_ge(turned, c + 1)
                        for b0 in range(0, 4, 2):
                            nc.scalar.copy(hotT[:, b0 * 8:b0 * 8 + 16, :].rearrange("p (a q) e -> p a (q e)", a=2), turned16[:, b0:b0 + 2, :])
                        nc.scalar.copy(hotT[:, 32:2 * TB, :].rearrange("p q e -> p (q e)"), turned16[:, 4, 0:(2 * TB - 32) * P]).then_inc(ev, 1)
                        then(c)
                return block

            def exp_edges(c):
                act.wait_ge(logits, c + 1)
                nc.scalar.activation(p_stage[:, :], logit[:, :], ACT.Exp).then_inc(exped, 1)
            blocks(act, turn_block(turned_p, turned_p_ev, exp_edges))
            blocks(act, turn_block(turned_q, turned_q_ev, lambda c: None))

        def turn_hots(pe, c, hot, turned, ev):
            pe.wait_ge(hot, c + 1)
            pe.wait_ge(ev, c)
            for q in range(2 * TB):
                tr = nc.tensor.transpose(turned16[:, q // 8, (q % 8) * P:(q % 8 + 1) * P], hot16[:, q // 2, (q % 2) * P:(q % 2 + 1) * P], ident16[:, :])
            tr.then_inc(turned, 1)
            pe.wait_ge(ev, c + 1)

        def pick(pe, n, s, table, width, inc):
            for k in range(TB):
                for half in range(2):
                    mm = nc.tensor.matmul(bank[5][:, k * width:(k + 1) * width], hotT[:, 2 * k + half, :],
                                          table[:, bass.ds(n + 2 * s + half, 1), :].rearrange("p a w -> p (a w)"),
                                          start=(half == 0), stop=(half == 1))
            mm.then_inc(inc, 1)

        def attend_pe(pe, S_):
            pe.wait_ge(n_prep, 1)
            nc.tensor.transpose(bank[7][0:1, 0:P], low_col[:, :], ident[:, :]).then_inc(low_pe, 1)
            pe.wait_ge(n_prep, 2)
            nc.tensor.matmul(bank[7][:, P:P + 1], ones[0:1, :], low_one[:, :], start=True, stop=True).then_inc(low_pe, 1)

            def max_block(n, h, m):
                for g, (lo_, hi_) in enumerate(GROUPS):
                    pe.wait_ge(diag, n * NG + (g + 1))
                    pe.wait_ge(eq_read, n * NG + (0 if g < 2 else 1))
                    for k in range(lo_, hi_):
                        mm = nc.tensor.matmul(eq_tile(g, k), ones[:, :], onehot[:, k, :], start=True, stop=True)
                    mm.then_inc(eq_mm, 1)
                first = pe.snap(n * S_)
                with pe.Fori(0, S_) as s:
                    c = first + s
                    pe.wait_ge(ops_ready, n + 1)
                    pe.wait_ge(A2.hot, c + 1)
                    pe.wait_ge(max_read, c)
                    for half in range(2):
                        for k in range(TB):
                            mm = nc.tensor.matmul(bank[6 + half][:, k * SW:(k + 1) * SW], hot16[:, k, half * P:(half + 1) * P], ops16[:, k, :], start=True, stop=True)
                    mm.then_inc(maxed, 1)
            blocks(pe, max_block)

            pe.wait_ge(n_chain, TARGET_STEPS)
            def p_block_(n, h, m):
                first = pe.snap(n * S_)
                with pe.Fori(0, S_) as s:
                    c = first + s
                    turn_hots(pe, c, hot_p, turned_p, turned_p_ev)
                    pick(pe, n, s, target16, 6 * R2, picked_p)
                    pe.wait_ge(p_ops, c + 1)
                    pe.wait_ge(den_done, c)
                    for half in range(2):
                        for k in range(TB):
                            mm = nc.tensor.matmul(bank[6][:, half * 3 * R2:(half + 1) * 3 * R2], hot16[:, k, half * P:(half + 1) * P], ops16[:, k, 0:3 * R2], start=(k == 0), stop=(k == TB - 1))
                    mm.then_inc(den_mm, 1)
            blocks(pe, p_block_)

            pe.wait_ge(n_chain, SHARE_STEPS)
            def q_block_(n, h, m):
                first = pe.snap(n * S_)
                with pe.Fori(0, S_) as s:
                    c = first + s
                    turn_hots(pe, c, hot_q, turned_q, turned_q_ev)
                    pick(pe, n, s, share16, 3 * R2, picked_q)
                    pe.wait_ge(reloaded[h], (m + 1) * 16)
                    pe.wait_ge(wsum_ready, c + 1)
                    pe.wait_ge(A2.acc_done, c)
                    for k in range(TB):
                        mm = nc.tensor.matmul(bank[7][:, 0:PAIR], ring[:, h, k, 0:F], onehot[:, k, :], start=(k == 0), stop=(k == TB - 1))
                    mm.then_inc(A2.summed, 1)
            blocks(pe, q_block_)

        wsum_ready = sem("wsum_ready")
        TARGET_STEPS, SHARE_STEPS = 16, 28

        def attend_dve(dve, S_):
            al = nc.vector
            tl1 = tails[1]
            dve.wait_ge(tl1.ev_dve, NB)
            al.tensor_reduce(low_col[:, :], scores[:, :, 0:R2], mybir.AxisListType.XY, ALU.min).then_inc(n_prep, 1)
            al.memset(U[:, :, :], 0.0)
            al.memset(D[:, :, :], 0.0)
            al.tensor_copy(ident16[:, :], ident[:, :])
            al.tensor_copy(iota16[:, :], iota[:, :])
            for r in range(R2):
                al.tensor_scalar(rel_mask[:, :, r], tab[:, 3, :], float(r), None, ALU.is_equal)
            al.scalar_tensor_tensor(pair_key[:, :, :].rearrange("p b k -> p (b k)"), tab[:, 3, :], float(NPAD), tab[:, 1, :], ALU.mult, ALU.add)
            dve.wait_ge(low_pe, 1)
            al.tensor_reduce(low_one[:, :], bank[7][0:1, 0:P], AX, ALU.min).then_inc(n_prep, 1)
            dve.wait_ge(low_pe, 2)
            al.tensor_copy(low[:, :], bank[7][:, P:P + 1]).then_inc(low_set, 1)
            dve.wait_ge(low_set, 1)

            mb = Chain(dve, m_block, 10)
            mr = Chain(dve, m_round, 9)

            def max_block(n, h, m):
                mb.begin(n)
                mb.wait()
                dve.wait_ge(A2.gathered[h], A2.gathered_by(h, m))
                dve.wait_ge(eq_mm, n * NG)
                mb.did(al.tensor_scalar(v_stage[:, :], ring[:, h, :, F], low[:, :], None, ALU.subtract))
                al.tensor_copy(row(s_edge, n), ring[:, h, :, F]).then_inc(extracted, 1)
                mb.did(al.tensor_copy(kk_stage[:, :], row(pair_key, n)))
                mb.link(al.tensor_copy(mask_stage[:, :, :], rel_mask[:, bass.ds(n * TB, TB), :]))
                for g, (lo_, hi_) in enumerate(GROUPS):
                    for k in range(lo_, hi_):
                        al.tensor_scalar(onehot[:, k, 0:P], ident[:, :], kk_stage[:, k:k + 1], None, ALU.mult)
                        last = al.tensor_scalar(onehot[:, k, P:PAIR], ident[:, :], v_stage[:, k:k + 1], None, ALU.mult)
                    last.then_inc(diag, 1)
                for g, (lo_, hi_) in enumerate(GROUPS):
                    dve.wait_ge(rows_read, n * NG + (g + 1))
                    for k in range(lo_, hi_):
                        last = al.scalar_tensor_tensor(v_equal[:, k, :], eq_tile(g, k)[:, 0:P], kk_stage[:, k:k + 1], v_rows[:, k, :], ALU.is_equal, ALU.mult)
                    last.then_inc(eq_read, 1)
                dve.wait_ge(eq_read, n * NG + NG)
                mb.link(al.tensor_reduce(group_max[:, :], v_equal, AX, ALU.max))
                mb.link(al.tensor_tensor(masked[:, :, :], mask_stage[:, :, :], group_max[:, :].rearrange("p (k o) -> p k o", o=1).to_broadcast([P, TB, R2]), ALU.mult))
                thirds(mb, masked[:, :, :], ops16[:, :, 0:R2], ops16[:, :, R2:2 * R2], ops16[:, :, 2 * R2:3 * R2], rest[:, :, :])
                mb.did(al.tensor_copy(ops16[:, :, 3 * R2:SW], mask_stage[:, :, :]))
                al.tensor_copy(key_stage[:, :], row(key0, n)).then_inc(ops_ready, 1)
                first = dve.snap(n * S_)
                with dve.Fori(0, S_) as s:
                    c = first + s
                    dve.wait_ge(ops_ready, n + 1)
                    mr.begin(c)
                    mr.wait()
                    for k in range(TB):
                        last = al.tensor_scalar(hot16[:, k, :], iota16[:, :], key_stage[:, k:k + 1], None, ALU.is_equal)
                    last.then_inc(A2.hot, 1)
                    mr.link(al.tensor_scalar(key_wrap[:, :], key_stage[:, :], float(PAIR), float(SPAN), ALU.is_lt, ALU.mult))
                    mr.did(al.scalar_tensor_tensor(key_stage[:, :], key_stage[:, :], float(-PAIR), key_wrap[:, :], ALU.add, ALU.add))
                    dve.wait_ge(maxed, c + 1)
                    both = psum[:, 6:8, 0:TB * SW]
                    al.tensor_copy(out_u[:, :, :, :].rearrange("p a k w -> p a (k w)"), both).then_inc(max_read, 1)
                    dve.wait_ge(max_read, c + 1)
                    mr.link(al.tensor_tensor(val_u[:, :, :, :], out_u[:, :, :, 0:R2], out_u[:, :, :, R2:2 * R2], ALU.add))
                    mr.link(al.tensor_tensor(val_u[:, :, :, :], val_u[:, :, :, :], out_u[:, :, :, 2 * R2:3 * R2], ALU.add))
                    cnt = out_u[:, :, :, 3 * R2:SW]
                    mr.link(al.tensor_scalar(cnt, cnt, 1.0, None, ALU.max))
                    mr.link(al.reciprocal(cnt, cnt))
                    mr.link(al.tensor_tensor(val_u[:, :, :, :], val_u[:, :, :, :], cnt, ALU.mult))
                    mr.link(al.tensor_reduce(max_u[:, :, :], val_u[:, :, :, :].rearrange("p a k r -> p a r k"), AX, ALU.max))
                    sums = U[:, bass.ds(n + 2 * s, 2), :]
                    mr.did(al.tensor_tensor(sums, sums, max_u[:, :, :], ALU.max))
            blocks(dve, max_block)
            dve.wait_ge(m_round, NB * S_ * 9)

            ch = Chain(dve, n_chain)
            top, mx, _, ps_ = node
            s_n, d_n = scores[:, :, 0:R2], scores[:, :, R2:2 * R2]
            ch.link(al.tensor_tensor(top[:, :, :], U[:, 1:NB + 1, :], U[:, RING + 1:RING + NB + 1, :], ALU.max))
            ch.link(al.tensor_scalar(top[:, :, :], top[:, :, :], low[:, :], None, ALU.add))
            ch.link(al.tensor_tensor(top[:, :, :], top[:, :, :], s_n, ALU.max))
            ch.link(al.tensor_tensor(top[:, :, :], top[:, :, :], d_n, ALU.add))
            ch.link(al.scalar_tensor_tensor(mx[:, :, :], top[:, :, :], SLOPE, top[:, :, :], ALU.mult, ALU.max))
            ch.link(al.memset(target[:, :, :], 0.0))
            for at in (1, RING + 1):
                ch.did(al.tensor_copy(target[:, at:at + NB, 0:R2], d_n))
                ch.link(al.tensor_copy(target[:, at:at + NB, R2:2 * R2], mx[:, :, :]))
            w = 2 * R2
            thirds(ch, target[:, :, :], target16[:, :, 0:w], target16[:, :, w:2 * w], target16[:, :, 2 * w:3 * w], target_rest[:, :, :])
            ch.link(al.tensor_tensor(ps_[:, :, :], s_n, d_n, ALU.add))
            ch.link(al.scalar_tensor_tensor(ps_[:, :, :], ps_[:, :, :], SLOPE, ps_[:, :, :], ALU.mult, ALU.max))
            assert ch.k == TARGET_STEPS, ch.k
            al.tensor_tensor(ps_[:, :, :], ps_[:, :, :], mx[:, :, :], ALU.subtract).then_inc(self_logit, 1)

            pb_ = Chain(dve, p_block, 4)
            pr = Chain(dve, p_round, 21)

            def p_block_(n, h, m):
                pb_.begin(n)
                pb_.wait()
                pb_.did(al.memset(p_acc[:, :], 0.0))
                pb_.did(al.tensor_copy(key_stage[:, :], row(key0, n)))
                pb_.did(al.tensor_copy(v_stage[:, :], row(s_edge, n)))
                pb_.did(al.tensor_copy(mask_stage[:, :, :], rel_mask[:, bass.ds(n * TB, TB), :]))
                first = dve.snap(n * S_)
                with dve.Fori(0, S_) as s:
                    c = first + s
                    pb_.wait()
                    pr.begin(c)
                    pr.wait()
                    for k in range(TB):
                        last = al.tensor_scalar(hot16[:, k, :], iota16[:, :], key_stage[:, k:k + 1], None, ALU.is_equal)
                    last.then_inc(hot_p, 1)
                    pr.did(al.tensor_scalar(in_win[:, :], key_stage[:, :], float(PAIR), None, ALU.is_lt))
                    next_pair(dve, pr)
                    dve.wait_ge(picked_p, c + 1)
                    pr.link(al.tensor_copy(picked[:, :, :, :].rearrange("p k a w -> p (k a w)"), bank[5][:, 0:TB * 6 * R2]))
                    pr.link(al.tensor_tensor(pick_sum[:, :, :], picked[:, :, 0, :], picked[:, :, 1, :], ALU.add))
                    pr.link(al.tensor_tensor(pick_sum[:, :, :], pick_sum[:, :, :], picked[:, :, 2, :], ALU.add))
                    for half in range(2):
                        part = pick_sum[:, :, half * R2:(half + 1) * R2]
                        pr.did(al.tensor_tensor(part, part, mask_stage[:, :, :], ALU.mult))
                    pr.wait()
                    pr.link(al.tensor_reduce(dm_edge[:, :, :], pick_sum[:, :, :].rearrange("p k (a r) -> p k a r", a=2), AX, ALU.add))
                    pr.link(al.tensor_tensor(logit[:, :], v_stage[:, :], dm_edge[:, :, 0], ALU.add))
                    pr.link(al.scalar_tensor_tensor(logit[:, :], logit[:, :], SLOPE, logit[:, :], ALU.mult, ALU.max))
                    pr.link(al.tensor_tensor(logit[:, :], logit[:, :], dm_edge[:, :, 1], ALU.subtract))
                    al.tensor_scalar(logit[:, :], logit[:, :], 1.0, None, ALU.min).then_inc(logits, 1)
                    dve.wait_ge(exped, c + 1)
                    pr.link(al.tensor_tensor(masked[:, :, :], mask_stage[:, :, :], p_stage[:, :].rearrange("p (k o) -> p k o", o=1).to_broadcast([P, TB, R2]), ALU.mult))
                    thirds(pr, masked[:, :, :], ops16[:, :, 0:R2], ops16[:, :, R2:2 * R2], ops16[:, :, 2 * R2:3 * R2], rest[:, :, :])
                    al.tensor_tensor(in_win[:, :], in_win[:, :], p_stage[:, :], ALU.mult).then_inc(p_ops, 1)
                    dve.wait_ge(p_ops, c + 1)
                    pr.did(al.tensor_tensor(p_acc[:, :], p_acc[:, :], in_win[:, :], ALU.add))
                    dve.wait_ge(den_mm, c + 1)
                    pr.link(al.tensor_copy(den_u[:, :, :, :].rearrange("p a t r -> p (a t r)"), bank[6][:, 0:6 * R2]))
                    pr.link(al.tensor_tensor(den_w[:, :, :], den_u[:, :, 0, :], den_u[:, :, 1, :], ALU.add))
                    pr.link(al.tensor_tensor(den_w[:, :, :], den_w[:, :, :], den_u[:, :, 2, :], ALU.add))
                    sums = D[:, bass.ds(n + 2 * s, 2), :]
                    al.tensor_tensor(sums, sums, den_w[:, :, :], ALU.add).then_inc(den_done, 1)
                pr.eng.wait_ge(p_round, (first + S_) * 21)
                al.tensor_copy(row(p_edge, n), p_acc[:, :]).then_inc(p_kept, 1)
                dve.wait_ge(p_kept, n + 1)
            blocks(dve, p_block_)
            dve.wait_ge(den_done, NB * S_)

            dve.wait_ge(self_exp, 1)
            ch.link(al.tensor_tensor(top[:, :, :], D[:, 1:NB + 1, :], D[:, RING + 1:RING + NB + 1, :], ALU.add))
            ch.link(al.tensor_tensor(top[:, :, :], top[:, :, :], ps_[:, :, :], ALU.add))
            ch.link(al.reciprocal(top[:, :, :], top[:, :, :]))
            ch.did(al.tensor_tensor(alpha_self[:, :, :], ps_[:, :, :], top[:, :, :], ALU.mult))
            share = target[:, :, 0:R2]
            ch.did(al.memset(acc[:, :], 0.0))
            ch.link(al.memset(target[:, :, :], 0.0))
            ch.did(al.tensor_copy(target[:, 1:NB + 1, 0:R2], top[:, :, :]))
            ch.link(al.tensor_copy(target[:, RING + 1:RING + NB + 1, 0:R2], top[:, :, :]))
            thirds(ch, share, share16[:, :, 0:R2], share16[:, :, R2:2 * R2], share16[:, :, 2 * R2:3 * R2], target_rest[:, :, 0:R2])
            assert ch.k == SHARE_STEPS, ch.k

            qb = Chain(dve, q_block, 3)
            qr = Chain(dve, q_round, 8)

            def q_block_(n, h, m):
                first = dve.snap(n * S_)
                dve.wait_ge(q_round, first * 8)
                qb.begin(n)
                qb.wait()
                qb.did(al.tensor_copy(key_stage[:, :], row(key0, n)))
                qb.did(al.tensor_copy(v_stage[:, :], row(p_edge, n)))
                qb.did(al.tensor_copy(mask_stage[:, :, :], rel_mask[:, bass.ds(n * TB, TB), :]))
                with dve.Fori(0, S_) as s:
                    c = first + s
                    qb.wait()
                    qr.begin(c)
                    qr.wait()
                    for k in range(TB):
                        last = al.tensor_scalar(hot16[:, k, :], iota16[:, :], key_stage[:, k:k + 1], None, ALU.is_equal)
                    last.then_inc(hot_q, 1)
                    dve.wait_ge(picked_q, c + 1)
                    got = picked[:, :, :, 0:R2]
                    qr.link(al.tensor_copy(got, bank[5][:, 0:TB * 3 * R2].rearrange("p (k a w) -> p k a w", k=TB, a=3)))
                    part = pick_sum[:, :, 0:R2]
                    qr.link(al.tensor_tensor(part, got[:, :, 0, :], got[:, :, 1, :], ALU.add))
                    qr.link(al.tensor_tensor(part, part, got[:, :, 2, :], ALU.add))
                    qr.link(al.tensor_tensor(part, part, mask_stage[:, :, :], ALU.mult))
                    qr.link(al.tensor_reduce(logit[:, :], part, AX, ALU.add))
                    qr.link(al.tensor_tensor(p_stage[:, :], logit[:, :], v_stage[:, :], ALU.mult))
                    for k in range(TB):
                        last = al.tensor_scalar(onehot[:, k, :], iota[:, :], key_stage[:, k:k + 1], p_stage[:, k:k + 1], ALU.is_equal, ALU.mult)
                    last.then_inc(wsum_ready, 1)
                    next_pair(dve, qr)
                    dve.wait_ge(A2.summed, c + 1)
                    dve.wait_ge(A2.acc_done, c)
                    sums = acc[:, bass.ds((n + 2 * s) * P, PAIR)]
                    al.tensor_tensor(sums, sums, bank[7][:, 0:PAIR], ALU.add).then_inc(A2.acc_done, 1)
            blocks(dve, q_block_)
            fold(dve, A2, tails[2], S_)

        block = ctx.enter_context(nc.Block())
        PS = passes

        @block.sync
        def _(sp):
            edge_arrays = ["src", "dst", "edge_type_2", "edge_type_4", "edge_type_8"]
            sp.wait_ge(pads_set, 1)
            full, part = (NCH - 1) * RC * P, (ROWS - 1 - (NCH - 1) * RC)
            for i, name in enumerate(edge_arrays):
                sp.dma_start(edge_rows[:, i, 0:NCH - 1, :], a[name][0:full].rearrange("(q p e) -> p q e", p=RC, e=P)).then_inc(edges_in, 16)
                sp.dma_start(edge_rows[0:part, i, NCH - 1, :], a[name][full:full + part * P].rearrange("(p e) -> p e", e=P)).then_inc(edges_in, 16)
                sp.dma_start(edge_rows[part:part + 1, i, NCH - 1, 0:REST], a[name][full + part * P:E].rearrange("(p e) -> p e", p=1)).then_inc(edges_in, 16)
            for t in range(NB):
                here = min(P, N - t * P)
                sp.dma_start(X[0:here, t, :], a["x"][t * P:t * P + here, :]).then_inc(x_in, 16)
            for l in range(upto + 1):
                if l == 2:
                    keep_rows(sp)
                    reload_rows(sp)
                if l < 3:
                    tail_sp(sp, tails[l])
            if upto == 3:
                store_out(sp, tails[3])
            else:
                tl = tails[upto]
                sp.wait_ge(tl.x_kept, NBATCH)
                for t in range(NB):
                    here = min(P, N - t * P)
                    sp.dma_start(out[t * P:t * P + here, :], X[0:here, t, :]).then_inc(out_stored, 16)
                sp.wait_ge(out_stored, NB * 16)

        @block.gpsimd
        def _(pool):
            nc.gpsimd.iota(iota[:, :], [[1, PAIR]], base=0, channel_multiplier=0, allow_small_or_imprecise_dtypes=True).then_inc(iota_set, 1)
            nc.gpsimd.iota(prow[:, :], [[1, 1]], base=0, channel_multiplier=1, allow_small_or_imprecise_dtypes=True).then_inc(iota_set, 1)
            nc.gpsimd.iota(block_base[:, :], [[P, NB]], base=-P, channel_multiplier=0, allow_small_or_imprecise_dtypes=True).then_inc(iota_set, 1)
            for l in range(upto + 1):
                if l:
                    pool.wait_ge(PS[l].ready, NB * 16)
                gather_pass(pool, PS[l])

        @block.scalar
        def _(act):
            mats = ["L0_gnn_W1", "L0_gnn_W2", "L1_gnn_W_data", "L1_gnn_W_control", "L1_gnn_W_self", "L2_gnn_W_self", "L3_gnn_root_weight"]
            for i, name in enumerate(mats):
                act.dma_start(wraw[:, i, :], a[name]).then_inc(weights_in, 16)
            act.dma_start(wraw[:, 7:7 + R2, :], a["L2_gnn_W_rel"].rearrange("r i o -> i r o")).then_inc(weights_in, 16)
            act.dma_start(wraw[:, 7 + R2:7 + R2 + NBASE, :], a["L3_gnn_weight"].rearrange("r i o -> i r o")).then_inc(weights_in, 16)
            for i, name in enumerate(["L0_gnn_b1", "L0_gnn_gamma", "L0_gnn_beta"]):
                act.dma_start(small[i:i + 1, :], a[name].rearrange("(p n) -> p n", p=1)).then_inc(weights_in, 16)
            act.dma_start(small[3:3 + R2, :], a["L2_gnn_att_src"]).then_inc(weights_in, 16)
            act.dma_start(small[3 + R2:3 + 2 * R2, :], a["L2_gnn_att_dst"]).then_inc(weights_in, 16)
            for i, name in enumerate(["L0_gnn_b2", "L1_gnn_b_data", "L1_gnn_b_control", "L1_gnn_b_self", "L2_gnn_b_self", "L3_gnn_bias"]):
                act.dma_start(rows_b[:, i, :], a[name].rearrange("(p n) -> p n", p=1).to_broadcast([P, F])).then_inc(weights_in, 16)
            act.dma_start(rows_b[:, 6:6 + R2, :].rearrange("p a f -> p (a f)"), a["L2_gnn_b_rel"].rearrange("(p r) n -> p (r n)", p=1).to_broadcast([P, R2 * F])).then_inc(weights_in, 16)
            act.dma_start(wcomp[:, :], a["L3_gnn_w_comp"].rearrange("(p r) n -> p (r n)", p=1).to_broadcast([P, R3 * NBASE])).then_inc(weights_in, 16)

            act.wait_ge(shifts_ready, 1)
            S_ = act.value_load(shifts[0:1, 0:1], min_val=1, max_val=SHIFTS)
            for l in range(upto + 1):
                ps = PS[l]
                if l != 2:
                    stage_indices(act, ps, S_, lambda n, h, m: act.wait_ge(ps.summed, (n + 1) * S_))
                if l == 0:
                    power_act(act)
                    gin_act(act)
                if l == 2:
                    attend_act(act, S_)
                tail_act(act, tails[l])

        @block.tensor
        def _(pe):
            prepare_pe(pe)
            pe.wait_ge(shifts_ready, 1)
            S_ = pe.value_load(shifts[0:1, 0:1], min_val=1, max_val=SHIFTS)
            for l in range(upto + 1):
                if l != 2:
                    sum_pass_pe(pe, PS[l], S_)
                if l == 0:
                    power_pe(pe)
                    gin_pe(pe)
                if l == 2:
                    attend_pe(pe, S_)
                tail_pe(pe, tails[l])

        @block.vector
        def _(dve):
            prepare_dve(dve)
            S_ = dve.value_load(shifts[0:1, 0:1], min_val=1, max_val=SHIFTS)
            for l in range(upto + 1):
                if l != 2:
                    sum_pass_dve(dve, PS[l], S_)
                    fold(dve, PS[l], tails[l], S_)
                if l == 0:
                    power_dve(dve)
                    gin_dve(dve)
                if l == 2:
                    attend_dve(dve, S_)
                tail_dve(dve, tails[l])


_INS = ["x", "src", "dst", "edge_type_2", "edge_type_4", "edge_type_8",
        "L0_gnn_W1", "L0_gnn_b1", "L0_gnn_gamma", "L0_gnn_beta", "L0_gnn_W2", "L0_gnn_b2",
        "L1_gnn_W_data", "L1_gnn_b_data", "L1_gnn_W_control", "L1_gnn_b_control", "L1_gnn_W_self", "L1_gnn_b_self",
        "L2_gnn_W_self", "L2_gnn_b_self", "L2_gnn_W_rel", "L2_gnn_b_rel", "L2_gnn_att_src", "L2_gnn_att_dst",
        "L3_gnn_weight", "L3_gnn_w_comp", "L3_gnn_root_weight", "L3_gnn_bias"]


def kernel(**inputs):
    import numpy as _np
    import concourse.bacc as _bacc
    from concourse import mybir as _mybir
    from concourse.bass_utils import run_bass_kernel_spmd as _run

    nc = _bacc.Bacc("TRN2", target_bir_lowering=False, num_devices=1)
    arrays, aps = {}, {}
    for name in _INS:
        value = _np.ascontiguousarray(inputs[name])
        arrays[f"in_{name}"] = value
        aps[name] = nc.dram_tensor(f"in_{name}", value.shape, _mybir.dt.from_np(value.dtype), kind="ExternalInput").ap()
    out = nc.dram_tensor("out_x", inputs["x"].shape, _mybir.dt.float32, kind="ExternalOutput").ap()
    build_gnn(nc, aps, out)
    r = _run(nc, [arrays], core_ids=[0])
    return r.results[0]["out_x"]
```

```python
from contextlib import ExitStack

import concourse.bass as bass
from concourse import mybir

ALU = mybir.AluOpType
ACT = mybir.ActivationFunctionType
F32 = mybir.dt.float32
BF16 = mybir.dt.bfloat16
I32 = mybir.dt.int32
I16 = mybir.dt.int16
AX = mybir.AxisListType.X

P = 128
EPS = 1e-05
TINY = 1e-12
SLOPE = 0.2
POWER_STEPS = 30
POWER_HALVES = 3
POWER_PAIRS = POWER_STEPS // POWER_HALVES


class Chain:

    def __init__(self, eng, sem, steps=None):
        self.eng, self.sem, self.steps, self.base, self.k = eng, sem, steps, 0, 0

    def begin(self, round_number):
        assert self.steps is not None and self.k in (0, self.steps), (self.k, self.steps)
        self.base, self.k = round_number * self.steps, 0

    def did(self, instruction):
        self.k += 1
        instruction.then_inc(self.sem, 1)

    def wait(self):
        self.eng.wait_ge(self.sem, self.base + self.k)

    def link(self, instruction):
        self.did(instruction)
        self.wait()


def build_gnn(nc, a, out, upto=3):
    N, F = a["x"].shape
    E = a["src"].shape[0]
    R1, R2, R3, NBASE = 2, a["L2_gnn_W_rel"].shape[0], a["L3_gnn_w_comp"].shape[0], a["L3_gnn_weight"].shape[0]
    assert F == P
    NB = -(-N // P)
    NPAD = NB * P
    LAST = N - (NB - 1) * P
    TB = E // N
    LEAD = TB // 2
    SLOTS = NB * TB
    ROWS = -(-E // P)
    REST = E - (ROWS - 1) * P
    TRAIL = SLOTS - LEAD - ROWS
    assert 0 <= TRAIL < TB
    NCH = 4
    RC = ROWS // NCH
    assert RC * NCH == ROWS and RC <= P
    RING = NB + 1 + (NB + 1) % 2
    SHIFTS = RING // 2
    PAIR = 2 * P
    SPAN = RING * P
    ACCT = 2 * RING
    NOBODY = 1 << 20
    NOBODY16 = 30000
    OFF = [(2 * k + 1) * P // (2 * TB) + P // 2 - LEAD * P // TB for k in range(TB)]
    assert OFF[0] >= 0 and OFF[-1] + P <= PAIR
    GW = F + 4
    BATCH = 5
    NBATCH = NB // BATCH
    assert NBATCH * BATCH == NB and NB % 2 == 1
    SW = R2 * 3 + 4

    t1 = nc.dram_tensor("table1", (R1 * NPAD, F), F32).ap()
    t2 = nc.dram_tensor("table2", (R2 * NPAD, GW), F32).ap()
    t3 = nc.dram_tensor("table3", (R3 * NPAD, F), F32).ap()
    kept = nc.dram_tensor("kept_rows", (NB, P, TB * GW), F32).ap()
    dst_rows = nc.dram_tensor("dst_rows", (SLOTS, P), I16).ap()
    pair_rows = nc.dram_tensor("pair_rows", (SLOTS, P), I16).ap()

    with ExitStack() as ctx:
        def sb(name, shape, dt=F32):
            return ctx.enter_context(nc.sbuf_tensor(name, shape, dt))

        def sem(name):
            return ctx.enter_context(nc.semaphore(name))

        psum = ctx.enter_context(nc.psum_tensor("psum", [P, 8, 512], F32))
        bank = [psum[:, i, :] for i in range(8)]

        X = sb("X", [P, NB, F])
        S = sb("S", [P, NB, F])
        acc = sb("acc", [P, ACCT * P])
        featT = acc[:, P:P + NPAD]
        ring = sb("ring", [P, 2, TB, GW])
        onehot = sb("onehot", [P, TB, P])
        idx_stage = sb("idx_stage", [P, 2, TB], I32)
        key_stage = sb("key_stage", [P, TB])
        key_wrap = sb("key_wrap", [P, TB])
        iota = sb("iota", [P, PAIR])
        prow = sb("prow", [P, 1])
        ident = sb("ident", [P, P])
        ones = sb("ones", [P, P])
        block_base = sb("block_base", [P, NB])
        edge_rows = ring[0:RC].rearrange("p h k g -> p (h k g)")[:, 0:5 * NCH * P].bitcast(I32).rearrange(
            "p (a q e) -> p a q e", a=5, q=NCH)
        edge_rows_f = acc[0:RC, 0:5 * NCH * P].rearrange("p (a q e) -> p a q e", a=5, q=NCH)
        edge_rows_p = acc[0:RC, 5 * NCH * P:6 * NCH * P].rearrange("p (q e) -> p q e", q=NCH)
        row16 = sb("row16", [RC, 2, NCH, P], I16)
        fill16 = sb("fill16", [max(LEAD, TRAIL), P], I16)
        tab = sb("tab", [P, 5, SLOTS])
        idx = sb("idx", [P, 4, SLOTS], I32)
        key0 = sb("key0", [P, NB, TB])
        key_win = sb("key_win", [P, NB, TB])
        key_w = sb("key_w", [P, NB, TB])
        off_row = sb("off_row", [P, TB])
        in_pair = sb("in_pair", [P, 2])
        count = sb("count", [1, 2])
        shifts = sb("shifts", [1, 2], I32)
        zeros16 = sb("zeros16", [1, 512], BF16)
        wraw = sb("wraw", [P, 7 + R2 + NBASE, F])
        wT = sb("wT", [P, 5 + R2, F])
        small = sb("small", [3 + 2 * R2, F])
        smallT = sb("smallT", [P, 3 + 2 * R2])
        rows_b = sb("rows_b", [P, 6 + R2, F])
        wcomp = sb("wcomp", [P, R3 * NBASE])
        wcat2 = sb("wcat2", [P, F + 2 * R2])
        wcat3 = sb("wcat3", [P, R3, F])
        tb = sb("tb", [P, BATCH, R3 * F])
        XT = tb[:, :, :].rearrange("p a b -> p (a b)")[:, 0:NPAD]
        stg = sb("stg", [P, BATCH, F])
        y = sb("y", [P, BATCH, F])
        xn = sb("xn", [P, BATCH, F])
        xt = sb("xt", [P, BATCH, F])
        st6 = sb("st6", [P, BATCH, 6])
        mv = sb("mv", [P, BATCH, 2])
        rstd = sb("rstd", [P, BATCH])
        eps = sb("eps", [P, 1])
        u = sb("u", [P, 2])
        v = sb("v", [P, 2])
        raw = sb("raw", [P, 2])
        sq = sb("sq", [P, 2])
        nrm = sb("nrm", [P, 2])
        inv_sigma = sb("inv_sigma", [P, 2])
        NCHK = -(-N // 512)
        bn6 = sb("bn6", [P, NCHK, 6])
        bnmv = sb("bnmv", [P, 2])
        bn_scale = sb("bn_scale", [P, 1])
        bn_shift = sb("bn_shift", [P, 1])

        pads_set = sem("pads_set")
        edges_in = sem("edges_in")
        x_in = sem("x_in")
        weights_in = sem("weights_in")
        iota_set = sem("iota_set")
        v_prep = sem("v_prep")
        edges_f = sem("edges_f")
        rows16_set = sem("rows16_set")
        rows16_kept = sem("rows16_kept")
        edge_tr = sem("edge_tr")
        edge_ev = sem("edge_ev")
        ident_set = sem("ident_set")
        idx_ready = sem("idx_ready")
        match_summed = sem("match_summed")
        match_total = sem("match_total")
        shifts_ready = sem("shifts_ready")
        w_tr = sem("w_tr")
        w_ev = sem("w_ev")
        x_tr = sem("x_tr")
        x_ev = sem("x_ev")
        wa_done = sem("wa_done")
        weights_ready = sem("weights_ready")
        pw_pe = sem("pw_pe")
        pw_act = sem("pw_act")
        pw_v = sem("pw_v")
        out_stored = sem("out_stored")
        dve_turn = sem("dve_turn")

        def blocks(eng, body):
            with eng.Fori(0, NB // 2) as m:
                body(2 * m, 0, m)
                body(2 * m + 1, 1, m)
            body(NB - 1, 0, NB // 2)

        def blocks_between(eng, body, steps):
            at = POWER_PAIRS
            with eng.Fori(0, at) as m:
                for h in range(2):
                    body(2 * m + h, h, m, lambda: steps(m * (2 * POWER_HALVES) + h * POWER_HALVES, h * POWER_HALVES))
            with eng.Fori(at, NB // 2) as m:
                for h in range(2):
                    body(2 * m + h, h, m, None)
            body(NB - 1, 0, NB // 2, None)

        USES = [NB - NB // 2, NB // 2]
        staged = [sem(f"staged{h}") for h in range(2)]
        gathered = [sem(f"gathered{h}") for h in range(2)]
        pool_go = sem("pool_go")

        sum_sems = [sem(name) for name in ("hot", "summed", "acc_done")]
        attend_sems = [sem(name) for name in ("max_hot", "weighted", "weighted_done")]
        key_staged = sem("key_staged")
        key_shift = sem("key_shift")
        acc_zero = sem("acc_zero")

        class Pass:
            def __init__(self, n, table, idx_row, width):
                self.n, self.table, self.idx_row, self.width = n, table, idx_row, width
                self.staged, self.gathered, self.go = staged, gathered, pool_go
                self.before = NB * [0, 1, 0, 2][n]
                self.hot, self.summed, self.acc_done = attend_sems if n == 2 else sum_sems
                self.key_staged, self.key_shift, self.acc_zero = key_staged, key_shift, acc_zero
                if n:
                    self.ready = sem(f"table_ready{n}")

            def staged_by(self, h, m):
                return m + (1 + self.n * USES[h])

            def gathered_by(self, h, m):
                skipped = 0 if h else LEAD
                last = isinstance(m, int) and m == USES[0] - 1
                before = self.n * (USES[h] * TB - (0 if h else LEAD + TRAIL))
                return (m + 1) * (16 * TB) + 16 * (before - skipped - (TRAIL if last else 0))

        passes = [Pass(0, a["x"], 0, F), Pass(1, t1, 1, F), Pass(2, t2, 2, GW), Pass(3, t3, 3, F)]

        def stage_indices(act, ps, T_, steps=None):
            def stage(n, h):
                nc.scalar.copy(idx_stage[:, h, :], idx[:, ps.idx_row, bass.ds(n * TB, TB)]).then_inc(ps.staged[h], 1)

            def ahead(m, h, power):
                if power:
                    steps(m * (2 * POWER_HALVES) + h * POWER_HALVES, h * POWER_HALVES)
                act.wait_ge(ps.summed, (2 * m + (ps.before + h + 1)) * T_)
                stage(2 * m + 2 + h, h)
            act.wait_ge(idx_ready, 1)
            stage(0, 0)
            stage(1, 1)
            at = POWER_PAIRS if steps else 0
            if steps:
                with act.Fori(0, at) as m:
                    for h in range(2):
                        ahead(m, h, True)
            with act.Fori(at, NB // 2 - 1) as m:
                for h in range(2):
                    ahead(m, h, False)
            ahead(NB // 2 - 1, 0, False)

        def gather_pass(pool, ps):
            def block(n, h, m, tiles):
                pool.wait_ge(ps.staged[h], ps.staged_by(h, m))
                pool.sem_inc(ps.go, 1)
                for k in tiles:
                    pool.indirect_dma_start(
                        ring[:, h, k, 0:ps.width], None, ps.table,
                        bass.IndirectOffsetOnAxis(ap=idx_stage[:, h, k:k + 1], axis=0)).then_inc(ps.gathered[h], 16)
            block(0, 0, 0, range(LEAD, TB))
            block(1, 1, 0, range(TB))
            with pool.Fori(1, NB // 2) as m:
                block(2 * m, 0, m, range(TB))
                block(2 * m + 1, 1, m, range(TB))
            block(NB - 1, 0, NB // 2, range(TB - TRAIL))

        def window_sums(c, b, lhs, width):
            nc.tensor.matmul(bank[b][0:width, 0:PAIR], zeros16[:, 0:width], zeros16[:, 0:PAIR], start=True, stop=False, skip_group_check=True)
            for k in range(TB):
                a_, b_ = lhs(k)
                mm = nc.tensor.matmul(bank[b][0:width, OFF[k]:OFF[k] + P], a_, b_, start=False, stop=(k == TB - 1), skip_group_check=True)
            return mm

        def sum_pass_pe(pe, ps, T_, steps=None):
            def block(n, h, m, power=None):
                if power:
                    power()
                first = pe.snap((n + ps.before) * T_)
                with pe.Fori(0, T_) as t:
                    c = first + t
                    pe.wait_ge(ps.gathered[h], ps.gathered_by(h, m))
                    pe.wait_ge(ps.hot, c + 1)
                    pe.wait_ge(ps.acc_done, c)
                    window_sums(c, 0, lambda k: (ring[:, h, k, 0:F], onehot[:, k, :]), P).then_inc(ps.summed, 1)
            if steps:
                blocks_between(pe, block, steps)
            else:
                blocks(pe, block)

        def all_onehots(hot):
            return nc.vector.tensor_tensor(
                hot[:, :, :], iota[:, 0:P].rearrange("p (o n) -> p o n", o=1).to_broadcast([P, TB, P]),
                key_stage[:, :].rearrange("p (k o) -> p k o", o=1).to_broadcast([P, TB, P]), ALU.is_equal)

        def next_window(chain, width):
            chain.link(nc.vector.tensor_scalar(key_wrap[:, :], key_stage[:, :], float(width), float(SPAN), ALU.is_lt, ALU.mult))
            chain.did(nc.vector.scalar_tensor_tensor(key_stage[:, :], key_stage[:, :], float(-width), key_wrap[:, :], ALU.add, ALU.add))

        def sum_pass_dve(dve, ps, T_, steps=None):
            nc.vector.memset(acc[:, :], 0.0).then_inc(ps.acc_zero, 1)
            dve.wait_ge(ps.acc_zero, ps.before // NB + 1)
            keys = Chain(dve, ps.key_shift, 2)

            def block(n, h, m, power=None):
                if power:
                    power()
                first = dve.snap((n + ps.before) * T_)
                dve.wait_ge(ps.key_shift, first * 2)
                nc.vector.tensor_copy(key_stage[:, :], row(key_win, n)).then_inc(ps.key_staged, 1)
                with dve.Fori(0, T_) as t:
                    dve.wait_ge(ps.key_staged, n + (ps.before + 1))
                    keys.begin(first + t)
                    keys.wait()
                    all_onehots(onehot).then_inc(ps.hot, 1)
                    next_window(keys, P)
                    dve.wait_ge(ps.summed, first + t + 1)
                    dve.wait_ge(ps.acc_done, first + t)
                    sums = acc[:, bass.ds((n + t) * P, PAIR)]
                    nc.vector.tensor_tensor(sums, sums, bank[0][:, 0:PAIR], ALU.add).then_inc(ps.acc_done, 1)
            if steps:
                blocks_between(dve, block, steps)
            else:
                blocks(dve, block)

        def row(t, n):
            return t[:, bass.ds(n, 1), :].rearrange("p a k -> p (a k)")

        class Tail:
            def __init__(self, l):
                self.l = l
                self.uses = 2 if l == 2 else 1
                self.next = passes[l + 1] if l < 3 else None
                self.lhs = sem(f"lhs{l}")
                self.own = sem(f"own{l}")
                self.y_read = sem(f"y_read{l}")
                self.stats = sem(f"stats{l}")
                self.rooted = sem(f"rooted{l}")
                self.normed = sem(f"normed{l}")
                if l < 3:
                    self.x_kept = sem(f"x_kept{l}")
                    self.turned = sem(f"turned{l}")
                    self.turned_ev = sem(f"turned_ev{l}")
                    self.tabled = sem(f"tabled{l}")
                if l < 2:
                    self.ev_dve = sem(f"ev_dve{l}")
                if l in (1, 2):
                    self.ev_act = sem(f"ev_act{l}")
                self.chain = sem(f"tail_chain{l}")
                self.folded = sem(f"folded{l}")
                if l == 2:
                    self.h_in = sem(f"h_in{l}")

        tails = [Tail(l) for l in range(upto + 1)]
        psA = psum[:, 0:2, :].rearrange("p a b -> p (a b)")[:, 0:BATCH * F].rearrange("p (j f) -> p j f", f=F)
        psT = psum[:, 2:4, :].rearrange("p a b -> p (a b)")[:, 0:BATCH * F].rearrange("p (j f) -> p j f", f=F)
        SETS = [[4, 5], [6, 7]]
        h_self = ring[:, :, :, :].rearrange("p a b c -> p (a b c)")[:, 0:BATCH * R2 * GW].rearrange(
            "p (j r g) -> p j r g", j=BATCH, r=R2)

        def tile_batch(t, b):
            return t[:, bass.ds(b * BATCH, BATCH), :]

        def fold(dve, ps, tl, T_):
            dve.wait_ge(ps.acc_done, (NB + ps.before) * T_)
            nc.vector.tensor_tensor(featT, featT, acc[:, (RING + 1) * P:(RING + 1) * P + NPAD], ALU.add).then_inc(tl.folded, 1)

        def tail_act(act, tl):
            l = tl.l
            act.wait_ge(tl.folded, 1)
            with act.Fori(0, NBATCH) as b:
                act.wait_ge(tl.own, b * tl.uses)
                src_ = featT[:, bass.ds(b * (BATCH * P), BATCH * P)]
                dst_ = stg[:, :, :].rearrange("p j f -> p (j f)")
                if l == 0:
                    nc.scalar.activation(dst_, src_, ACT.Identity, bias=bn_shift[:, :], scale=bn_scale[:, :]).then_inc(tl.lhs, 1)
                else:
                    nc.scalar.copy(dst_, src_).then_inc(tl.lhs, 1)
                act.wait_ge(tl.stats, b + 1)
                nc.scalar.activation(rstd[:, :], mv[:, :, 1], ACT.Sqrt, bias=eps[:, :]).then_inc(tl.rooted, 1)
                if l == 3:
                    return
                act.wait_ge(tl.normed, b + 1)
                nc.scalar.copy(tile_batch(X, b), xn[:, :, :]).then_inc(tl.x_kept, 1)
                act.wait_ge(tl.turned, b + 1)
                act.wait_ge(tl.tabled, b * BATCH)
                nc.scalar.copy(xt[:, :, :], psT).then_inc(tl.turned_ev, 1)
                if l == 0:
                    return
                act.wait_ge(tl.next.ready, b * (BATCH * 16))
                for j in range(BATCH):
                    act.wait_ge(tl.tabled, b * BATCH + (j + 1))
                    s0 = SETS[j % 2]
                    if l == 1:
                        tv = tb[:, j, 0:R2 * GW].rearrange("p (r g) -> p r g", r=R2)
                        nc.scalar.copy(tv[:, :, 0:F], bank[s0[0]].rearrange("p (r f) -> p r f", r=R2)).then_inc(tl.ev_act, 1)
                    else:
                        half = R3 // 2 * F
                        nc.scalar.copy(tb[:, j, 0:half], bank[s0[0]])
                        nc.scalar.copy(tb[:, j, half:2 * half], bank[s0[1]]).then_inc(tl.ev_act, 1)

        def tail_pe(pe, tl):
            l = tl.l
            with pe.Fori(0, NBATCH) as b:
                pe.wait_ge(tl.lhs, b + 1)
                pe.wait_ge(tl.y_read, b * tl.uses)
                for j in range(BATCH):
                    mm = nc.tensor.matmul(psA[:, j, :], stg[:, j, :], (wT[:, 1, :] if l == 0 else ident[:, :]), start=True, stop=True)
                mm.then_inc(tl.own, 1)
                if l == 3:
                    return
                pe.wait_ge(tl.normed, b + 1)
                pe.wait_ge(tl.turned_ev, b)
                for j in range(BATCH):
                    mm = nc.tensor.transpose(psT[:, j, :], xn[:, j, :], ident[:, :])
                mm.then_inc(tl.turned, 1)
                pe.wait_ge(tl.turned_ev, b + 1)
                if l == 2:
                    pe.wait_ge(tl.y_read, b * 2 + 1)
                    for j in range(BATCH):
                        mm = nc.tensor.matmul(psA[:, j, :], xt[:, j, :], wraw[:, 6, :], start=True, stop=True)
                    mm.then_inc(tl.own, 1)
                for j in range(BATCH):
                    before = b * BATCH + (j - 1 if j >= 2 else 0)
                    if l < 2:
                        pe.wait_ge(tl.ev_dve, before)
                    if l > 0:
                        pe.wait_ge(tl.ev_act, before)
                    s0 = SETS[j % 2]
                    x_j = xt[:, j, :]
                    if l == 0:
                        mm = nc.tensor.matmul(bank[s0[0]][:, 0:3 * F], x_j, wT[:, 2:5, :].rearrange("p a f -> p (a f)"), start=True, stop=True)
                    elif l == 1:
                        nc.tensor.matmul(bank[s0[0]], x_j, wraw[:, 7:7 + R2, :].rearrange("p a f -> p (a f)"), start=True, stop=True)
                        mm = nc.tensor.matmul(bank[s0[1]][:, 0:F + 2 * R2], x_j, wcat2[:, :], start=True, stop=True)
                    else:
                        for c in range(2):
                            mm = nc.tensor.matmul(bank[s0[c]], x_j, wcat3[:, 4 * c:4 * c + 4, :].rearrange("p a f -> p (a f)"), start=True, stop=True)
                    mm.then_inc(tl.tabled, 1)

        def tail_dve(dve, tl):
            l = tl.l
            steps = {0: 2, 1: 3, 2: 2 + 1 + R2, 3: 3}[l]
            chain = Chain(dve, tl.chain, steps)
            if l > 0:
                if l < 3:
                    dve.wait_ge(tails[l - 1].ev_dve, NB)
                else:
                    dve.wait_ge(tails[2].y_read, NBATCH * 2)
                dve.wait_ge(tails[l - 1].x_kept, NBATCH)
            else:
                dve.wait_ge(x_ev, -(-NB // 4) + 1)
            if l == 1:
                dve.wait_ge(passes[1].ready, NB * 16)
                for j in range(BATCH):
                    nc.vector.memset(tb[:, j, 0:R2 * GW].rearrange("p (r g) -> p r g", r=R2)[:, :, F + 1:GW], 0.0)
            with dve.Fori(0, NBATCH) as b:
                chain.begin(b)
                dve.wait_ge(tl.own, b * tl.uses + 1)
                dve.wait_ge(tl.normed, b)
                if l == 0:
                    nc.vector.tensor_tensor(y[:, :, :], psA, tile_batch(X, b), ALU.add).then_inc(tl.y_read, 1)
                    dve.wait_ge(tl.y_read, b * tl.uses + 1)
                elif l in (1, 3):
                    nc.vector.tensor_tensor(y[:, :, :], psA, tile_batch(S, b), ALU.add).then_inc(tl.y_read, 1)
                    dve.wait_ge(tl.y_read, b * tl.uses + 1)
                    chain.link(nc.vector.scalar_tensor_tensor(y[:, :, :], y[:, :, :], 0.0, tile_batch(X, b), ALU.max, ALU.add))
                else:
                    nc.vector.tensor_tensor(y[:, :, :], psA, tile_batch(S, b), ALU.add).then_inc(tl.y_read, 1)
                    dve.wait_ge(tl.y_read, b * tl.uses + 1)
                    chain.link(nc.vector.tensor_tensor(y[:, :, :], y[:, :, :], tile_batch(X, b), ALU.add))
                    nc.vector.tensor_copy(al_stage[:, :, :], tile_batch(alpha_self, b)).then_inc(al_staged, 1)
                    dve.wait_ge(al_staged, b + 1)
                    dve.wait_ge(tl.h_in, (b + 1) * (16 * BATCH))
                    for r in range(R2):
                        for j in range(BATCH):
                            last = nc.vector.scalar_tensor_tensor(y[:, j, :], h_self[:, j, r, 0:F], al_stage[:, j, r:r + 1], y[:, j, :], ALU.mult, ALU.add)
                        chain.link(last)
                for j in range(BATCH):
                    last = nc.vector.bn_stats(st6[:, j, :], y[:, j, :])
                chain.link(last)
                dve.sem_inc(dve_turn, 1)
                for j in range(BATCH):
                    last = nc.vector.bn_aggr(mv[:, j, :], st6[:, j, :])
                last.then_inc(tl.stats, 1)
                dve.wait_ge(tl.rooted, b + 1)
                chain.link(nc.vector.reciprocal(rstd[:, :], rstd[:, :]))
                if l < 3:
                    dve.wait_ge(tl.x_kept, b)
                    dve.wait_ge(tl.turned, b)
                else:
                    dve.wait_ge(out_stored, b * 16 * BATCH)
                for j in range(BATCH):
                    last = nc.vector.tensor_scalar(xn[:, j, :], y[:, j, :], mv[:, j, 0:1], rstd[:, j:j + 1], ALU.subtract, ALU.mult)
                last.then_inc(tl.normed, 1)
                if l == 3:
                    return
                if l == 2:
                    dve.wait_ge(tl.own, b * 2 + 2)
                    nc.vector.tensor_tensor(tile_batch(S, b), psA, rows_b[:, 5:6, :].to_broadcast([P, BATCH, F]), ALU.add).then_inc(tl.y_read, 1)
                    return
                for j in range(BATCH):
                    t = b * BATCH + j
                    dve.wait_ge(tl.tabled, t + 1)
                    if l == 0:
                        if j == 0:
                            dve.wait_ge(tl.next.ready, b * (BATCH * 16))
                        pst = bank[SETS[j % 2][0]]
                        nc.vector.tensor_tensor(tb[:, j, 0:2 * F], pst[:, 0:2 * F], rows_b[:, 1:3, :].rearrange("p a f -> p (a f)"), ALU.add)
                        nc.vector.tensor_tensor(row(S, t), pst[:, 2 * F:3 * F], rows_b[:, 3, :], ALU.add).then_inc(tl.ev_dve, 1)
                    elif l == 1:
                        pst = bank[SETS[j % 2][1]]
                        if j == 0:
                            dve.wait_ge(tl.next.ready, b * (BATCH * 16))
                        nc.vector.tensor_copy(row(scores, t), pst[:, F:F + 2 * R2])
                        nc.vector.tensor_copy(tb[:, j, 0:R2 * GW].rearrange("p (r g) -> p r g", r=R2)[:, :, F], pst[:, F:F + R2])
                        nc.vector.tensor_tensor(row(S, t), pst[:, 0:F], rows_b[:, 4, :], ALU.add).then_inc(tl.ev_dve, 1)

        def tail_sp(sp, tl):
            l = tl.l
            with sp.Fori(0, NBATCH) as b:
                if l == 2:
                    own_rows(sp, b)
                for j in range(BATCH):
                    t = b * BATCH + j
                    if l < 2:
                        sp.wait_ge(tl.ev_dve, t + 1)
                    if l > 0:
                        sp.wait_ge(tl.ev_act, t + 1)
                    if l == 0:
                        dst_ = t1.rearrange("(r n) f -> n r f", r=R1)[bass.ds(t * P, P), :, :]
                        src_ = tb[:, j, 0:R1 * F].rearrange("p (r f) -> p r f", r=R1)
                    elif l == 1:
                        dst_ = t2.rearrange("(r n) f -> n r f", r=R2)[bass.ds(t * P, P), :, :]
                        src_ = tb[:, j, 0:R2 * GW].rearrange("p (r f) -> p r f", r=R2)
                    else:
                        dst_ = t3.rearrange("(r n) f -> n r f", r=R3)[bass.ds(t * P, P), :, :]
                        src_ = tb[:, j, 0:R3 * F].rearrange("p (r f) -> p r f", r=R3)
                    sp.dma_start(dst_, src_).then_inc(tl.next.ready, 16)

        def store_out(sp, tl):
            with sp.Fori(0, NBATCH - 1) as b:
                sp.wait_ge(tl.normed, b + 1)
                for j in range(BATCH):
                    sp.dma_start(out[bass.ds((b * BATCH + j) * P, P), :], xn[:, j, :]).then_inc(out_stored, 16)
            sp.wait_ge(tl.normed, NBATCH)
            for j in range(BATCH):
                t = (NBATCH - 1) * BATCH + j
                here = min(P, N - t * P)
                sp.dma_start(out[t * P:t * P + here, :], xn[0:here, j, :]).then_inc(out_stored, 16)
            sp.wait_ge(out_stored, NB * 16)

        def prepare_dve(dve):
            ch = Chain(dve, v_prep)
            for i in range(5):
                nc.vector.memset(edge_rows[:, i, NCH - 1, :], NOBODY if i == 1 else 0)
                nc.vector.memset(tab[:, i, 0:LEAD], float(NOBODY) if i == 1 else 0.0)
                nc.vector.memset(tab[:, i, LEAD + ROWS:SLOTS], float(NOBODY) if i == 1 else 0.0)
            nc.vector.memset(X[:, NB - 1, :], 0.0).then_inc(pads_set, 1)
            nc.vector.memset(ones[:, :], 1.0)
            nc.vector.memset(eps[:, :], EPS)
            nc.vector.memset(u[:, :], float(P) ** -0.5)
            dve.wait_ge(iota_set, 4)
            nc.vector.tensor_scalar(ident[:, :], iota[:, 0:P], prow[:, :], None, ALU.is_equal).then_inc(ident_set, 1)
            dve.wait_ge(edges_in, 16 * 15)
            nc.vector.tensor_copy(edge_rows_f, edge_rows[:, :, :, :]).then_inc(edges_f, 1)
            nc.vector.memset(fill16[:, :], NOBODY16)
            dve.wait_ge(edges_f, 1)
            nc.vector.memset(ring[:, 0, 0:LEAD, :], 0.0)
            nc.vector.tensor_scalar(row16[:, 0, :, :], edge_rows_f[:, 1, :, :], float(NOBODY16), None, ALU.min)
            ch.link(nc.vector.scalar_tensor_tensor(edge_rows_p, edge_rows_f[:, 3, :, :], float(NPAD), edge_rows_f[:, 1, :, :], ALU.mult, ALU.add))
            nc.vector.tensor_scalar(row16[:, 1, :, :], edge_rows_p, float(NOBODY16), None, ALU.min).then_inc(rows16_set, 1)
            for i in range(5):
                dve.wait_ge(edge_tr, i + 1)
                last = nc.vector.tensor_copy(tab[:, i, LEAD:LEAD + ROWS], bank[i][:, 0:ROWS])
            last.then_inc(edge_ev, 1)
            dve.wait_ge(edge_ev, 1)
            nc.vector.tensor_copy(idx[:, 0, :], tab[:, 0, :])
            for i in range(1, 4):
                last = nc.vector.scalar_tensor_tensor(idx[:, i, :], tab[:, 1 + i, :], float(NPAD), tab[:, 0, :], ALU.mult, ALU.add)
            last.then_inc(idx_ready, 1)
            base = block_base[:, :].rearrange("p (b o) -> p b o", o=1).to_broadcast([P, NB, TB])
            dst_f = tab[:, 1, :].rearrange("p (b k) -> p b k", k=TB)
            ch.link(nc.vector.tensor_tensor(key_w[:, :, :], dst_f, base, ALU.subtract))
            ch.link(nc.vector.tensor_scalar(key0[:, :, :], key_w[:, :, :], 0.0, float(SPAN), ALU.is_lt, ALU.mult))
            ch.link(nc.vector.tensor_tensor(key0[:, :, :], key0[:, :, :], key_w[:, :, :], ALU.add))
            for k in range(TB):
                last = nc.vector.memset(off_row[:, k:k + 1], float(OFF[k]))
            ch.link(last)
            offs = off_row[:, :].rearrange("p (o k) -> p o k", o=1).to_broadcast([P, NB, TB])
            ch.link(nc.vector.tensor_tensor(key_w[:, :, :], key0[:, :, :], offs, ALU.subtract))
            ch.link(nc.vector.tensor_scalar(key_win[:, :, :], key_w[:, :, :], 0.0, float(SPAN), ALU.is_lt, ALU.mult))
            ch.link(nc.vector.tensor_tensor(key_win[:, :, :], key_win[:, :, :], key_w[:, :, :], ALU.add))
            ch.link(nc.vector.tensor_scalar(key_w[:, :, :], key0[:, :, :], float(PAIR), None, ALU.is_lt))
            ch.link(nc.vector.tensor_reduce(in_pair[:, 0:1], key_w[:, :, :].rearrange("p b k -> p (b k)"), AX, ALU.add))
            ch.link(nc.vector.tensor_scalar(key_w[:, :, :], key_win[:, :, :], float(P), None, ALU.is_lt))
            nc.vector.memset(zeros16[:, :], 0.0)
            nc.vector.tensor_reduce(in_pair[:, 1:2], key_w[:, :, :].rearrange("p b k -> p (b k)"), AX, ALU.add).then_inc(match_summed, 1)
            dve.wait_ge(match_total, 1)
            for i, rounds in enumerate((SHIFTS, 2 * SHIFTS)):
                last = nc.vector.tensor_scalar(count[:, i:i + 1], bank[5][0:1, i:i + 1], float(E), float(1 - rounds), ALU.is_equal, ALU.mult)
            ch.link(last)
            for i, rounds in enumerate((SHIFTS, 2 * SHIFTS)):
                last = nc.vector.tensor_scalar(shifts[:, i:i + 1], count[:, i:i + 1], float(rounds), None, ALU.add)
            last.then_inc(shifts_ready, 1)
            dve.wait_ge(weights_in, 16 * WEIGHT_LOADS)
            for g in range(3):
                dve.wait_ge(w_tr, g + 1)
                n = min(4, 5 + R2 - 4 * g)
                nc.vector.tensor_copy(wT[:, 4 * g:4 * g + n, :].rearrange("p a f -> p (a f)"), bank[5 + g][:, 0:n * P])
            dve.wait_ge(w_tr, 4)
            nc.vector.tensor_copy(smallT[:, :], bank[4][:, 0:3 + 2 * R2])
            nc.vector.tensor_copy(wcat2[:, 0:F], wraw[:, 5, :]).then_inc(w_ev, 1)
            for r in range(R2):
                ch.link(nc.vector.tensor_tensor(rows_b[:, 4, :], rows_b[:, 4, :], rows_b[:, 6 + r, :], ALU.add))
            for k in range(NBASE):
                for r in range(R3):
                    w = wcomp[:, r * NBASE + k:r * NBASE + k + 1]
                    base_k = wraw[:, 7 + R2 + k, :]
                    if k == 0:
                        last = nc.vector.tensor_scalar(wcat3[:, r, :], base_k, w, None, ALU.mult)
                    else:
                        last = nc.vector.scalar_tensor_tensor(wcat3[:, r, :], base_k, w, wcat3[:, r, :], ALU.mult, ALU.add)
                ch.link(last)
            dve.wait_ge(wa_done, 1)
            nc.vector.tensor_copy(wcat2[:, F:F + 2 * R2], bank[4][:, 64:64 + 2 * R2]).then_inc(weights_ready, 1)
            for g in range(-(-NB // 4)):
                dve.wait_ge(x_tr, g + 1)
                n = min(4, NB - 4 * g)
                nc.vector.tensor_copy(XT[:, 4 * g * P:(4 * g + n) * P], bank[1 + g % 2][:, 0:n * P]).then_inc(x_ev, 1)
            ch.wait()
            nc.vector.tensor_tensor(X[:, :, :], X[:, :, :], rows_b[:, 0:1, :].to_broadcast([P, NB, F]), ALU.add).then_inc(x_ev, 1)

        WEIGHT_LOADS = 7 + 2 + 3 + 2 + 6 + 1 + 1

        def prepare_pe(pe):
            pe.wait_ge(ident_set, 1)
            pe.wait_ge(edges_f, 1)
            for i in range(5):
                for q in range(NCH):
                    tr = nc.tensor.transpose(bank[i][:, q * RC:(q + 1) * RC], edge_rows_f[:, i, q, :], ident[0:RC, 0:RC])
                tr.then_inc(edge_tr, 1)
            pe.wait_ge(match_summed, 1)
            nc.tensor.matmul(bank[5][0:1, 0:2], ones[:, 0:1], in_pair[:, :], start=True, stop=True).then_inc(match_total, 1)
            pe.wait_ge(shifts_ready, 1)
            pe.wait_ge(weights_in, 16 * WEIGHT_LOADS)
            order = list(range(5)) + list(range(7, 7 + R2))
            for g in range(3):
                for i, w in enumerate(order[4 * g:4 * g + 4]):
                    tr = nc.tensor.transpose(bank[5 + g][:, i * P:(i + 1) * P], wraw[:, w, :], ident[:, :])
                tr.then_inc(w_tr, 1)
            nc.tensor.transpose(bank[4][:, 0:3 + 2 * R2], small[:, :], ident[0:3 + 2 * R2, 0:3 + 2 * R2]).then_inc(w_tr, 1)
            pe.wait_ge(w_ev, 1)
            for r in range(R2):
                mm = nc.tensor.matmul(bank[4][:, 64 + r:64 + r + R2 + 1:R2], wT[:, 5 + r, :], smallT[:, 3 + r:3 + r + R2 + 1:R2], start=True, stop=True)
            mm.then_inc(wa_done, 1)
            pe.wait_ge(x_in, 16 * NB)
            for g in range(-(-NB // 4)):
                if g >= 2:
                    pe.wait_ge(x_ev, g - 1)
                for i in range(min(4, NB - 4 * g)):
                    tr = nc.tensor.transpose(bank[1 + g % 2][:, i * P:(i + 1) * P], X[:, 4 * g + i, :], ident[:, :])
                tr.then_inc(x_tr, 1)

        PW = 5

        def half_pe(pe, i, odd):
            weights, vec = (wT, v) if odd else (wraw, u)
            pe.wait_ge(pw_v, i * PW)
            for c in range(2):
                mm = nc.tensor.matmul(bank[7][:, c:c + 1], weights[:, c, :], vec[:, c:c + 1], start=True, stop=True)
            mm.then_inc(pw_pe, 1)
            pe.wait_ge(pw_v, i * PW + 2)
            nc.tensor.matmul(bank[6][:, 2:4], ones[:, :], sq[:, :], start=True, stop=True).then_inc(pw_pe, 1)

        def half_act(act, i, odd):
            act.wait_ge(pw_pe, i * 2 + 2)
            nc.scalar.activation(nrm[:, :], bank[6][:, 2:4], ACT.Sqrt).then_inc(pw_act, 1)

        def half_dve(dve, i, odd):
            dest = u if odd else v
            ch = Chain(dve, pw_v, PW)
            ch.begin(i)
            dve.wait_ge(pw_pe, i * 2 + 1)
            ch.link(nc.vector.tensor_copy(raw[:, :], bank[7][:, 0:2]))
            ch.did(nc.vector.tensor_tensor(sq[:, :], raw[:, :], raw[:, :], ALU.mult))
            dve.wait_ge(pw_act, i + 1)
            ch.link(nc.vector.tensor_scalar(nrm[:, :], nrm[:, :], TINY, None, ALU.add))
            ch.link(nc.vector.reciprocal(nrm[:, :], nrm[:, :]))
            ch.did(nc.vector.tensor_tensor(dest[:, :], raw[:, :], nrm[:, :], ALU.mult))

        def steps_of(eng, half):
            def steps(first, parity):
                for k in range(POWER_HALVES):
                    half(eng, first + k, (parity + k) % 2)
            return steps

        def power_steps_pe(pe):
            return steps_of(pe, half_pe)

        def power_steps_act(act):
            return steps_of(act, half_act)

        def power_steps_dve(dve):
            return steps_of(dve, half_dve)

        def power_pe(pe):
            n = 2 * POWER_STEPS
            half_pe(pe, n, 0)
            pe.wait_ge(pw_v, (n + 1) * PW)
            for c in range(2):
                mm = nc.tensor.matmul(bank[7][:, c:c + 1], wT[:, c, :], v[:, c:c + 1], start=True, stop=True)
            mm.then_inc(pw_pe, 1)
            pe.wait_ge(pw_v, (n + 1) * PW + 1)
            nc.tensor.matmul(bank[6][:, 2:4], ones[:, :], sq[:, :], start=True, stop=True).then_inc(pw_pe, 1)

        def power_act(act):
            half_act(act, 2 * POWER_STEPS, 0)

        def power_dve(dve):
            n = 2 * POWER_STEPS
            half_dve(dve, n, 0)
            ch = Chain(dve, pw_v, PW)
            ch.begin(n + 1)
            dve.wait_ge(pw_pe, (n + 1) * 2 + 1)
            ch.did(nc.vector.tensor_tensor(sq[:, :], bank[7][:, 0:2], u[:, :], ALU.mult))
            dve.wait_ge(pw_pe, (n + 1) * 2 + 2)
            ch.link(nc.vector.reciprocal(inv_sigma[:, :], bank[6][:, 2:4]))
            nc.vector.tensor_scalar(wT[:, 1, :], wT[:, 1, :], inv_sigma[:, 1:2], None, ALU.mult).then_inc(sigma_ready, 1)

        sigma_ready = sem("sigma_ready")
        gin_mm = sem("gin_mm")
        gin_relu = sem("gin_relu")
        gin_stats = sem("gin_stats")
        gin_root = sem("gin_root")
        gin_norm = sem("gin_norm")
        gin_ready = sem("gin_ready")
        x_added = sem("x_added")

        def chunks():
            return [(c, c * 512, min(512, NPAD - c * 512)) for c in range(-(-NPAD // 512))]

        def gin_pe(pe):
            pe.wait_ge(x_added, 1)
            for c, at, w in chunks():
                if c >= 2:
                    pe.wait_ge(gin_relu, c - 1)
                nc.tensor.matmul(bank[1 + c % 2][:, 0:w], wT[:, 0, :], featT[:, at:at + w], start=True, stop=True).then_inc(gin_mm, 1)

        def gin_act(act):
            act.wait_ge(sigma_ready, 1)
            for c, at, w in chunks():
                act.wait_ge(gin_mm, c + 1)
                nc.scalar.activation(featT[:, at:at + w], bank[1 + c % 2][:, 0:w], ACT.Relu, bias=smallT[:, 0:1], scale=inv_sigma[:, 0:1]).then_inc(gin_relu, 1)
            act.wait_ge(gin_stats, NCHK + 1)
            nc.scalar.activation(bn_scale[:, :], bnmv[:, 1:2], ACT.Sqrt, bias=eps[:, :]).then_inc(gin_root, 1)
            act.wait_ge(gin_ready, 1)

        def gin_dve(dve):
            dve.wait_ge(tails[0].folded, 1)
            nc.vector.tensor_tensor(featT, featT, XT, ALU.add).then_inc(x_added, 1)
            for c in range(NCHK):
                dve.wait_ge(gin_relu, c + 1)
                nc.vector.bn_stats(bn6[:, c, :], featT[:, 512 * c:min(512 * c + 512, N)]).then_inc(gin_stats, 1)
            dve.wait_ge(gin_stats, NCHK)
            nc.vector.bn_aggr(bnmv[:, :], bn6[:, :, :].rearrange("p a b -> p (a b)")).then_inc(gin_stats, 1)
            dve.wait_ge(gin_root, 1)
            ch = Chain(dve, gin_norm)
            ch.link(nc.vector.reciprocal(bn_scale[:, :], bn_scale[:, :]))
            ch.link(nc.vector.tensor_tensor(bn_scale[:, :], bn_scale[:, :], smallT[:, 1:2], ALU.mult))
            ch.link(nc.vector.tensor_tensor(bn_shift[:, :], bn_scale[:, :], bnmv[:, 0:1], ALU.mult))
            nc.vector.tensor_tensor(bn_shift[:, :], smallT[:, 2:3], bn_shift[:, :], ALU.subtract).then_inc(gin_ready, 1)

        scores = sb("scores", [P, NB, 2 * R2])
        alpha_self = sb("alpha_self", [P, NB, R2])
        al_stage = sb("al_stage", [P, BATCH, R2])
        al_staged = sem("al_staged")
        rel_mask = sb("rel_mask", [P, SLOTS, R2], BF16)
        pair_key = sb("pair_key", [P, NB, TB])
        iota16 = sb("iota16", [P, PAIR], BF16)
        node_of = sb("node_of", [P, ACCT])
        low_col = sb("low_col", [P, 1])
        low_one = sb("low_one", [1, 1])
        neg_low = sb("neg_low", [P, 1])
        s_edge = sb("s_edge", [P, NB, TB])
        p_edge = sb("p_edge", [P, NB, TB])
        z_edge = key_w
        v_stage = sb("v_stage", [P, TB])
        kk_stage = sb("kk_stage", [P, TB])
        mask_stage = sb("mask_stage", [P, TB, R2])
        group_max = sb("group_max", [P, TB])
        masked = sb("masked", [P, TB, R2])
        rest = sb("rest", [P, TB, R2])
        ops16 = sb("ops16", [P, TB, SW], BF16)
        hot16 = sb("hot16", [P, TB, PAIR], BF16)
        hotT = sb("hotT", [P, 2, TB * P], BF16)
        out_u = sb("out_u", [P, 2, TB, SW])
        val_u = sb("val_u", [P, 2, TB, R2])
        max_u = sb("max_u", [P, 2, R2])
        U = sb("U", [P, ACCT, R2])
        D = sb("D", [P, ACCT, 3, R2])
        D_sum = sb("D_sum", [P, ACCT, R2])
        node = [sb(f"node{i}", [P, NB, R2]) for i in range(4)]
        target = sb("target", [P, ACCT, 2 * R2])
        target_rest = sb("target_rest", [P, ACCT, 2 * R2])
        target16 = sb("target16", [P, ACCT, 3 * 2 * R2], BF16)
        share16 = sb("share16", [P, ACCT, 3 * R2], BF16)
        picked = sb("picked", [P, TB, 3 * 2 * R2])
        pick_sum = sb("pick_sum", [P, TB, 2 * R2])
        dm_edge = sb("dm_edge", [P, NB, TB, 2])
        den_u = sb("den_u", [P, 2, 3, R2])
        sum_u = sb("sum_u", [P, PAIR])
        v_equal = acc[:, 0:TB * P].rearrange("p (k e) -> p k e", k=TB)
        rows16 = acc[:, TB * P:2 * TB * P].bitcast(I16).rearrange("p (h e) -> p h e", h=2)
        all16 = acc[:, 0:SLOTS * 3 * R2 // 2].bitcast(BF16).rearrange("p (k w) -> p k w", k=SLOTS)
        ring_flat = ring[:, :, :, :].rearrange("p a b c -> p (a b c)")
        all_masked = ring_flat[:, 0:SLOTS * R2].rearrange("p (k r) -> p k r", r=R2)
        all_rest = ring_flat[:, SLOTS * R2:2 * SLOTS * R2].rearrange("p (k r) -> p k r", r=R2)

        n_prep = sem("n_prep")
        low_pe = sem("low_pe")
        low_set = sem("low_set")
        extracted = sem("extracted")
        v_taken = sem("v_taken")
        kept_in = [sem(f"kept_in{h}") for h in range(2)]
        rows_in = [sem(f"rows_in{h}") for h in range(2)]
        diag = sem("diag")
        v_rows = sem("v_rows")
        eq_read = sem("eq_read")
        m_block = sem("m_block")
        m_round = sem("m_round")
        ops_ready = sem("ops_ready")
        maxed = sem("maxed")
        max_read = sem("max_read")
        self_logit = sem("self_logit")
        self_exp = sem("self_exp")
        n_chain = sem("n_chain")
        logits = sem("logits")
        exped = sem("exped")
        e_chain = sem("e_chain")
        p_ops = sem("p_ops")
        den_block = sem("den_block")
        den_round = sem("den_round")
        den_hot = [sem(f"den_hot{g}") for g in range(2)]
        den_mm = [sem(f"den_mm{g}") for g in range(2)]
        den_out = sem("den_out")
        den_done = sem("den_done")
        d_zero = sem("d_zero")
        shares = sem("shares")
        reloaded = [sem(f"reloaded{h}") for h in range(2)]
        w_block = sem("w_block")
        w_round = sem("w_round")
        w_hot = [sem(f"w_hot{g}") for g in range(2)]
        w_used = sem("w_used")
        w_out = sem("w_out")
        VB = 4
        VBANKS = -(-TB // VB)
        TILES = [(0, (TB + 1) // 2), ((TB + 1) // 2, TB)]
        A2 = passes[2]

        def thirds(ch, src_, hi, mid, lo, rest_):
            ch.link(nc.vector.tensor_copy(hi, src_))
            ch.link(nc.vector.tensor_tensor(rest_, src_, hi, ALU.subtract))
            ch.link(nc.vector.tensor_copy(mid, rest_))
            ch.link(nc.vector.tensor_tensor(lo, rest_, mid, ALU.subtract))

        def blocks_ahead(eng, body):
            with eng.Fori(0, NB // 2 - 1) as m:
                body(2 * m, 0, m, True)
                body(2 * m + 1, 1, m, True)
            body(NB - 3, 0, NB // 2 - 1, True)
            body(NB - 2, 1, NB // 2 - 1, False)
            body(NB - 1, 0, NB // 2, False)

        pick_sems = ([sem(f"pick_hot{g}") for g in range(2)], [sem(f"pick_used{g}") for g in range(2)],
                     sem("pick_out"), sem("pick_read"), sem("pick_chain"), sem("pick_zero"))

        class Pick:
            def __init__(self, i, values, table, dest):
                self.i, self.values, self.table, self.dest = i, values, table, dest
                self.width = 3 * values * R2
                self.hot, self.used, self.out, self.read, self.chain, self.zero = pick_sems
                self.before = i * NB
                self.STEPS = 6

            def rows_by(self, h, m):
                return (m + (1 + (1 + self.i) * USES[h])) * 16

            def sp(self, sp, S_):
                def load(n, h):
                    sp.dma_start(rows16[:, h, :], dst_rows[bass.ds(n * TB, TB), :].rearrange("(o k) e -> o (k e)", o=1).to_broadcast([P, TB * P])).then_inc(rows_in[h], 16)
                load(0, 0)
                load(1, 1)
                with sp.Fori(0, NB // 2 - 1) as m:
                    for h in range(2):
                        sp.wait_ge(self.hot[1], (2 * m + (self.before + h + 1)) * S_)
                        load(2 * m + (2 + h), h)
                sp.wait_ge(self.hot[1], S_ * (self.before + NB - 2))
                load(NB - 1, 0)

            def dve(self, dve, S_):
                def block(n, h, m):
                    first = dve.snap((n + self.before) * S_)
                    with dve.Fori(0, S_) as s:
                        dve.wait_ge(rows_in[h], self.rows_by(h, m))
                        for g in range(2):
                            dve.wait_ge(self.used[g], first + s)
                            nc.vector.tensor_scalar(hotT[:, g, :], rows16[:, h, :], node_of[:, bass.ds(n + 2 * s + g, 1)], None, ALU.is_equal).then_inc(self.hot[g], 1)
                blocks(dve, block)

            def pe(self, pe, S_):
                w = self.width
                def block(n, h, m):
                    first = pe.snap((n + self.before) * S_)
                    with pe.Fori(0, S_) as s:
                        c = first + s
                        for g in range(2):
                            pe.wait_ge(self.hot[g], c + 1)
                            if g == 0:
                                pe.wait_ge(self.out, c)
                                nc.tensor.matmul(bank[5][:, 0:TB * w], zeros16[:, 0:P], zeros16[:, 0:TB * w], start=True, stop=False, skip_group_check=True)
                            for k in range(TB):
                                mm = nc.tensor.matmul(bank[5][:, k * w:(k + 1) * w], hotT[:, g, k * P:(k + 1) * P],
                                                      self.table[:, bass.ds(n + 2 * s + g, 1), :].rearrange("p a w -> p (a w)"),
                                                      start=False, stop=(g == 1 and k == TB - 1), skip_group_check=True)
                            mm.then_inc(self.used[g], 1)
                blocks(pe, block)

            def act(self, act, S_):
                w = self.width
                def block(n, h, m):
                    first = act.snap((n + self.before) * S_)
                    with act.Fori(0, S_) as s:
                        c = first + s
                        act.wait_ge(self.used[1], c + 1)
                        act.wait_ge(self.read, c)
                        nc.scalar.copy(picked[:, :, 0:w], bank[5][:, 0:TB * w].rearrange("p (k w) -> p k w", k=TB)).then_inc(self.out, 1)
                blocks(act, block)

            def add(self, eng, al, S_):
                v = self.values
                pk = picked[:, :, 0:self.width].rearrange("p k (a r) -> p k a r", r=R2)
                ps_ = pick_sum[:, :, 0:v * R2]
                pr = ps_.rearrange("p k (a r) -> p k a r", r=R2)
                ch = Chain(eng, self.chain, self.STEPS)
                al.memset(self.dest[:, :, :, :], 0.0).then_inc(self.zero, 1)
                eng.wait_ge(self.zero, self.i + 1)

                def block(n, h, m):
                    first = eng.snap((n + self.before) * S_)
                    with eng.Fori(0, S_) as s:
                        c = first + s
                        ch.begin(c)
                        ch.wait()
                        eng.wait_ge(self.out, c + 1)
                        mask = rel_mask[:, bass.ds(n * TB, TB), :].rearrange("p k (a r) -> p k a r", a=1).to_broadcast([P, TB, 3 * v, R2])
                        ch.link(al.tensor_tensor(pk, pk, mask, ALU.mult))
                        ch.link(al.tensor_tensor(ps_, picked[:, :, 0:v * R2], picked[:, :, v * R2:2 * v * R2], ALU.add))
                        al.tensor_tensor(ps_, ps_, picked[:, :, 2 * v * R2:3 * v * R2], ALU.add).then_inc(self.read, 1)
                        eng.wait_ge(self.read, c + 1)
                        ch.link(al.tensor_tensor(pr[:, :, :, 0:2], pr[:, :, :, 0:2], pr[:, :, :, 2:4], ALU.add))
                        ch.link(al.tensor_tensor(pr[:, :, :, 0:1], pr[:, :, :, 0:1], pr[:, :, :, 1:2], ALU.add))
                        got = self.dest[:, bass.ds(n, 1), :, :].rearrange("p o k v -> p (o k) v")
                        ch.did(al.tensor_tensor(got, got, pr[:, :, :, 0], ALU.add))
                        ch.k += 1
                        eng.sem_inc(self.chain, 1)
                blocks(eng, block)
                eng.wait_ge(self.chain, S_ * ((self.before + NB) * self.STEPS))

        picks = [Pick(0, 2, target16, dm_edge), Pick(1, 1, share16, z_edge[:, :, :].rearrange("p b (k o) -> p b k o", o=1))]
        dm_pick, share_pick = picks

        def attend_sp(sp):
            S_ = sp.value_load(shifts[0:1, 0:1], min_val=1, max_val=SHIFTS)
            T_ = sp.value_load(shifts[0:1, 1:2], min_val=1, max_val=2 * SHIFTS)

            def load_keys(n, h):
                sp.dma_start(rows16[:, h, :], pair_rows[bass.ds(n * TB, TB), :].rearrange("(o k) e -> o (k e)", o=1).to_broadcast([P, TB * P])).then_inc(rows_in[h], 16)

            def keep(n, h, m):
                sp.wait_ge(A2.gathered[h], A2.gathered_by(h, m))
                sp.dma_start(kept[bass.ds(n, 1), :, :].rearrange("o p c -> (o p) c"),
                             ring[:, h, :, :].rearrange("p k g -> p (k g)")).then_inc(kept_in[h], 16)
                if not (isinstance(n, int) and n == NB - 1):
                    sp.wait_ge(eq_read, n * VBANKS)
                    load_keys(n + 1, 1 - h)
            sp.wait_ge(tails[1].folded, 1)
            sp.wait_ge(tails[1].lhs, NBATCH)
            load_keys(0, 0)
            blocks(sp, keep)
            sp.wait_ge(eq_read, NB * VBANKS)
            dm_pick.sp(sp, S_)

            sp.wait_ge(den_done, NB * S_)
            sp.wait_ge(kept_in[0], 16 * USES[0])
            sp.wait_ge(kept_in[1], 16 * USES[1])

            def load(n, h):
                sp.dma_start(ring[:, h, :, :].rearrange("p k g -> p (k g)"),
                             kept[bass.ds(n, 1), :, :].rearrange("o p c -> (o p) c")).then_inc(reloaded[h], 16)
            load(0, 0)
            load(1, 1)
            share_pick.sp(sp, S_)
            with sp.Fori(0, NB // 2 - 1) as m:
                for h in range(2):
                    sp.wait_ge(A2.summed, (2 * m + (h + 1)) * T_)
                    load(2 * m + (2 + h), h)
            sp.wait_ge(A2.summed, (NB - 2) * T_)
            load(NB - 1, 0)

        def own_rows(sp, b):
            tl = tails[2]
            sp.wait_ge(tl.folded, 1)
            sp.wait_ge(tl.normed, b)
            for j in range(BATCH):
                sp.dma_start(h_self[:, j, :, :], t2.rearrange("(r n) f -> n r f", r=R2)[bass.ds((b * BATCH + j) * P, P), :, :]).then_inc(tl.h_in, 16)

        def attend_act(act, S_, T_):
            def stage(n, h):
                nc.scalar.copy(idx_stage[:, h, :], idx[:, 2, bass.ds(n * TB, TB)]).then_inc(A2.staged[h], 1)
            act.wait_ge(tails[1].normed, NBATCH)
            stage(0, 0)
            stage(1, 1)
            act.wait_ge(low_set, 1)

            def block(n, h, m, ahead):
                act.wait_ge(A2.gathered[h], A2.gathered_by(h, m))
                act.wait_ge(v_rows, n * VBANKS)
                nc.scalar.activation(v_stage[:, :], ring[:, h, :, F], ACT.Identity, bias=neg_low[:, :]).then_inc(v_taken, 1)
                nc.scalar.copy(row(s_edge, n), ring[:, h, :, F]).then_inc(extracted, 1)
                act.wait_ge(v_taken, n + 1)
                for k in range(TB):
                    last = nc.scalar.activation(onehot[:, k, :], ident[:, :], ACT.Copy, scale=v_stage[:, k:k + 1])
                    if k % VB == VB - 1 or k == TB - 1:
                        last.then_inc(diag, 1)
                if ahead:
                    act.wait_ge(kept_in[h], (m + 1) * 16)
                    act.wait_ge(extracted, n + 1)
                    stage(n + 2, h)
            blocks_ahead(act, block)
            act.wait_ge(self_logit, 1)
            nc.scalar.activation(node[3][:, :, :], node[3][:, :, :], ACT.Exp).then_inc(self_exp, 1)
            dm_pick.act(act, S_)
            act.wait_ge(logits, 1)
            nc.scalar.activation(p_edge[:, :, :], z_edge[:, :, :], ACT.Exp).then_inc(exped, 1)

            def den_out_(n, h, m):
                first = act.snap(n * S_)
                with act.Fori(0, S_) as s:
                    c = first + s
                    act.wait_ge(den_mm[1], c + 1)
                    act.wait_ge(den_done, c)
                    nc.scalar.copy(den_u[:, :, :, :].rearrange("p a t r -> p (a t r)"), bank[6][:, 0:6 * R2]).then_inc(den_out, 1)
            blocks(act, den_out_)
            share_pick.act(act, S_)

            def sums_out(n, h, m):
                first = act.snap(n * T_)
                with act.Fori(0, T_) as t:
                    c = first + t
                    act.wait_ge(A2.summed, c + 1)
                    act.wait_ge(A2.acc_done, c)
                    nc.scalar.copy(sum_u[:, :], bank[7][:, 0:PAIR]).then_inc(w_out, 1)
            blocks(act, sums_out)

        def attend_pe(pe, S_, T_):
            pe.wait_ge(n_prep, 1)
            nc.tensor.transpose(bank[7][0:1, 0:P], low_col[:, :], ident[:, :]).then_inc(low_pe, 1)
            pe.wait_ge(n_prep, 2)
            nc.tensor.matmul(bank[7][:, P:P + 1], ones[0:1, :], low_one[:, :], start=True, stop=True).then_inc(low_pe, 1)

            def max_block(n, h, m):
                pe.wait_ge(eq_read, n * VBANKS)
                for b in range(VBANKS):
                    pe.wait_ge(diag, n * VBANKS + (b + 1))
                    for k in range(VB * b, min(VB * b + VB, TB)):
                        mm = nc.tensor.matmul(bank[b][:, (k % VB) * P:(k % VB + 1) * P], ones[:, :], onehot[:, k, :], start=True, stop=True)
                    mm.then_inc(v_rows, 1)
                first = pe.snap(n * S_)
                with pe.Fori(0, S_) as s:
                    c = first + s
                    pe.wait_ge(ops_ready, n + 1)
                    pe.wait_ge(A2.hot, c + 1)
                    pe.wait_ge(max_read, c)
                    for half in range(2):
                        for k in range(TB):
                            mm = nc.tensor.matmul(bank[6 + half][:, k * SW:(k + 1) * SW], hot16[:, k, half * P:(half + 1) * P], ops16[:, k, :], start=True, stop=True)
                    mm.then_inc(maxed, 1)
            blocks(pe, max_block)

            pe.wait_ge(n_chain, TARGET_STEPS)
            dm_pick.pe(pe, S_)

            pe.wait_ge(p_ops, 1)

            def den_block_(n, h, m):
                first = pe.snap(n * S_)
                with pe.Fori(0, S_) as s:
                    c = first + s
                    pe.wait_ge(den_out, c)
                    nc.tensor.matmul(bank[6][:, 0:6 * R2], zeros16[:, 0:P], zeros16[:, 0:6 * R2], start=True, stop=False, skip_group_check=True)
                    for g, (lo_, hi_) in enumerate(TILES):
                        pe.wait_ge(den_hot[g], c + 1)
                        for k in range(lo_, hi_):
                            for half in range(2):
                                mm = nc.tensor.matmul(bank[6][:, half * 3 * R2:(half + 1) * 3 * R2], hot16[:, k, half * P:(half + 1) * P],
                                                      all16[:, bass.ds(n * TB + k, 1), :].rearrange("p o w -> p (o w)"),
                                                      start=False, stop=(k == TB - 1 and half == 1), skip_group_check=True)
                        mm.then_inc(den_mm[g], 1)
            blocks(pe, den_block_)

            pe.wait_ge(n_chain, SHARE_STEPS)
            share_pick.pe(pe, S_)

            def sum_block(n, h, m):
                first = pe.snap(n * T_)
                with pe.Fori(0, T_) as t:
                    c = first + t
                    pe.wait_ge(reloaded[h], (m + 1) * 16)
                    pe.wait_ge(w_out, c)
                    nc.tensor.matmul(bank[7][:, 0:PAIR], zeros16[:, 0:P], zeros16[:, 0:PAIR], start=True, stop=False, skip_group_check=True)
                    for g, (lo_, hi_) in enumerate(TILES):
                        pe.wait_ge(w_hot[g], c + 1)
                        for k in range(lo_, hi_):
                            mm = nc.tensor.matmul(bank[7][:, OFF[k]:OFF[k] + P], ring[:, h, k, 0:F], onehot[:, k, :], start=False, stop=(k == TB - 1), skip_group_check=True)
                        mm.then_inc(w_used if g == 0 else A2.summed, 1)
            blocks(pe, sum_block)

        TARGET_STEPS, SHARE_STEPS = 16, 28

        def attend_dve(dve, S_, T_):
            al = nc.vector
            tl1 = tails[1]
            dve.wait_ge(tl1.ev_dve, NB)
            al.tensor_reduce(low_col[:, :], scores[:, :, 0:R2], mybir.AxisListType.XY, ALU.min).then_inc(n_prep, 1)
            al.memset(U[:, :, :], 0.0)
            al.tensor_copy(iota16[:, :], iota[:, :])
            for r in range(R2):
                al.tensor_scalar(rel_mask[:, :, r], tab[:, 3, :], float(r), None, ALU.is_equal)
            al.scalar_tensor_tensor(pair_key[:, :, :].rearrange("p b k -> p (b k)"), tab[:, 3, :], float(NPAD), tab[:, 1, :], ALU.mult, ALU.add)
            dve.wait_ge(low_pe, 1)
            al.tensor_reduce(low_one[:, :], bank[7][0:1, 0:P], AX, ALU.min).then_inc(n_prep, 1)
            dve.wait_ge(low_pe, 2)
            al.tensor_scalar(neg_low[:, :], bank[7][:, P:P + 1], -1.0, None, ALU.mult).then_inc(low_set, 1)
            dve.wait_ge(low_set, 1)

            mb = Chain(dve, m_block, 9)
            mr = Chain(dve, m_round, 9)

            def max_block(n, h, m):
                mb.begin(n)
                mb.wait()
                mb.did(al.tensor_copy(kk_stage[:, :], row(pair_key, n)))
                mb.link(al.tensor_copy(mask_stage[:, :, :], rel_mask[:, bass.ds(n * TB, TB), :]))
                dve.wait_ge(rows_in[h], (m + 1) * 16)
                for b in range(VBANKS):
                    dve.wait_ge(v_rows, n * VBANKS + (b + 1))
                    for k in range(VB * b, min(VB * b + VB, TB)):
                        last = al.scalar_tensor_tensor(v_equal[:, k, :], rows16[:, h, k * P:(k + 1) * P], kk_stage[:, k:k + 1], bank[b][:, (k % VB) * P:(k % VB + 1) * P], ALU.is_equal, ALU.mult)
                    last.then_inc(eq_read, 1)
                dve.wait_ge(eq_read, n * VBANKS + VBANKS)
                mb.link(al.tensor_reduce(group_max[:, :], v_equal, AX, ALU.max))
                mb.link(al.tensor_tensor(masked[:, :, :], mask_stage[:, :, :], group_max[:, :].rearrange("p (k o) -> p k o", o=1).to_broadcast([P, TB, R2]), ALU.mult))
                thirds(mb, masked[:, :, :], ops16[:, :, 0:R2], ops16[:, :, R2:2 * R2], ops16[:, :, 2 * R2:3 * R2], rest[:, :, :])
                mb.did(al.tensor_copy(ops16[:, :, 3 * R2:SW], mask_stage[:, :, :]))
                al.tensor_copy(key_stage[:, :], row(key0, n)).then_inc(ops_ready, 1)
                first = dve.snap(n * S_)
                with dve.Fori(0, S_) as s:
                    c = first + s
                    dve.wait_ge(ops_ready, n + 1)
                    mr.begin(c)
                    mr.wait()
                    for k in range(TB):
                        last = al.tensor_scalar(hot16[:, k, :], iota16[:, :], key_stage[:, k:k + 1], None, ALU.is_equal)
                    last.then_inc(A2.hot, 1)
                    next_window(mr, PAIR)
                    dve.wait_ge(maxed, c + 1)
                    both = psum[:, 6:8, 0:TB * SW]
                    al.tensor_copy(out_u[:, :, :, :].rearrange("p a k w -> p a (k w)"), both).then_inc(max_read, 1)
                    dve.wait_ge(max_read, c + 1)
                    mr.link(al.tensor_tensor(val_u[:, :, :, :], out_u[:, :, :, 0:R2], out_u[:, :, :, R2:2 * R2], ALU.add))
                    mr.link(al.tensor_tensor(val_u[:, :, :, :], val_u[:, :, :, :], out_u[:, :, :, 2 * R2:3 * R2], ALU.add))
                    cnt = out_u[:, :, :, 3 * R2:SW]
                    mr.link(al.tensor_scalar(cnt, cnt, 1.0, None, ALU.max))
                    mr.link(al.reciprocal(cnt, cnt))
                    mr.link(al.tensor_tensor(val_u[:, :, :, :], val_u[:, :, :, :], cnt, ALU.mult))
                    mr.link(al.tensor_reduce(max_u[:, :, :], val_u[:, :, :, :].rearrange("p a k r -> p a r k"), AX, ALU.max))
                    sums = U[:, bass.ds(n + 2 * s, 2), :]
                    mr.did(al.tensor_tensor(sums, sums, max_u[:, :, :], ALU.max))
            blocks(dve, max_block)
            dve.wait_ge(m_round, S_ * (NB * 9))

            ch = Chain(dve, n_chain)
            top, mx, _, ps_ = node
            s_n, d_n = scores[:, :, 0:R2], scores[:, :, R2:2 * R2]
            ch.link(al.tensor_tensor(top[:, :, :], U[:, 1:NB + 1, :], U[:, RING + 1:RING + NB + 1, :], ALU.max))
            ch.link(al.tensor_scalar(top[:, :, :], top[:, :, :], neg_low[:, :], None, ALU.subtract))
            ch.link(al.tensor_tensor(top[:, :, :], top[:, :, :], s_n, ALU.max))
            ch.link(al.tensor_tensor(top[:, :, :], top[:, :, :], d_n, ALU.add))
            ch.link(al.scalar_tensor_tensor(mx[:, :, :], top[:, :, :], SLOPE, top[:, :, :], ALU.mult, ALU.max))
            ch.link(al.memset(target[:, :, :], 0.0))
            for at in (1, RING + 1):
                ch.did(al.tensor_copy(target[:, at:at + NB, 0:R2], d_n))
                ch.link(al.tensor_copy(target[:, at:at + NB, R2:2 * R2], mx[:, :, :]))
            w = 2 * R2
            thirds(ch, target[:, :, :], target16[:, :, 0:w], target16[:, :, w:2 * w], target16[:, :, 2 * w:3 * w], target_rest[:, :, :])
            ch.link(al.tensor_tensor(ps_[:, :, :], s_n, d_n, ALU.add))
            ch.link(al.scalar_tensor_tensor(ps_[:, :, :], ps_[:, :, :], SLOPE, ps_[:, :, :], ALU.mult, ALU.max))
            assert ch.k == TARGET_STEPS, ch.k
            al.tensor_tensor(ps_[:, :, :], ps_[:, :, :], mx[:, :, :], ALU.subtract).then_inc(self_logit, 1)

            dm_pick.dve(dve, S_)
            dve.wait_ge(picked_all, 1)
            dve.wait_ge(kept_in[0], 16 * USES[0])
            dve.wait_ge(kept_in[1], 16 * USES[1])
            dve.wait_ge(extracted, NB)
            for g in range(2):
                dve.wait_ge(dm_pick.hot[g], S_ * NB)
            ec = Chain(dve, e_chain)
            ec.link(al.tensor_tensor(z_edge[:, :, :], s_edge[:, :, :], dm_edge[:, :, :, 0], ALU.add))
            ec.link(al.scalar_tensor_tensor(z_edge[:, :, :], z_edge[:, :, :], SLOPE, z_edge[:, :, :], ALU.mult, ALU.max))
            ec.link(al.tensor_tensor(z_edge[:, :, :], z_edge[:, :, :], dm_edge[:, :, :, 1], ALU.subtract))
            al.tensor_scalar(z_edge[:, :, :], z_edge[:, :, :], 1.0, None, ALU.min).then_inc(logits, 1)
            dve.wait_ge(exped, 1)
            ec.link(al.tensor_tensor(all_masked, rel_mask[:, :, :], p_edge[:, :, :].rearrange("p b (k o) -> p (b k) o", o=1).to_broadcast([P, SLOTS, R2]), ALU.mult))
            ec.link(al.tensor_copy(all16[:, :, 0:R2], all_masked))
            ec.link(al.tensor_tensor(all_rest, all_masked, all16[:, :, 0:R2], ALU.subtract))
            ec.link(al.tensor_copy(all16[:, :, R2:2 * R2], all_rest))
            al.tensor_tensor(all16[:, :, 2 * R2:3 * R2], all_rest, all16[:, :, R2:2 * R2], ALU.subtract).then_inc(p_ops, 1)

            db = Chain(dve, den_block, 1)
            dr = Chain(dve, den_round, 2)

            def den_block_(n, h, m):
                first = dve.snap(n * S_)
                dve.wait_ge(den_round, first * 2)
                db.begin(n)
                db.did(al.tensor_copy(key_stage[:, :], row(key0, n)))
                with dve.Fori(0, S_) as s:
                    c = first + s
                    db.wait()
                    dr.begin(c)
                    dr.wait()
                    for g, (lo_, hi_) in enumerate(TILES):
                        dve.wait_ge(den_mm[g], c)
                        for k in range(lo_, hi_):
                            last = al.tensor_scalar(hot16[:, k, :], iota16[:, :], key_stage[:, k:k + 1], None, ALU.is_equal)
                        last.then_inc(den_hot[g], 1)
                    dve.wait_ge(den_hot[1], c + 1)
                    next_window(dr, PAIR)
            blocks(dve, den_block_)
            dve.wait_ge(den_done, S_ * NB)

            dve.wait_ge(self_exp, 1)
            ch.link(al.tensor_tensor(D_sum[:, :, :], D[:, :, 0, :], D[:, :, 1, :], ALU.add))
            ch.link(al.tensor_tensor(D_sum[:, :, :], D_sum[:, :, :], D[:, :, 2, :], ALU.add))
            ch.link(al.tensor_tensor(top[:, :, :], D_sum[:, 1:NB + 1, :], D_sum[:, RING + 1:RING + NB + 1, :], ALU.add))
            ch.link(al.tensor_tensor(top[:, :, :], top[:, :, :], ps_[:, :, :], ALU.add))
            ch.link(al.reciprocal(top[:, :, :], top[:, :, :]))
            ch.did(al.tensor_tensor(alpha_self[:, :, :], ps_[:, :, :], top[:, :, :], ALU.mult))
            share = target[:, :, 0:R2]
            ch.link(al.memset(target[:, :, :], 0.0))
            ch.did(al.tensor_copy(target[:, 1:NB + 1, 0:R2], top[:, :, :]))
            ch.link(al.tensor_copy(target[:, RING + 1:RING + NB + 1, 0:R2], top[:, :, :]))
            thirds(ch, share, share16[:, :, 0:R2], share16[:, :, R2:2 * R2], share16[:, :, 2 * R2:3 * R2], target_rest[:, :, 0:R2])
            assert ch.k == SHARE_STEPS + 1, ch.k

            share_pick.dve(dve, S_)
            dve.wait_ge(picked_all, 2)
            for g in range(2):
                dve.wait_ge(share_pick.hot[g], S_ * (2 * NB))
            ec.did(al.tensor_tensor(p_edge[:, :, :], p_edge[:, :, :], z_edge[:, :, :], ALU.mult))
            al.memset(acc[:, :], 0.0).then_inc(shares, 1)
            ec.wait()

            wb = Chain(dve, w_block, 2)
            wr = Chain(dve, w_round, 2)

            def sum_block(n, h, m):
                first = dve.snap(n * T_)
                dve.wait_ge(w_round, first * 2)
                for g in range(2):
                    dve.wait_ge(w_hot[g], first)
                wb.begin(n)
                wb.did(al.tensor_copy(key_stage[:, :], row(key_win, n)))
                wb.did(al.tensor_copy(v_stage[:, :], row(p_edge, n)))
                with dve.Fori(0, T_) as t:
                    c = first + t
                    wb.wait()
                    wr.begin(c)
                    wr.wait()
                    for g, (lo_, hi_) in enumerate(TILES):
                        dve.wait_ge(w_used if g == 0 else A2.summed, c)
                        for k in range(lo_, hi_):
                            last = al.tensor_scalar(onehot[:, k, :], iota[:, 0:P], key_stage[:, k:k + 1], v_stage[:, k:k + 1], ALU.is_equal, ALU.mult)
                        last.then_inc(w_hot[g], 1)
                    dve.wait_ge(w_hot[1], c + 1)
                    next_window(wr, P)
            blocks(dve, sum_block)
            fold(dve, A2, tails[2], T_)

        picked_all = sem("picked_all")

        def attend_pool(pool, S_, T_):
            al = nc.gpsimd
            al.memset(D[:, :, :, :], 0.0).then_inc(d_zero, 1)
            dm_pick.add(pool, al, S_)
            pool.sem_inc(picked_all, 1)
            pool.wait_ge(d_zero, 1)

            def den_block_(n, h, m):
                first = pool.snap(n * S_)
                with pool.Fori(0, S_) as s:
                    c = first + s
                    pool.wait_ge(den_out, c + 1)
                    pool.wait_ge(den_done, c)
                    sums = D[:, bass.ds(n + 2 * s, 2), :, :].rearrange("p a t r -> p (a t r)")
                    al.tensor_tensor(sums, sums, den_u[:, :, :, :].rearrange("p a t r -> p (a t r)"), ALU.add).then_inc(den_done, 1)
            blocks(pool, den_block_)
            share_pick.add(pool, al, S_)
            pool.sem_inc(picked_all, 1)
            pool.wait_ge(shares, 1)

            def sum_block(n, h, m):
                first = pool.snap(n * T_)
                with pool.Fori(0, T_) as t:
                    c = first + t
                    pool.wait_ge(w_out, c + 1)
                    pool.wait_ge(A2.acc_done, c)
                    sums = acc[:, bass.ds((n + t) * P, PAIR)]
                    al.tensor_tensor(sums, sums, sum_u[:, :], ALU.add).then_inc(A2.acc_done, 1)
            blocks(pool, sum_block)

        block = ctx.enter_context(nc.Block())
        PS = passes

        @block.sync
        def _(sp):
            edge_arrays = ["src", "dst", "edge_type_2", "edge_type_4", "edge_type_8"]
            sp.wait_ge(pads_set, 1)
            full, part = (NCH - 1) * RC * P, (ROWS - 1 - (NCH - 1) * RC)
            for i, name in enumerate(edge_arrays):
                sp.dma_start(edge_rows[:, i, 0:NCH - 1, :], a[name][0:full].rearrange("(q p e) -> p q e", p=RC, e=P)).then_inc(edges_in, 16)
                sp.dma_start(edge_rows[0:part, i, NCH - 1, :], a[name][full:full + part * P].rearrange("(p e) -> p e", e=P)).then_inc(edges_in, 16)
                sp.dma_start(edge_rows[part:part + 1, i, NCH - 1, 0:REST], a[name][full + part * P:E].rearrange("(p e) -> p e", p=1)).then_inc(edges_in, 16)
            for t in range(NB):
                here = min(P, N - t * P)
                sp.dma_start(X[0:here, t, :], a["x"][t * P:t * P + here, :]).then_inc(x_in, 16)
            sp.wait_ge(rows16_set, 1)
            for i, rows in enumerate((dst_rows, pair_rows)):
                sp.dma_start(rows[LEAD:LEAD + ROWS, :].rearrange("(q p) e -> p q e", p=RC), row16[:, i, :, :]).then_inc(rows16_kept, 16)
                sp.dma_start(rows[0:LEAD, :], fill16[0:LEAD, :]).then_inc(rows16_kept, 16)
                if TRAIL:
                    sp.dma_start(rows[LEAD + ROWS:SLOTS, :], fill16[0:TRAIL, :]).then_inc(rows16_kept, 16)
            sp.wait_ge(rows16_kept, 16 * 2 * (3 if TRAIL else 2))
            for l in range(upto + 1):
                if l == 2:
                    attend_sp(sp)
                if l < 3:
                    tail_sp(sp, tails[l])
            if upto == 3:
                store_out(sp, tails[3])
            else:
                tl = tails[upto]
                sp.wait_ge(tl.x_kept, NBATCH)
                for t in range(NB):
                    here = min(P, N - t * P)
                    sp.dma_start(out[t * P:t * P + here, :], X[0:here, t, :]).then_inc(out_stored, 16)
                sp.wait_ge(out_stored, NB * 16)

        @block.gpsimd
        def _(pool):
            nc.gpsimd.iota(iota[:, :], [[1, PAIR]], base=0, channel_multiplier=0, allow_small_or_imprecise_dtypes=True).then_inc(iota_set, 1)
            nc.gpsimd.iota(prow[:, :], [[1, 1]], base=0, channel_multiplier=1, allow_small_or_imprecise_dtypes=True).then_inc(iota_set, 1)
            nc.gpsimd.iota(block_base[:, :], [[P, NB]], base=-P, channel_multiplier=0, allow_small_or_imprecise_dtypes=True).then_inc(iota_set, 1)
            nc.gpsimd.iota(node_of[:, :], [[0, 2], [P, RING]], base=-P, channel_multiplier=1, allow_small_or_imprecise_dtypes=True).then_inc(iota_set, 1)
            for l in range(upto + 1):
                if l:
                    pool.wait_ge(PS[l].ready, NB * 16)
                gather_pass(pool, PS[l])
                if l == 2:
                    S_ = pool.value_load(shifts[0:1, 0:1], min_val=1, max_val=SHIFTS)
                    T_ = pool.value_load(shifts[0:1, 1:2], min_val=1, max_val=2 * SHIFTS)
                    attend_pool(pool, S_, T_)

        @block.scalar
        def _(act):
            mats = ["L0_gnn_W1", "L0_gnn_W2", "L1_gnn_W_data", "L1_gnn_W_control", "L1_gnn_W_self", "L2_gnn_W_self", "L3_gnn_root_weight"]
            for i, name in enumerate(mats):
                act.dma_start(wraw[:, i, :], a[name]).then_inc(weights_in, 16)
            act.dma_start(wraw[:, 7:7 + R2, :], a["L2_gnn_W_rel"].rearrange("r i o -> i r o")).then_inc(weights_in, 16)
            act.dma_start(wraw[:, 7 + R2:7 + R2 + NBASE, :], a["L3_gnn_weight"].rearrange("r i o -> i r o")).then_inc(weights_in, 16)
            for i, name in enumerate(["L0_gnn_b1", "L0_gnn_gamma", "L0_gnn_beta"]):
                act.dma_start(small[i:i + 1, :], a[name].rearrange("(p n) -> p n", p=1)).then_inc(weights_in, 16)
            act.dma_start(small[3:3 + R2, :], a["L2_gnn_att_src"]).then_inc(weights_in, 16)
            act.dma_start(small[3 + R2:3 + 2 * R2, :], a["L2_gnn_att_dst"]).then_inc(weights_in, 16)
            for i, name in enumerate(["L0_gnn_b2", "L1_gnn_b_data", "L1_gnn_b_control", "L1_gnn_b_self", "L2_gnn_b_self", "L3_gnn_bias"]):
                act.dma_start(rows_b[:, i, :], a[name].rearrange("(p n) -> p n", p=1).to_broadcast([P, F])).then_inc(weights_in, 16)
            act.dma_start(rows_b[:, 6:6 + R2, :].rearrange("p a f -> p (a f)"), a["L2_gnn_b_rel"].rearrange("(p r) n -> p (r n)", p=1).to_broadcast([P, R2 * F])).then_inc(weights_in, 16)
            act.dma_start(wcomp[:, :], a["L3_gnn_w_comp"].rearrange("(p r) n -> p (r n)", p=1).to_broadcast([P, R3 * NBASE])).then_inc(weights_in, 16)

            act.wait_ge(shifts_ready, 1)
            S_ = act.value_load(shifts[0:1, 0:1], min_val=1, max_val=SHIFTS)
            T_ = act.value_load(shifts[0:1, 1:2], min_val=1, max_val=2 * SHIFTS)
            for l in range(upto + 1):
                ps = PS[l]
                if l != 2:
                    stage_indices(act, ps, T_, power_steps_act(act) if l == 0 else None)
                if l == 0:
                    power_act(act)
                    gin_act(act)
                if l == 2:
                    attend_act(act, S_, T_)
                tail_act(act, tails[l])

        @block.tensor
        def _(pe):
            prepare_pe(pe)
            pe.wait_ge(shifts_ready, 1)
            S_ = pe.value_load(shifts[0:1, 0:1], min_val=1, max_val=SHIFTS)
            T_ = pe.value_load(shifts[0:1, 1:2], min_val=1, max_val=2 * SHIFTS)
            for l in range(upto + 1):
                if l != 2:
                    sum_pass_pe(pe, PS[l], T_, power_steps_pe(pe) if l == 0 else None)
                if l == 0:
                    power_pe(pe)
                    gin_pe(pe)
                if l == 2:
                    attend_pe(pe, S_, T_)
                tail_pe(pe, tails[l])

        @block.vector
        def _(dve):
            prepare_dve(dve)
            S_ = dve.value_load(shifts[0:1, 0:1], min_val=1, max_val=SHIFTS)
            T_ = dve.value_load(shifts[0:1, 1:2], min_val=1, max_val=2 * SHIFTS)
            for l in range(upto + 1):
                if l != 2:
                    sum_pass_dve(dve, PS[l], T_, power_steps_dve(dve) if l == 0 else None)
                    fold(dve, PS[l], tails[l], T_)
                if l == 0:
                    power_dve(dve)
                    gin_dve(dve)
                if l == 2:
                    attend_dve(dve, S_, T_)
                tail_dve(dve, tails[l])


_INS = ["x", "src", "dst", "edge_type_2", "edge_type_4", "edge_type_8",
        "L0_gnn_W1", "L0_gnn_b1", "L0_gnn_gamma", "L0_gnn_beta", "L0_gnn_W2", "L0_gnn_b2",
        "L1_gnn_W_data", "L1_gnn_b_data", "L1_gnn_W_control", "L1_gnn_b_control", "L1_gnn_W_self", "L1_gnn_b_self",
        "L2_gnn_W_self", "L2_gnn_b_self", "L2_gnn_W_rel", "L2_gnn_b_rel", "L2_gnn_att_src", "L2_gnn_att_dst",
        "L3_gnn_weight", "L3_gnn_w_comp", "L3_gnn_root_weight", "L3_gnn_bias"]


def kernel(**inputs):
    import numpy as _np
    import concourse.bacc as _bacc
    from concourse import mybir as _mybir
    from concourse.bass_utils import run_bass_kernel_spmd as _run

    nc = _bacc.Bacc("TRN2", target_bir_lowering=False, num_devices=1)
    arrays, aps = {}, {}
    for name in _INS:
        value = _np.ascontiguousarray(inputs[name])
        arrays[f"in_{name}"] = value
        aps[name] = nc.dram_tensor(f"in_{name}", value.shape, _mybir.dt.from_np(value.dtype), kind="ExternalInput").ap()
    out = nc.dram_tensor("out_x", inputs["x"].shape, _mybir.dt.float32, kind="ExternalOutput").ap()
    build_gnn(nc, aps, out)
    r = _run(nc, [arrays], core_ids=[0])
    return r.results[0]["out_x"]
```

```python
from contextlib import ExitStack

import concourse.bass as bass
from concourse import mybir

ALU = mybir.AluOpType
ACT = mybir.ActivationFunctionType
F32 = mybir.dt.float32
BF16 = mybir.dt.bfloat16
I32 = mybir.dt.int32
I16 = mybir.dt.int16
AX = mybir.AxisListType.X

P = 128
EPS = 1e-05
TINY = 1e-12
SLOPE = 0.2
START = 1
POWER_STEPS = 30
POWER_HALVES = 3
POWER_PAIRS = POWER_STEPS // POWER_HALVES


class Chain:

    def __init__(self, eng, sem, steps=None):
        self.eng, self.sem, self.steps, self.base, self.k = eng, sem, steps, 0, 0

    def begin(self, round_number):
        assert self.steps is not None and self.k in (0, self.steps), (self.k, self.steps)
        self.base, self.k = round_number * self.steps, 0

    def did(self, instruction):
        self.k += 1
        instruction.then_inc(self.sem, 1)

    def wait(self):
        self.eng.wait_ge(self.sem, self.base + self.k + START)

    def link(self, instruction):
        self.did(instruction)
        self.wait()


def build_gnn(nc, a, out, upto=3):
    N, F = a["x"].shape
    E = a["src"].shape[0]
    R1, R2, R3, NBASE = 2, a["L2_gnn_W_rel"].shape[0], a["L3_gnn_w_comp"].shape[0], a["L3_gnn_weight"].shape[0]
    assert F == P
    NB = -(-N // P)
    NPAD = NB * P
    LAST = N - (NB - 1) * P
    TB = E // N
    LEAD = TB // 2
    SLOTS = NB * TB
    ROWS = -(-E // P)
    REST = E - (ROWS - 1) * P
    TRAIL = SLOTS - LEAD - ROWS
    assert 0 <= TRAIL < TB
    NCH = 4
    RC = ROWS // NCH
    assert RC * NCH == ROWS and RC <= P
    RING = NB + 1 + (NB + 1) % 2
    SHIFTS = RING // 2
    PAIR = 2 * P
    SPAN = RING * P
    ACCT = 2 * RING
    NOBODY = 1 << 20
    NOBODY16 = 30000
    OFF = [(2 * k + 1) * P // (2 * TB) + P // 2 - LEAD * P // TB for k in range(TB)]
    assert OFF[0] >= 0 and OFF[-1] + P <= PAIR
    GW = F + 4
    BATCH = 5
    NBATCH = NB // BATCH
    assert NBATCH * BATCH == NB and NB % 2 == 1
    SW = R2 * 3 + 4

    t1 = nc.dram_tensor("table1", (R1 * NPAD, F), F32).ap()
    t2 = nc.dram_tensor("table2", (R2 * NPAD, GW), F32).ap()
    t3 = nc.dram_tensor("table3", (R3 * NPAD, F), F32).ap()
    kept = nc.dram_tensor("kept_rows", (NB, P, TB * GW), F32).ap()
    dst_rows = nc.dram_tensor("dst_rows", (SLOTS, P), I16).ap()
    pair_rows = nc.dram_tensor("pair_rows", (SLOTS, P), I16).ap()

    with ExitStack() as ctx:
        def sb(name, shape, dt=F32):
            return ctx.enter_context(nc.sbuf_tensor(name, shape, dt))

        def sem(name):
            return ctx.enter_context(nc.semaphore(name))

        counters = []

        def counter(name):
            counters.append(sem(name))
            return counters[-1]

        psum = ctx.enter_context(nc.psum_tensor("psum", [P, 8, 512], F32))
        bank = [psum[:, i, :] for i in range(8)]

        X = sb("X", [P, NB, F])
        S = sb("S", [P, NB, F])
        acc = sb("acc", [P, ACCT * P])
        featT = acc[:, P:P + NPAD]
        ring = sb("ring", [P, 2, TB, GW])
        onehot = sb("onehot", [P, TB, P])
        idx_stage = sb("idx_stage", [P, 2, TB], I32)
        key_stage = sb("key_stage", [P, TB])
        iota = sb("iota", [P, PAIR])
        prow = sb("prow", [P, 1])
        ident = sb("ident", [P, P])
        ones = sb("ones", [P, P])
        block_base = sb("block_base", [P, NB])
        edge_rows = ring[0:RC].rearrange("p h k g -> p (h k g)")[:, 0:5 * NCH * P].bitcast(I32).rearrange(
            "p (a q e) -> p a q e", a=5, q=NCH)
        edge_rows_f = acc[0:RC, 0:5 * NCH * P].rearrange("p (a q e) -> p a q e", a=5, q=NCH)
        edge_rows_p = acc[0:RC, 5 * NCH * P:6 * NCH * P].rearrange("p (q e) -> p q e", q=NCH)
        row16 = sb("row16", [RC, 2, NCH, P], I16)
        fill16 = sb("fill16", [max(LEAD, TRAIL), P], I16)
        tab = sb("tab", [P, 5, SLOTS])
        idx = sb("idx", [P, 4, SLOTS], I32)
        key0 = sb("key0", [P, NB, TB])
        key_win = sb("key_win", [P, NB, TB])
        key_w = sb("key_w", [P, NB, TB])
        off_row = sb("off_row", [P, TB])
        in_pair = sb("in_pair", [P, 2])
        count = sb("count", [1, 2])
        shifts = sb("shifts", [1, 2], I32)
        zeros16 = sb("zeros16", [1, 512], BF16)
        wraw = sb("wraw", [P, 7 + R2 + NBASE, F])
        wT = sb("wT", [P, 5 + R2, F])
        small = sb("small", [3 + 2 * R2, F])
        smallT = sb("smallT", [P, 3 + 2 * R2])
        rows_b = sb("rows_b", [P, 6 + R2, F])
        wcomp = sb("wcomp", [P, R3 * NBASE])
        wcat2 = sb("wcat2", [P, F + 2 * R2])
        wcat3 = sb("wcat3", [P, R3, F])
        tb = sb("tb", [P, BATCH, R3 * F])
        stg = sb("stg", [P, BATCH, F])
        y = sb("y", [P, BATCH, F])
        xn = sb("xn", [P, BATCH, F])
        xt = sb("xt", [P, BATCH, F])
        st6 = sb("st6", [P, BATCH, 6])
        mv = sb("mv", [P, BATCH, 2])
        rstd = sb("rstd", [P, BATCH])
        eps = sb("eps", [P, 1])
        u = sb("u", [P, 2])
        v = sb("v", [P, 2])
        raw = sb("raw", [P, 2])
        sq = sb("sq", [P, 2])
        nrm = sb("nrm", [P, 2])
        inv_sigma = sb("inv_sigma", [P, 2])
        NCHK = -(-N // 512)
        bn6 = sb("bn6", [P, NCHK, 6])
        bnmv = sb("bnmv", [P, 2])
        bn_scale = sb("bn_scale", [P, 1])
        bn_shift = sb("bn_shift", [P, 1])

        pads_set = sem("pads_set")
        edges_in = sem("edges_in")
        x_in = sem("x_in")
        weights_in = sem("weights_in")
        iota_set = sem("iota_set")
        v_prep = counter("v_prep")
        edges_f = sem("edges_f")
        rows16_set = sem("rows16_set")
        rows16_kept = sem("rows16_kept")
        edge_tr = sem("edge_tr")
        edge_ev = sem("edge_ev")
        ident_set = sem("ident_set")
        idx_ready = sem("idx_ready")
        match_summed = sem("match_summed")
        match_total = sem("match_total")
        shifts_ready = sem("shifts_ready")
        w_tr = sem("w_tr")
        w_ev = sem("w_ev")
        w3_chain = counter("w3_chain")
        x_tr = sem("x_tr")
        x_ev = sem("x_ev")
        x_biased = sem("x_biased")
        wa_done = sem("wa_done")
        pw_pe = sem("pw_pe")
        pw_act = sem("pw_act")
        pw_v = counter("pw_v")
        out_stored = counter("out_stored")
        dve_turn = sem("dve_turn")

        def blocks(eng, body):
            with eng.Fori(0, NB // 2) as m:
                body(2 * m, 0, m)
                body(2 * m + 1, 1, m)
            body(NB - 1, 0, NB // 2)

        def blocks_between(eng, body, steps, last):
            at = POWER_PAIRS
            with eng.Fori(0, at) as m:
                for h in range(2):
                    body(2 * m + h, h, m, lambda: steps(m * (2 * POWER_HALVES) + h * POWER_HALVES, h * POWER_HALVES))
            body(2 * at, 0, at, last)
            body(2 * at + 1, 1, at, None)
            with eng.Fori(at + 1, NB // 2) as m:
                for h in range(2):
                    body(2 * m + h, h, m, None)
            body(NB - 1, 0, NB // 2, None)

        USES = [NB - NB // 2, NB // 2]
        staged = [sem(f"staged{h}") for h in range(2)]
        gathered = [sem(f"gathered{h}") for h in range(2)]
        pool_go = sem("pool_go")

        sum_sems = [sem("hot"), counter("summed"), counter("acc_done")]
        attend_sems = [sem("max_hot"), counter("weighted"), counter("weighted_done")]
        key_staged = sem("key_staged")
        key_shift = counter("key_shift")
        acc_zero = sem("acc_zero")

        class Pass:
            def __init__(self, n, table, idx_row, width):
                self.n, self.table, self.idx_row, self.width = n, table, idx_row, width
                self.staged, self.gathered, self.go = staged, gathered, pool_go
                self.before = NB * [0, 1, 0, 2][n]
                self.hot, self.summed, self.acc_done = attend_sems if n == 2 else sum_sems
                self.key_staged, self.key_shift, self.acc_zero = key_staged, key_shift, acc_zero
                if n:
                    self.ready = counter(f"table_ready{n}")

            def staged_by(self, h, m):
                return m + (1 + self.n * USES[h])

            def gathered_by(self, h, m):
                skipped = 0 if h else LEAD
                last = isinstance(m, int) and m == USES[0] - 1
                before = self.n * (USES[h] * TB - (0 if h else LEAD + TRAIL))
                return (m + 1) * (16 * TB) + 16 * (before - skipped - (TRAIL if last else 0))

        passes = [Pass(0, a["x"], 0, F), Pass(1, t1, 1, F), Pass(2, t2, 2, GW), Pass(3, t3, 3, F)]

        def stage(ps, n, h):
            nc.scalar.copy(idx_stage[:, h, :], idx[:, ps.idx_row, bass.ds(n * TB, TB)]).then_inc(ps.staged[h], 1)

        def stage_indices(act, ps, T_, steps=None):
            def ahead(m, h, power=None):
                if power:
                    power()
                act.wait_ge(ps.summed, (2 * m + (ps.before + h + 1)) * T_ + START)
                stage(ps, 2 * m + 2 + h, h)
            at = 0
            if steps:
                at = POWER_PAIRS + 1
                with act.Fori(0, POWER_PAIRS) as m:
                    for h in range(2):
                        ahead(m, h, lambda: steps[0](m * (2 * POWER_HALVES) + h * POWER_HALVES, h * POWER_HALVES))
                ahead(POWER_PAIRS, 0, steps[1])
                ahead(POWER_PAIRS, 1)
            if at < NB // 2 - 1:
                with act.Fori(at, NB // 2 - 1) as m:
                    for h in range(2):
                        ahead(m, h)
            ahead(NB // 2 - 1, 0)

        def gather_pass(pool, ps):
            def block(n, h, m, tiles):
                pool.wait_ge(ps.staged[h], ps.staged_by(h, m))
                pool.sem_inc(ps.go, 1)
                for k in tiles:
                    pool.indirect_dma_start(
                        ring[:, h, k, 0:ps.width], None, ps.table,
                        bass.IndirectOffsetOnAxis(ap=idx_stage[:, h, k:k + 1], axis=0)).then_inc(ps.gathered[h], 16)
            block(0, 0, 0, range(LEAD, TB))
            block(1, 1, 0, range(TB))
            with pool.Fori(1, NB // 2) as m:
                block(2 * m, 0, m, range(TB))
                block(2 * m + 1, 1, m, range(TB))
            block(NB - 1, 0, NB // 2, range(TB - TRAIL))

        def window_sums(c, b, lhs, width):
            nc.tensor.matmul(bank[b][0:width, 0:PAIR], zeros16[:, 0:width], zeros16[:, 0:PAIR], start=True, stop=False, skip_group_check=True)
            for k in range(TB):
                a_, b_ = lhs(k)
                mm = nc.tensor.matmul(bank[b][0:width, OFF[k]:OFF[k] + P], a_, b_, start=False, stop=(k == TB - 1), skip_group_check=True)
            return mm

        def sum_pass_pe(pe, ps, T_, steps=None):
            def block(n, h, m, power=None):
                if power:
                    power()
                first = pe.snap((n + ps.before) * T_)
                with pe.Fori(0, T_) as t:
                    c = first + t
                    pe.wait_ge(ps.gathered[h], ps.gathered_by(h, m))
                    pe.wait_ge(ps.hot, c + 1)
                    pe.wait_ge(ps.acc_done, c + START)
                    window_sums(c, 0, lambda k: (ring[:, h, k, 0:F], onehot[:, k, :]), P).then_inc(ps.summed, 1)
            if steps:
                blocks_between(pe, block, *steps)
            else:
                blocks(pe, block)

        def all_onehots(hot):
            return nc.vector.tensor_tensor(
                hot[:, :, :], iota[:, 0:P].rearrange("p (o n) -> p o n", o=1).to_broadcast([P, TB, P]),
                key_stage[:, :].rearrange("p (k o) -> p k o", o=1).to_broadcast([P, TB, P]), ALU.is_equal)

        def next_window(chain, width):
            chain.did(nc.vector.tensor_scalar(key_stage[:, :], key_stage[:, :], float(-width), None, ALU.add))

        def sum_pass_dve(dve, ps, T_, steps=None):
            if ps.n:
                nc.vector.memset(acc[:, :], 0.0).then_inc(ps.acc_zero, 1)
            else:
                dve.wait_ge(x_ev, -(-NB // 4))
            dve.wait_ge(ps.acc_zero, ps.before // NB + 1)
            keys = Chain(dve, ps.key_shift, 1)

            def block(n, h, m, power=None):
                if power:
                    power()
                first = dve.snap((n + ps.before) * T_)
                dve.wait_ge(ps.key_shift, first + START)
                nc.vector.tensor_copy(key_stage[:, :], row(key_win, n)).then_inc(ps.key_staged, 1)
                with dve.Fori(0, T_) as t:
                    dve.wait_ge(ps.key_staged, n + (ps.before + 1))
                    keys.begin(first + t)
                    keys.wait()
                    all_onehots(onehot).then_inc(ps.hot, 1)
                    dve.wait_ge(ps.hot, first + t + 1)
                    next_window(keys, P)
                    dve.wait_ge(ps.summed, first + t + 1 + START)
                    dve.wait_ge(ps.acc_done, first + t + START)
                    sums = acc[:, bass.ds((n + t) * P, PAIR)]
                    nc.vector.tensor_tensor(sums, sums, bank[0][:, 0:PAIR], ALU.add).then_inc(ps.acc_done, 1)
            if steps:
                blocks_between(dve, block, *steps)
            else:
                blocks(dve, block)

        def row(t, n):
            return t[:, bass.ds(n, 1), :].rearrange("p a k -> p (a k)")

        class Tail:
            def __init__(self, l):
                self.l = l
                self.next = passes[l + 1] if l < 3 else None
                self.lhs = sem(f"lhs{l}")
                self.own = counter(f"own{l}")
                self.y_read = counter(f"y_read{l}")
                self.stats = sem(f"stats{l}")
                self.rooted = sem(f"rooted{l}")
                self.normed = counter(f"normed{l}")
                if l < 3:
                    self.x_kept = counter(f"x_kept{l}")
                    self.turned = counter(f"turned{l}")
                    self.turned_ev = counter(f"turned_ev{l}")
                    self.tabled = counter(f"tabled{l}")
                if l < 2:
                    self.ev_dve = counter(f"ev_dve{l}")
                if l in (1, 2):
                    self.ev_act = counter(f"ev_act{l}")
                self.chain = counter(f"tail_chain{l}")
                self.folded = sem(f"folded{l}")
                if l == 2:
                    self.h_in = [sem(f"h_in{h}") for h in range(2)]
                    self.rooted_mm = sem("root_mm")
                    self.root_read = counter("root_read")

        tails = [Tail(l) for l in range(upto + 1)]
        psA = psum[:, 0:2, :].rearrange("p a b -> p (a b)")[:, 0:BATCH * F].rearrange("p (j f) -> p j f", f=F)
        psT = psum[:, 2:4, :].rearrange("p a b -> p (a b)")[:, 0:BATCH * F].rearrange("p (j f) -> p j f", f=F)
        SETS = [[4, 5], [6, 7]]
        h_self = [t[:, at:at + BATCH * R2 * GW].rearrange("p (j r g) -> p j r g", j=BATCH, r=R2)
                  for t, at in ((ring[:, :, :, :].rearrange("p a b c -> p (a b c)"), 0), (acc, (RING + 1) * P))]

        def own_rows_by(f, parity):
            return (f + (2 - parity)) * (8 * BATCH)

        def tile_batch(t, b):
            return t[:, bass.ds(b * BATCH, BATCH), :]

        def fold(dve, ps, tl, T_):
            dve.wait_ge(ps.acc_done, (NB + ps.before) * T_ + START)
            w = BATCH * P
            for b in range(NBATCH):
                part = featT[:, b * w:(b + 1) * w]
                nc.vector.tensor_tensor(part, part, acc[:, (RING + 1) * P + b * w:(RING + 1) * P + (b + 1) * w], ALU.add).then_inc(tl.folded, 1)

        assert NBATCH % 2 == 1 and NBATCH > 2

        def tail_act(act, tl):
            l = tl.l

            def stage(f):
                act.wait_ge(tl.folded, f + 1)
                act.wait_ge(tl.own, f + START)
                src_ = featT[:, bass.ds(f * (BATCH * P), BATCH * P)]
                dst_ = stg[:, :, :].rearrange("p j f -> p (j f)")
                if l == 0:
                    nc.scalar.activation(dst_, src_, ACT.Identity, bias=bn_shift[:, :], scale=bn_scale[:, :]).then_inc(tl.lhs, 1)
                else:
                    nc.scalar.copy(dst_, src_).then_inc(tl.lhs, 1)

            def root(f):
                act.wait_ge(tl.stats, f + 1)
                nc.scalar.activation(rstd[:, :], mv[:, :, 1], ACT.Sqrt, bias=eps[:, :]).then_inc(tl.rooted, 1)

            def back(b, stage_next, root_next):
                act.wait_ge(tl.normed, b + 1 + START)
                nc.scalar.copy(tile_batch(X, b), xn[:, :, :]).then_inc(tl.x_kept, 1)
                act.wait_ge(tl.turned, b + 1 + START)
                act.wait_ge(tl.tabled, b * BATCH + START)
                nc.scalar.copy(xt[:, :, :], psT).then_inc(tl.turned_ev, 1)
                if stage_next:
                    stage(b + 2)
                if l == 0:
                    if root_next:
                        root(b + 1)
                    return
                act.wait_ge(tl.next.ready, b * (BATCH * 16) + START)
                for j in range(BATCH):
                    if root_next and j == BATCH - 1:
                        root(b + 1)
                    act.wait_ge(tl.tabled, b * BATCH + (j + 1) + START)
                    s0 = SETS[j % 2]
                    if l == 1:
                        tv = tb[:, j, 0:R2 * GW].rearrange("p (r g) -> p r g", r=R2)
                        nc.scalar.copy(tv[:, :, 0:F], bank[s0[0]].rearrange("p (r f) -> p r f", r=R2)).then_inc(tl.ev_act, 1)
                    else:
                        half = R3 // 2 * F
                        nc.scalar.copy(tb[:, j, 0:half], bank[s0[0]])
                        nc.scalar.copy(tb[:, j, half:2 * half], bank[s0[1]]).then_inc(tl.ev_act, 1)
            stage(0)
            if l == 3:
                with act.Fori(0, NBATCH - 1) as f:
                    stage(f + 1)
                    root(f)
                root(NBATCH - 1)
                return
            stage(1)
            root(0)
            with act.Fori(0, NBATCH - 2) as b:
                back(b, True, True)
            back(NBATCH - 2, False, True)
            back(NBATCH - 1, False, False)

        def tail_pe(pe, tl):
            l = tl.l

            def front(f):
                pe.wait_ge(tl.lhs, f + 1)
                pe.wait_ge(tl.y_read, f + START)
                for j in range(BATCH):
                    mm = nc.tensor.matmul(psA[:, j, :], stg[:, j, :], (wT[:, 1, :] if l == 0 else ident[:, :]), start=True, stop=True)
                mm.then_inc(tl.own, 1)

            def back(b):
                pe.wait_ge(tl.normed, b + 1 + START)
                pe.wait_ge(tl.turned_ev, b + START)
                if l == 2:
                    pe.wait_ge(tl.root_read, b + START)
                for j in range(BATCH):
                    mm = nc.tensor.transpose(psT[:, j, :], xn[:, j, :], ident[:, :])
                mm.then_inc(tl.turned, 1)
                pe.wait_ge(tl.turned_ev, b + 1 + START)
                if l == 2:
                    for j in range(BATCH):
                        mm = nc.tensor.matmul(psT[:, j, :], xt[:, j, :], wraw[:, 6, :], start=True, stop=True)
                    mm.then_inc(tl.rooted_mm, 1)
                for j in range(BATCH):
                    before = b * BATCH + (j - 1 if j >= 2 else 0)
                    if l < 2:
                        pe.wait_ge(tl.ev_dve, before + START)
                    if l > 0:
                        pe.wait_ge(tl.ev_act, before + START)
                    s0 = SETS[j % 2]
                    x_j = xt[:, j, :]
                    if l == 0:
                        mm = nc.tensor.matmul(bank[s0[0]][:, 0:3 * F], x_j, wT[:, 2:5, :].rearrange("p a f -> p (a f)"), start=True, stop=True)
                    elif l == 1:
                        nc.tensor.matmul(bank[s0[0]], x_j, wraw[:, 7:7 + R2, :].rearrange("p a f -> p (a f)"), start=True, stop=True)
                        mm = nc.tensor.matmul(bank[s0[1]][:, 0:F + 2 * R2], x_j, wcat2[:, :], start=True, stop=True)
                    else:
                        for c in range(2):
                            mm = nc.tensor.matmul(bank[s0[c]], x_j, wcat3[:, 4 * c:4 * c + 4, :].rearrange("p a f -> p (a f)"), start=True, stop=True)
                    mm.then_inc(tl.tabled, 1)
            if l == 3:
                with pe.Fori(0, NBATCH) as f:
                    front(f)
                return
            front(0)
            front(1)
            with pe.Fori(0, NBATCH - 2) as b:
                back(b)
                front(b + 2)
            back(NBATCH - 2)
            back(NBATCH - 1)

        def tail_dve(dve, tl):
            l = tl.l
            steps = {0: 2, 1: 3, 2: 2 + 1 + R2, 3: 3}[l]
            chain = Chain(dve, tl.chain, steps)
            if l > 0:
                if l < 3:
                    dve.wait_ge(tails[l - 1].ev_dve, NB + START)
                else:
                    dve.wait_ge(tails[2].root_read, NBATCH + START)
                dve.wait_ge(tails[l - 1].x_kept, NBATCH + START)
            else:
                dve.wait_ge(x_biased, 1)
            if l == 1:
                dve.wait_ge(passes[1].ready, NB * 16 + START)
                for j in range(BATCH):
                    nc.vector.memset(tb[:, j, 0:R2 * GW].rearrange("p (r g) -> p r g", r=R2)[:, :, F + 1:GW], 0.0)

            def statistics(f, parity):
                chain.begin(f)
                dve.wait_ge(tl.own, f + 1 + START)
                dve.wait_ge(tl.normed, f + START)
                if l == 0:
                    nc.vector.tensor_tensor(y[:, :, :], psA, tile_batch(X, f), ALU.add).then_inc(tl.y_read, 1)
                    dve.wait_ge(tl.y_read, f + 1 + START)
                elif l in (1, 3):
                    nc.vector.tensor_tensor(y[:, :, :], psA, tile_batch(S, f), ALU.add).then_inc(tl.y_read, 1)
                    dve.wait_ge(tl.y_read, f + 1 + START)
                    chain.link(nc.vector.scalar_tensor_tensor(y[:, :, :], y[:, :, :], 0.0, tile_batch(X, f), ALU.max, ALU.add))
                else:
                    nc.vector.tensor_tensor(y[:, :, :], psA, tile_batch(S, f), ALU.add).then_inc(tl.y_read, 1)
                    dve.wait_ge(tl.y_read, f + 1 + START)
                    chain.link(nc.vector.tensor_tensor(y[:, :, :], y[:, :, :], tile_batch(X, f), ALU.add))
                    nc.vector.tensor_copy(al_stage[:, :, :], tile_batch(alpha_self, f)).then_inc(al_staged, 1)
                    dve.wait_ge(al_staged, f + 1)
                    dve.wait_ge(tl.h_in[parity], own_rows_by(f, parity))
                    for r in range(R2):
                        for j in range(BATCH):
                            last = nc.vector.scalar_tensor_tensor(y[:, j, :], h_self[parity][:, j, r, 0:F], al_stage[:, j, r:r + 1], y[:, j, :], ALU.mult, ALU.add)
                        chain.link(last)
                for j in range(BATCH):
                    last = nc.vector.bn_stats(st6[:, j, :], y[:, j, :])
                chain.link(last)
                dve.sem_inc(dve_turn, 1)
                for j in range(BATCH):
                    last = nc.vector.bn_aggr(mv[:, j, :], st6[:, j, :])
                last.then_inc(tl.stats, 1)

            def norm(f):
                dve.wait_ge(tl.rooted, f + 1)
                chain.link(nc.vector.reciprocal(rstd[:, :], rstd[:, :]))
                if l < 3:
                    dve.wait_ge(tl.x_kept, f + START)
                    dve.wait_ge(tl.turned, f + START)
                for j in range(BATCH):
                    to = xn[:, j, :] if l < 3 else row(X, f * BATCH + j)
                    last = nc.vector.tensor_scalar(to, y[:, j, :], mv[:, j, 0:1], rstd[:, j:j + 1], ALU.subtract, ALU.mult)
                last.then_inc(tl.normed, 1)

            def own_terms(b):
                if l == 2:
                    dve.wait_ge(tl.rooted_mm, b + 1)
                    nc.vector.tensor_tensor(tile_batch(S, b), psT, rows_b[:, 5:6, :].to_broadcast([P, BATCH, F]), ALU.add).then_inc(tl.root_read, 1)
                    return
                for j in range(BATCH):
                    t = b * BATCH + j
                    dve.wait_ge(tl.tabled, t + 1 + START)
                    if l == 0:
                        if j == 0:
                            dve.wait_ge(tl.next.ready, b * (BATCH * 16) + START)
                        pst = bank[SETS[j % 2][0]]
                        nc.vector.tensor_tensor(tb[:, j, 0:2 * F], pst[:, 0:2 * F], rows_b[:, 1:3, :].rearrange("p a f -> p (a f)"), ALU.add)
                        nc.vector.tensor_tensor(row(S, t), pst[:, 2 * F:3 * F], rows_b[:, 3, :], ALU.add).then_inc(tl.ev_dve, 1)
                    elif l == 1:
                        pst = bank[SETS[j % 2][1]]
                        if j == 0:
                            dve.wait_ge(tl.next.ready, b * (BATCH * 16) + START)
                        nc.vector.tensor_copy(row(scores, t), pst[:, F:F + 2 * R2])
                        nc.vector.tensor_copy(tb[:, j, 0:R2 * GW].rearrange("p (r g) -> p r g", r=R2)[:, :, F], pst[:, F:F + R2])
                        nc.vector.tensor_tensor(row(S, t), pst[:, 0:F], rows_b[:, 4, :], ALU.add).then_inc(tl.ev_dve, 1)
            if l == 3:
                with dve.Fori(0, NBATCH) as f:
                    statistics(f, 0)
                    norm(f)
                return
            statistics(0, 0)
            norm(0)
            with dve.Fori(0, NBATCH // 2) as m:
                for k in range(2):
                    statistics(2 * m + (k + 1), 1 - k)
                    own_terms(2 * m + k)
                    norm(2 * m + (k + 1))
            own_terms(NBATCH - 1)

        def tail_sp(sp, tl):
            l = tl.l

            def store(b):
                for j in range(BATCH):
                    t = b * BATCH + j
                    if l < 2:
                        sp.wait_ge(tl.ev_dve, t + 1 + START)
                    if l > 0:
                        sp.wait_ge(tl.ev_act, t + 1 + START)
                    if l == 0:
                        dst_ = t1.rearrange("(r n) f -> n r f", r=R1)[bass.ds(t * P, P), :, :]
                        src_ = tb[:, j, 0:R1 * F].rearrange("p (r f) -> p r f", r=R1)
                    elif l == 1:
                        dst_ = t2.rearrange("(r n) f -> n r f", r=R2)[bass.ds(t * P, P), :, :]
                        src_ = tb[:, j, 0:R2 * GW].rearrange("p (r f) -> p r f", r=R2)
                    else:
                        dst_ = t3.rearrange("(r n) f -> n r f", r=R3)[bass.ds(t * P, P), :, :]
                        src_ = tb[:, j, 0:R3 * F].rearrange("p (r f) -> p r f", r=R3)
                    sp.dma_start(dst_, src_).then_inc(tl.next.ready, 16)
            if l == 2:
                own_rows(sp, 0)
                own_rows(sp, 1)
                for b in range(NBATCH):
                    if b + 2 < NBATCH:
                        own_rows(sp, b + 2)
                    store(b)
            else:
                with sp.Fori(0, NBATCH) as b:
                    store(b)

        def store_out(sp, tl):
            with sp.Fori(0, NBATCH - 1) as b:
                sp.wait_ge(tl.normed, b + 1 + START)
                for j in range(BATCH):
                    t = b * BATCH + j
                    sp.dma_start(out[bass.ds(t * P, P), :], row(X, t)).then_inc(out_stored, 16)
            sp.wait_ge(tl.normed, NBATCH + START)
            for t in range((NBATCH - 1) * BATCH, NB):
                here = min(P, N - t * P)
                sp.dma_start(out[t * P:t * P + here, :], X[0:here, t, :]).then_inc(out_stored, 16)
            sp.wait_ge(out_stored, NB * 16 + START)

        def prepare_dve(dve):
            ch = Chain(dve, v_prep)
            for i in range(5):
                nc.vector.memset(edge_rows[:, i, NCH - 1, :], NOBODY if i == 1 else 0)
                nc.vector.memset(tab[:, i, 0:LEAD], float(NOBODY) if i == 1 else 0.0)
                nc.vector.memset(tab[:, i, LEAD + ROWS:SLOTS], float(NOBODY) if i == 1 else 0.0)
            nc.vector.memset(X[:, NB - 1, :], 0.0).then_inc(pads_set, 1)
            nc.vector.memset(ones[:, :], 1.0)
            nc.vector.memset(eps[:, :], EPS)
            nc.vector.memset(u[:, :], float(P) ** -0.5)
            nc.vector.memset(zeros16[:, :], 0.0)
            nc.vector.memset(fill16[:, :], NOBODY16)
            for k in range(TB):
                last = nc.vector.memset(off_row[:, k:k + 1], float(OFF[k]))
            ch.did(last)
            dve.wait_ge(iota_set, 4)
            nc.vector.tensor_scalar(ident[:, :], iota[:, 0:P], prow[:, :], None, ALU.is_equal).then_inc(ident_set, 1)
            dve.wait_ge(edges_in, 16 * 15)
            nc.vector.tensor_copy(edge_rows_f, edge_rows[:, :, :, :]).then_inc(edges_f, 1)
            for i in range(5):
                dve.wait_ge(edge_tr, i + 1)
                last = nc.vector.tensor_copy(tab[:, i, LEAD:LEAD + ROWS], bank[i][:, 0:ROWS])
            last.then_inc(edge_ev, 1)
            dve.wait_ge(edge_ev, 1)
            nc.vector.tensor_copy(idx[:, 0, :], tab[:, 0, :])
            for i in range(1, 4):
                last = nc.vector.scalar_tensor_tensor(idx[:, i, :], tab[:, 1 + i, :], float(NPAD), tab[:, 0, :], ALU.mult, ALU.add)
            last.then_inc(idx_ready, 1)
            base = block_base[:, :].rearrange("p (b o) -> p b o", o=1).to_broadcast([P, NB, TB])
            dst_f = tab[:, 1, :].rearrange("p (b k) -> p b k", k=TB)
            ch.link(nc.vector.tensor_tensor(key_w[:, :, :], dst_f, base, ALU.subtract))
            ch.link(nc.vector.tensor_scalar(key0[:, :, :], key_w[:, :, :], 0.0, float(SPAN), ALU.is_lt, ALU.mult))
            ch.link(nc.vector.tensor_tensor(key0[:, :, :], key0[:, :, :], key_w[:, :, :], ALU.add))
            offs = off_row[:, :].rearrange("p (o k) -> p o k", o=1).to_broadcast([P, NB, TB])
            ch.link(nc.vector.tensor_tensor(key_w[:, :, :], key0[:, :, :], offs, ALU.subtract))
            ch.link(nc.vector.tensor_scalar(key_win[:, :, :], key_w[:, :, :], 0.0, float(SPAN), ALU.is_lt, ALU.mult))
            ch.link(nc.vector.tensor_tensor(key_win[:, :, :], key_win[:, :, :], key_w[:, :, :], ALU.add))
            ch.link(nc.vector.tensor_scalar(key_w[:, :, :], key0[:, :, :], float(PAIR), None, ALU.is_lt))
            ch.link(nc.vector.tensor_reduce(in_pair[:, 0:1], key_w[:, :, :].rearrange("p b k -> p (b k)"), AX, ALU.add))
            ch.link(nc.vector.tensor_scalar(key_w[:, :, :], key_win[:, :, :], float(P), None, ALU.is_lt))
            nc.vector.tensor_reduce(in_pair[:, 1:2], key_w[:, :, :].rearrange("p b k -> p (b k)"), AX, ALU.add).then_inc(match_summed, 1)
            dve.wait_ge(match_total, 1)
            for i, rounds in enumerate((SHIFTS, 2 * SHIFTS)):
                last = nc.vector.tensor_scalar(count[:, i:i + 1], bank[5][0:1, i:i + 1], float(E), float(1 - rounds), ALU.is_equal, ALU.mult)
            ch.link(last)
            for i, rounds in enumerate((SHIFTS, 2 * SHIFTS)):
                last = nc.vector.tensor_scalar(shifts[:, i:i + 1], count[:, i:i + 1], float(rounds), None, ALU.add)
            last.then_inc(shifts_ready, 1)
            dve.wait_ge(edges_f, 1)
            nc.vector.memset(ring[:, 0, 0:LEAD, :], 0.0)
            nc.vector.tensor_scalar(row16[:, 0, :, :], edge_rows_f[:, 1, :, :], float(NOBODY16), None, ALU.min)
            ch.link(nc.vector.scalar_tensor_tensor(edge_rows_p, edge_rows_f[:, 3, :, :], float(NPAD), edge_rows_f[:, 1, :, :], ALU.mult, ALU.add))
            nc.vector.tensor_scalar(row16[:, 1, :, :], edge_rows_p, float(NOBODY16), None, ALU.min).then_inc(rows16_set, 1)
            dve.wait_ge(rows16_set, 1)
            nc.vector.memset(acc[:, :], 0.0).then_inc(acc_zero, 1)
            dve.wait_ge(weights_in, 16 * WEIGHT_LOADS)
            for g in range(3):
                dve.wait_ge(w_tr, g + 1)
                n = min(4, 5 + R2 - 4 * g)
                nc.vector.tensor_copy(wT[:, 4 * g:4 * g + n, :].rearrange("p a f -> p (a f)"), bank[5 + g][:, 0:n * P])
            dve.wait_ge(w_tr, 4)
            nc.vector.tensor_copy(smallT[:, :], bank[4][:, 0:3 + 2 * R2])
            nc.vector.tensor_copy(wcat2[:, 0:F], wraw[:, 5, :]).then_inc(w_ev, 1)
            for r in range(R2):
                ch.link(nc.vector.tensor_tensor(rows_b[:, 4, :], rows_b[:, 4, :], rows_b[:, 6 + r, :], ALU.add))
            dve.wait_ge(wa_done, 1)
            nc.vector.tensor_copy(wcat2[:, F:F + 2 * R2], bank[4][:, 64:64 + 2 * R2])

        WEIGHT_LOADS = 7 + 2 + 3 + 2 + 6 + 1 + 1

        def prepare_pe(pe):
            pe.wait_ge(ident_set, 1)
            pe.wait_ge(edges_f, 1)
            for i in range(5):
                for q in range(NCH):
                    tr = nc.tensor.transpose(bank[i][:, q * RC:(q + 1) * RC], edge_rows_f[:, i, q, :], ident[0:RC, 0:RC])
                tr.then_inc(edge_tr, 1)
            pe.wait_ge(match_summed, 1)
            nc.tensor.matmul(bank[5][0:1, 0:2], ones[:, 0:1], in_pair[:, :], start=True, stop=True).then_inc(match_total, 1)
            pe.wait_ge(shifts_ready, 1)
            pe.wait_ge(weights_in, 16 * WEIGHT_LOADS)
            order = list(range(5)) + list(range(7, 7 + R2))
            for g in range(3):
                for i, w in enumerate(order[4 * g:4 * g + 4]):
                    tr = nc.tensor.transpose(bank[5 + g][:, i * P:(i + 1) * P], wraw[:, w, :], ident[:, :])
                tr.then_inc(w_tr, 1)
            nc.tensor.transpose(bank[4][:, 0:3 + 2 * R2], small[:, :], ident[0:3 + 2 * R2, 0:3 + 2 * R2]).then_inc(w_tr, 1)
            pe.wait_ge(w_ev, 1)
            for r in range(R2):
                mm = nc.tensor.matmul(bank[4][:, 64 + r:64 + r + R2 + 1:R2], wT[:, 5 + r, :], smallT[:, 3 + r:3 + r + R2 + 1:R2], start=True, stop=True)
            mm.then_inc(wa_done, 1)
            pe.wait_ge(x_in, 16 * NB)
            for g in range(-(-NB // 4)):
                if g >= 2:
                    pe.wait_ge(x_ev, g - 1)
                for i in range(min(4, NB - 4 * g)):
                    tr = nc.tensor.transpose(bank[1 + g % 2][:, i * P:(i + 1) * P], X[:, 4 * g + i, :], ident[:, :])
                tr.then_inc(x_tr, 1)

        PW = 5

        def half_pe(pe, i, odd):
            weights, vec = (wT, v) if odd else (wraw, u)
            pe.wait_ge(pw_v, i * PW + START)
            for c in range(2):
                mm = nc.tensor.matmul(bank[7][:, c:c + 1], weights[:, c, :], vec[:, c:c + 1], start=True, stop=True)
            mm.then_inc(pw_pe, 1)
            pe.wait_ge(pw_v, i * PW + 2 + START)
            nc.tensor.matmul(bank[6][:, 2:4], ones[:, :], sq[:, :], start=True, stop=True).then_inc(pw_pe, 1)

        def half_act(act, i, odd):
            act.wait_ge(pw_pe, i * 2 + 2)
            nc.scalar.activation(nrm[:, :], bank[6][:, 2:4], ACT.Sqrt).then_inc(pw_act, 1)

        def half_dve(dve, i, odd):
            dest = u if odd else v
            ch = Chain(dve, pw_v, PW)
            ch.begin(i)
            dve.wait_ge(pw_pe, i * 2 + 1)
            ch.link(nc.vector.tensor_copy(raw[:, :], bank[7][:, 0:2]))
            ch.did(nc.vector.tensor_tensor(sq[:, :], raw[:, :], raw[:, :], ALU.mult))
            dve.wait_ge(pw_act, i + 1)
            ch.link(nc.vector.tensor_scalar(nrm[:, :], nrm[:, :], TINY, None, ALU.add))
            ch.link(nc.vector.reciprocal(nrm[:, :], nrm[:, :]))
            ch.did(nc.vector.tensor_tensor(dest[:, :], raw[:, :], nrm[:, :], ALU.mult))

        def steps_of(eng, half):
            def steps(first, parity):
                for k in range(POWER_HALVES):
                    half(eng, first + k, (parity + k) % 2)
            return steps

        def power_steps_pe(pe):
            return steps_of(pe, half_pe), lambda: power_pe(pe)

        def power_steps_act(act):
            return steps_of(act, half_act), lambda: power_act(act)

        def power_steps_dve(dve):
            return steps_of(dve, half_dve), lambda: power_dve(dve)

        def power_pe(pe):
            n = 2 * POWER_STEPS
            half_pe(pe, n, 0)
            pe.wait_ge(pw_v, (n + 1) * PW + START)
            for c in range(2):
                mm = nc.tensor.matmul(bank[7][:, c:c + 1], wT[:, c, :], v[:, c:c + 1], start=True, stop=True)
            mm.then_inc(pw_pe, 1)
            pe.wait_ge(pw_v, (n + 1) * PW + 1 + START)
            nc.tensor.matmul(bank[6][:, 2:4], ones[:, :], sq[:, :], start=True, stop=True).then_inc(pw_pe, 1)

        def power_act(act):
            half_act(act, 2 * POWER_STEPS, 0)

        def power_dve(dve):
            n = 2 * POWER_STEPS
            half_dve(dve, n, 0)
            ch = Chain(dve, pw_v, PW)
            ch.begin(n + 1)
            dve.wait_ge(pw_pe, (n + 1) * 2 + 1)
            ch.did(nc.vector.tensor_tensor(sq[:, :], bank[7][:, 0:2], u[:, :], ALU.mult))
            dve.wait_ge(pw_pe, (n + 1) * 2 + 2)
            ch.link(nc.vector.reciprocal(inv_sigma[:, :], bank[6][:, 2:4]))
            nc.vector.tensor_scalar(wT[:, 1, :], wT[:, 1, :], inv_sigma[:, 1:2], None, ALU.mult).then_inc(sigma_ready, 1)
            nc.vector.tensor_tensor(X[:, :, :], X[:, :, :], rows_b[:, 0:1, :].to_broadcast([P, NB, F]), ALU.add).then_inc(x_biased, 1)

        sigma_ready = sem("sigma_ready")
        gin_mm = sem("gin_mm")
        gin_relu = sem("gin_relu")
        gin_stats = sem("gin_stats")
        gin_root = sem("gin_root")
        gin_norm = counter("gin_norm")
        gin_ready = sem("gin_ready")

        def chunks():
            return [(c, c * 512, min(512, NPAD - c * 512)) for c in range(-(-NPAD // 512))]

        def gin_pe(pe):
            for c, at, w in chunks():
                pe.wait_ge(tails[0].folded, -(-(at + w) // (BATCH * P)))
                if c >= 2:
                    pe.wait_ge(gin_relu, c - 1)
                nc.tensor.matmul(bank[1 + c % 2][:, 0:w], wT[:, 0, :], featT[:, at:at + w], start=True, stop=True).then_inc(gin_mm, 1)

        def gin_act(act):
            act.wait_ge(sigma_ready, 1)
            for c, at, w in chunks():
                act.wait_ge(gin_mm, c + 1)
                nc.scalar.activation(featT[:, at:at + w], bank[1 + c % 2][:, 0:w], ACT.Relu, bias=smallT[:, 0:1], scale=inv_sigma[:, 0:1]).then_inc(gin_relu, 1)
            act.wait_ge(gin_stats, NCHK + 1)
            nc.scalar.activation(bn_scale[:, :], bnmv[:, 1:2], ACT.Sqrt, bias=eps[:, :]).then_inc(gin_root, 1)
            act.wait_ge(gin_ready, 1)

        def gin_dve(dve):
            for c in range(NCHK):
                dve.wait_ge(gin_relu, c + 1)
                nc.vector.bn_stats(bn6[:, c, :], featT[:, 512 * c:min(512 * c + 512, N)]).then_inc(gin_stats, 1)
            dve.wait_ge(gin_stats, NCHK)
            nc.vector.bn_aggr(bnmv[:, :], bn6[:, :, :].rearrange("p a b -> p (a b)")).then_inc(gin_stats, 1)
            dve.wait_ge(gin_root, 1)
            ch = Chain(dve, gin_norm)
            ch.link(nc.vector.reciprocal(bn_scale[:, :], bn_scale[:, :]))
            ch.link(nc.vector.tensor_tensor(bn_scale[:, :], bn_scale[:, :], smallT[:, 1:2], ALU.mult))
            ch.link(nc.vector.tensor_tensor(bn_shift[:, :], bn_scale[:, :], bnmv[:, 0:1], ALU.mult))
            nc.vector.tensor_tensor(bn_shift[:, :], smallT[:, 2:3], bn_shift[:, :], ALU.subtract).then_inc(gin_ready, 1)

        scores = sb("scores", [P, NB, 2 * R2])
        alpha_self = sb("alpha_self", [P, NB, R2])
        al_stage = sb("al_stage", [P, BATCH, R2])
        al_staged = sem("al_staged")
        rel_mask = sb("rel_mask", [P, SLOTS, R2], BF16)
        pair_key = sb("pair_key", [P, NB, TB])
        iota16 = sb("iota16", [P, PAIR], BF16)
        node_of = sb("node_of", [P, ACCT])
        low_col = sb("low_col", [P, 1])
        low_one = sb("low_one", [1, 1])
        neg_low = sb("neg_low", [P, 1])
        s_edge = sb("s_edge", [P, NB, TB])
        p_edge = sb("p_edge", [P, NB, TB])
        z_edge = key_w
        v_stage = sb("v_stage", [P, TB])
        kk_stage = sb("kk_stage", [P, TB])
        mask_stage = sb("mask_stage", [P, TB, R2])
        group_max = sb("group_max", [P, TB])
        masked = sb("masked", [P, TB, R2])
        rest = sb("rest", [P, TB, R2])
        ops16 = sb("ops16", [P, TB, SW], BF16)
        hot16 = sb("hot16", [P, TB, PAIR], BF16)
        hotT = sb("hotT", [P, 2, TB * P], BF16)
        cnt_u = sb("cnt_u", [P, 2, TB, R2])
        val_u = sb("val_u", [P, 2, TB, R2])
        max_u = sb("max_u", [P, 2, R2])
        U = sb("U", [P, ACCT, R2])
        D = sb("D", [P, ACCT, 3, R2])
        D_sum = sb("D_sum", [P, ACCT, R2])
        node = [sb(f"node{i}", [P, NB, R2]) for i in range(4)]
        target = sb("target", [P, ACCT, 2 * R2])
        target_rest = sb("target_rest", [P, ACCT, 2 * R2])
        target16 = sb("target16", [P, ACCT, 3 * 2 * R2], BF16)
        share16 = sb("share16", [P, ACCT, 3 * R2], BF16)
        picked = sb("picked", [P, TB, 3 * 2 * R2])
        pick_sum = sb("pick_sum", [P, TB, 2 * R2])
        dm_edge = sb("dm_edge", [P, NB, TB, 2])
        den_u = sb("den_u", [P, 2, 3, R2])
        sum_u = sb("sum_u", [P, PAIR])
        v_equal = acc[:, 0:TB * P].rearrange("p (k e) -> p k e", k=TB)
        rows16 = acc[:, TB * P:2 * TB * P].bitcast(I16).rearrange("p (h e) -> p h e", h=2)
        all16 = acc[:, 0:SLOTS * 3 * R2 // 2].bitcast(BF16).rearrange("p (k w) -> p k w", k=SLOTS)
        ring_flat = ring[:, :, :, :].rearrange("p a b c -> p (a b c)")
        all_masked = ring_flat[:, 0:SLOTS * R2].rearrange("p (k r) -> p k r", r=R2)
        all_rest = ring_flat[:, SLOTS * R2:2 * SLOTS * R2].rearrange("p (k r) -> p k r", r=R2)

        n_prep = sem("n_prep")
        low_pe = sem("low_pe")
        low_set = sem("low_set")
        extracted = sem("extracted")
        v_taken = sem("v_taken")
        kept_in = [sem(f"kept_in{h}") for h in range(2)]
        rows_in = [sem(f"rows_in{h}") for h in range(2)]
        diag = sem("diag")
        v_rows = counter("v_rows")
        eq_read = counter("eq_read")
        m_block = counter("m_block")
        m_round = counter("m_round")
        ops_ready = sem("ops_ready")
        maxed = sem("maxed")
        max_read = counter("max_read")
        self_logit = sem("self_logit")
        self_exp = sem("self_exp")
        n_chain = counter("n_chain")
        logits = sem("logits")
        exped = sem("exped")
        e_chain = counter("e_chain")
        p_ops = sem("p_ops")
        den_block = counter("den_block")
        den_round = counter("den_round")
        den_hot = [sem(f"den_hot{g}") for g in range(2)]
        den_mm = [counter(f"den_mm{g}") for g in range(2)]
        den_out = counter("den_out")
        den_done = counter("den_done")
        d_zero = sem("d_zero")
        acc_emptied = sem("acc_emptied")
        reloaded = [sem(f"reloaded{h}") for h in range(2)]
        w_block = counter("w_block")
        w_round = counter("w_round")
        w_hot = [counter(f"w_hot{g}") for g in range(2)]
        w_used = counter("w_used")
        w_out = counter("w_out")
        VB = 4
        VBANKS = -(-TB // VB)
        TILES = [(0, (TB + 1) // 2), ((TB + 1) // 2, TB)]
        A2 = passes[2]

        def thirds(ch, src_, hi, mid, lo, rest_):
            ch.link(nc.vector.tensor_copy(hi, src_))
            ch.link(nc.vector.tensor_tensor(rest_, src_, hi, ALU.subtract))
            ch.link(nc.vector.tensor_copy(mid, rest_))
            ch.link(nc.vector.tensor_tensor(lo, rest_, mid, ALU.subtract))

        def blocks_ahead(eng, body):
            with eng.Fori(0, NB // 2 - 1) as m:
                body(2 * m, 0, m, True)
                body(2 * m + 1, 1, m, True)
            body(NB - 3, 0, NB // 2 - 1, True)
            body(NB - 2, 1, NB // 2 - 1, False)
            body(NB - 1, 0, NB // 2, False)

        pick_sems = ([sem(f"pick_hot{g}") for g in range(2)], [counter(f"pick_used{g}") for g in range(2)],
                     counter("pick_out"), counter("pick_read"), counter("pick_chain"), sem("pick_zero"))

        class Pick:
            def __init__(self, i, values, table, dest):
                self.i, self.values, self.table, self.dest = i, values, table, dest
                self.width = 3 * values * R2
                self.hot, self.used, self.out, self.read, self.chain, self.zero = pick_sems
                self.before = i * NB
                self.STEPS = 4

            def rows_by(self, h, m):
                return (m + (1 + (1 + self.i) * USES[h])) * 16

            def sp(self, sp, S_):
                def load(n, h):
                    sp.dma_start(rows16[:, h, :], dst_rows[bass.ds(n * TB, TB), :].rearrange("(o k) e -> o (k e)", o=1).to_broadcast([P, TB * P])).then_inc(rows_in[h], 16)
                load(0, 0)
                load(1, 1)
                with sp.Fori(0, NB // 2 - 1) as m:
                    for h in range(2):
                        sp.wait_ge(self.hot[1], (2 * m + (self.before + h + 1)) * S_)
                        load(2 * m + (2 + h), h)
                sp.wait_ge(self.hot[1], S_ * (self.before + NB - 2))
                load(NB - 1, 0)

            def dve(self, dve, S_):
                pk = picked[:, :, 0:self.width].rearrange("p k (a r) -> p k a r", r=R2)

                def block(n, h, m):
                    first = dve.snap((n + self.before) * S_)
                    with dve.Fori(0, S_) as s:
                        dve.wait_ge(rows_in[h], self.rows_by(h, m))
                        for g in range(2):
                            dve.wait_ge(self.used[g], first + s + START)
                            nc.vector.tensor_scalar(hotT[:, g, :], rows16[:, h, :], node_of[:, bass.ds(n + 2 * s + g, 1)], None, ALU.is_equal).then_inc(self.hot[g], 1)
                        dve.wait_ge(self.used[1], first + s + 1 + START)
                        dve.wait_ge(self.read, first + s + START)
                        mask = rel_mask[:, bass.ds(n * TB, TB), :].rearrange("p k (a r) -> p k a r", a=1).to_broadcast([P, TB, 3 * self.values, R2])
                        nc.vector.tensor_tensor(pk, bank[5][:, 0:TB * self.width].rearrange("p (k a r) -> p k a r", k=TB, r=R2), mask, ALU.mult).then_inc(self.out, 1)
                blocks(dve, block)

            def pe(self, pe, S_):
                w = self.width
                def block(n, h, m):
                    first = pe.snap((n + self.before) * S_)
                    with pe.Fori(0, S_) as s:
                        c = first + s
                        for g in range(2):
                            pe.wait_ge(self.hot[g], c + 1)
                            if g == 0:
                                pe.wait_ge(self.out, c + START)
                                nc.tensor.matmul(bank[5][:, 0:TB * w], zeros16[:, 0:P], zeros16[:, 0:TB * w], start=True, stop=False, skip_group_check=True)
                            for k in range(TB):
                                mm = nc.tensor.matmul(bank[5][:, k * w:(k + 1) * w], hotT[:, g, k * P:(k + 1) * P],
                                                      self.table[:, bass.ds(n + 2 * s + g, 1), :].rearrange("p a w -> p (a w)"),
                                                      start=False, stop=(g == 1 and k == TB - 1), skip_group_check=True)
                            mm.then_inc(self.used[g], 1)
                blocks(pe, block)

            def add(self, eng, al, S_):
                v = self.values
                ps_ = pick_sum[:, :, 0:v * R2]
                pr = ps_.rearrange("p k (a r) -> p k a r", r=R2)
                ch = Chain(eng, self.chain, self.STEPS)
                al.memset(self.dest[:, :, :, :], 0.0).then_inc(self.zero, 1)
                eng.wait_ge(self.zero, self.i + 1)

                def block(n, h, m):
                    first = eng.snap((n + self.before) * S_)
                    with eng.Fori(0, S_) as s:
                        c = first + s
                        ch.begin(c)
                        ch.wait()
                        eng.wait_ge(self.out, c + 1 + START)
                        ch.link(al.tensor_tensor(ps_, picked[:, :, 0:v * R2], picked[:, :, v * R2:2 * v * R2], ALU.add))
                        al.tensor_tensor(ps_, ps_, picked[:, :, 2 * v * R2:3 * v * R2], ALU.add).then_inc(self.read, 1)
                        eng.wait_ge(self.read, c + 1 + START)
                        ch.link(al.tensor_tensor(pr[:, :, :, 0:2], pr[:, :, :, 0:2], pr[:, :, :, 2:4], ALU.add))
                        ch.link(al.tensor_tensor(pr[:, :, :, 0:1], pr[:, :, :, 0:1], pr[:, :, :, 1:2], ALU.add))
                        got = self.dest[:, bass.ds(n, 1), :, :].rearrange("p o k v -> p (o k) v")
                        ch.did(al.tensor_tensor(got, got, pr[:, :, :, 0], ALU.add))
                blocks(eng, block)
                eng.wait_ge(self.chain, S_ * ((self.before + NB) * self.STEPS) + START)

        picks = [Pick(0, 2, target16, dm_edge), Pick(1, 1, share16, z_edge[:, :, :].rearrange("p b (k o) -> p b k o", o=1))]
        dm_pick, share_pick = picks

        def attend_sp(sp):
            S_ = sp.value_load(shifts[0:1, 0:1], min_val=1, max_val=SHIFTS)
            T_ = sp.value_load(shifts[0:1, 1:2], min_val=1, max_val=2 * SHIFTS)

            def load_keys(n, h):
                sp.dma_start(rows16[:, h, :], pair_rows[bass.ds(n * TB, TB), :].rearrange("(o k) e -> o (k e)", o=1).to_broadcast([P, TB * P])).then_inc(rows_in[h], 16)

            def keep(n, h, m):
                sp.wait_ge(A2.gathered[h], A2.gathered_by(h, m))
                sp.dma_start(kept[bass.ds(n, 1), :, :].rearrange("o p c -> (o p) c"),
                             ring[:, h, :, :].rearrange("p k g -> p (k g)")).then_inc(kept_in[h], 16)
                if not (isinstance(n, int) and n == NB - 1):
                    sp.wait_ge(eq_read, n * VBANKS + START)
                    load_keys(n + 1, 1 - h)
            sp.wait_ge(tails[1].folded, NBATCH)
            sp.wait_ge(tails[1].lhs, NBATCH)
            load_keys(0, 0)
            blocks(sp, keep)
            sp.wait_ge(eq_read, NB * VBANKS + START)
            dm_pick.sp(sp, S_)

            sp.wait_ge(den_done, NB * S_ + START)
            sp.wait_ge(kept_in[0], 16 * USES[0])
            sp.wait_ge(kept_in[1], 16 * USES[1])

            def load(n, h):
                sp.dma_start(ring[:, h, :, :].rearrange("p k g -> p (k g)"),
                             kept[bass.ds(n, 1), :, :].rearrange("o p c -> (o p) c")).then_inc(reloaded[h], 16)
            load(0, 0)
            load(1, 1)
            share_pick.sp(sp, S_)
            with sp.Fori(0, NB // 2 - 1) as m:
                for h in range(2):
                    sp.wait_ge(A2.summed, (2 * m + (h + 1)) * T_ + START)
                    load(2 * m + (2 + h), h)
            sp.wait_ge(A2.summed, (NB - 2) * T_ + START)
            load(NB - 1, 0)

        def own_rows(sp, f):
            tl = tails[2]
            sp.wait_ge(tl.folded, NBATCH)
            if f >= 2:
                sp.wait_ge(tl.normed, f - 1 + START)
            for j in range(BATCH):
                sp.dma_start(h_self[f % 2][:, j, :, :], t2.rearrange("(r n) f -> n r f", r=R2)[(f * BATCH + j) * P:(f * BATCH + j + 1) * P, :, :]).then_inc(tl.h_in[f % 2], 16)

        def attend_act(act, S_, T_):
            def stage(n, h):
                nc.scalar.copy(idx_stage[:, h, :], idx[:, 2, bass.ds(n * TB, TB)]).then_inc(A2.staged[h], 1)
            act.wait_ge(tails[1].normed, NBATCH + START)
            stage(0, 0)
            stage(1, 1)
            act.wait_ge(low_set, 1)

            def block(n, h, m, ahead):
                act.wait_ge(A2.gathered[h], A2.gathered_by(h, m))
                act.wait_ge(v_rows, n * VBANKS + START)
                nc.scalar.activation(v_stage[:, :], ring[:, h, :, F], ACT.Identity, bias=neg_low[:, :]).then_inc(v_taken, 1)
                nc.scalar.copy(row(s_edge, n), ring[:, h, :, F]).then_inc(extracted, 1)
                act.wait_ge(v_taken, n + 1)
                for k in range(TB):
                    last = nc.scalar.activation(onehot[:, k, :], ident[:, :], ACT.Copy, scale=v_stage[:, k:k + 1])
                    if k % VB == VB - 1 or k == TB - 1:
                        last.then_inc(diag, 1)
                if ahead:
                    act.wait_ge(kept_in[h], (m + 1) * 16)
                    act.wait_ge(extracted, n + 1)
                    stage(n + 2, h)
            blocks_ahead(act, block)
            act.wait_ge(self_logit, 1)
            nc.scalar.activation(node[3][:, :, :], node[3][:, :, :], ACT.Exp).then_inc(self_exp, 1)
            act.wait_ge(logits, 1)
            nc.scalar.activation(p_edge[:, :, :], z_edge[:, :, :], ACT.Exp).then_inc(exped, 1)

            def den_out_(n, h, m):
                first = act.snap(n * S_)
                with act.Fori(0, S_) as s:
                    c = first + s
                    act.wait_ge(den_mm[1], c + 1 + START)
                    act.wait_ge(den_done, c + START)
                    nc.scalar.copy(den_u[:, :, :, :].rearrange("p a t r -> p (a t r)"), bank[6][:, 0:6 * R2]).then_inc(den_out, 1)
            blocks(act, den_out_)
            act.wait_ge(den_done, S_ * NB + START)
            for lo_, hi_ in ((0, TB * P), (2 * TB * P, ACCT * P)):
                last = nc.scalar.activation(acc[:, lo_:hi_], iota[:, 0:1].to_broadcast([P, hi_ - lo_]), ACT.Copy, scale=0.0)
            last.then_inc(acc_emptied, 1)

            def sums_out(n, h, m):
                first = act.snap(n * T_)
                with act.Fori(0, T_) as t:
                    c = first + t
                    act.wait_ge(A2.summed, c + 1 + START)
                    act.wait_ge(A2.acc_done, c + START)
                    nc.scalar.copy(sum_u[:, :], bank[7][:, 0:PAIR]).then_inc(w_out, 1)
            blocks(act, sums_out)

        def attend_pe(pe, S_, T_):
            pe.wait_ge(n_prep, 1)
            nc.tensor.transpose(bank[7][0:1, 0:P], low_col[:, :], ident[:, :]).then_inc(low_pe, 1)
            pe.wait_ge(n_prep, 2)
            nc.tensor.matmul(bank[7][:, P:P + 1], ones[0:1, :], low_one[:, :], start=True, stop=True).then_inc(low_pe, 1)

            def max_block(n, h, m):
                pe.wait_ge(eq_read, n * VBANKS + START)
                for b in range(VBANKS):
                    pe.wait_ge(diag, n * VBANKS + (b + 1))
                    for k in range(VB * b, min(VB * b + VB, TB)):
                        mm = nc.tensor.matmul(bank[b][:, (k % VB) * P:(k % VB + 1) * P], ones[:, :], onehot[:, k, :], start=True, stop=True)
                    mm.then_inc(v_rows, 1)
                first = pe.snap(n * S_)
                with pe.Fori(0, S_) as s:
                    c = first + s
                    pe.wait_ge(ops_ready, n + 1)
                    pe.wait_ge(A2.hot, c + 1)
                    pe.wait_ge(max_read, c + START)
                    for half in range(2):
                        for k in range(TB):
                            mm = nc.tensor.matmul(bank[6 + half][:, k * SW:(k + 1) * SW], hot16[:, k, half * P:(half + 1) * P], ops16[:, k, :], start=True, stop=True)
                    mm.then_inc(maxed, 1)
            blocks(pe, max_block)

            pe.wait_ge(n_chain, TARGET_STEPS + START)
            dm_pick.pe(pe, S_)

            pe.wait_ge(p_ops, 1)

            def den_block_(n, h, m):
                first = pe.snap(n * S_)
                with pe.Fori(0, S_) as s:
                    c = first + s
                    pe.wait_ge(den_out, c + START)
                    nc.tensor.matmul(bank[6][:, 0:6 * R2], zeros16[:, 0:P], zeros16[:, 0:6 * R2], start=True, stop=False, skip_group_check=True)
                    for g, (lo_, hi_) in enumerate(TILES):
                        pe.wait_ge(den_hot[g], c + 1)
                        for k in range(lo_, hi_):
                            for half in range(2):
                                mm = nc.tensor.matmul(bank[6][:, half * 3 * R2:(half + 1) * 3 * R2], hot16[:, k, half * P:(half + 1) * P],
                                                      all16[:, bass.ds(n * TB + k, 1), :].rearrange("p o w -> p (o w)"),
                                                      start=False, stop=(k == TB - 1 and half == 1), skip_group_check=True)
                        mm.then_inc(den_mm[g], 1)
            blocks(pe, den_block_)

            pe.wait_ge(n_chain, SHARE_STEPS + START)
            share_pick.pe(pe, S_)

            def sum_block(n, h, m):
                first = pe.snap(n * T_)
                with pe.Fori(0, T_) as t:
                    c = first + t
                    pe.wait_ge(reloaded[h], (m + 1) * 16)
                    pe.wait_ge(w_out, c + START)
                    nc.tensor.matmul(bank[7][:, 0:PAIR], zeros16[:, 0:P], zeros16[:, 0:PAIR], start=True, stop=False, skip_group_check=True)
                    for g, (lo_, hi_) in enumerate(TILES):
                        pe.wait_ge(w_hot[g], c + 1 + START)
                        for k in range(lo_, hi_):
                            mm = nc.tensor.matmul(bank[7][:, OFF[k]:OFF[k] + P], ring[:, h, k, 0:F], onehot[:, k, :], start=False, stop=(k == TB - 1), skip_group_check=True)
                        mm.then_inc(w_used if g == 0 else A2.summed, 1)
            blocks(pe, sum_block)

        TARGET_STEPS, SHARE_STEPS = 16, 28

        def attend_dve(dve, S_, T_):
            al = nc.vector
            tl1 = tails[1]
            dve.wait_ge(tl1.ev_dve, NB + START)
            al.tensor_reduce(low_col[:, :], scores[:, :, 0:R2], mybir.AxisListType.XY, ALU.min).then_inc(n_prep, 1)
            al.memset(U[:, :, :], 0.0)
            al.tensor_copy(iota16[:, :], iota[:, :])
            for r in range(R2):
                al.tensor_scalar(rel_mask[:, :, r], tab[:, 3, :], float(r), None, ALU.is_equal)
            al.scalar_tensor_tensor(pair_key[:, :, :].rearrange("p b k -> p (b k)"), tab[:, 3, :], float(NPAD), tab[:, 1, :], ALU.mult, ALU.add)
            dve.wait_ge(low_pe, 1)
            al.tensor_reduce(low_one[:, :], bank[7][0:1, 0:P], AX, ALU.min).then_inc(n_prep, 1)
            dve.wait_ge(low_pe, 2)
            al.tensor_scalar(neg_low[:, :], bank[7][:, P:P + 1], -1.0, None, ALU.mult).then_inc(low_set, 1)
            dve.wait_ge(low_set, 1)

            w3 = Chain(dve, w3_chain)
            for k in range(NBASE):
                for r in range(R3):
                    w = wcomp[:, r * NBASE + k:r * NBASE + k + 1]
                    base_k = wraw[:, 7 + R2 + k, :]
                    if k == 0:
                        last = nc.vector.tensor_scalar(wcat3[:, r, :], base_k, w, None, ALU.mult)
                    else:
                        last = nc.vector.scalar_tensor_tensor(wcat3[:, r, :], base_k, w, wcat3[:, r, :], ALU.mult, ALU.add)
                w3.link(last)

            mb = Chain(dve, m_block, 9)
            mr = Chain(dve, m_round, 6)

            def max_block(n, h, m):
                mb.begin(n)
                mb.wait()
                mb.did(al.tensor_copy(kk_stage[:, :], row(pair_key, n)))
                mb.link(al.tensor_copy(mask_stage[:, :, :], rel_mask[:, bass.ds(n * TB, TB), :]))
                dve.wait_ge(rows_in[h], (m + 1) * 16)
                for b in range(VBANKS):
                    dve.wait_ge(v_rows, n * VBANKS + (b + 1) + START)
                    for k in range(VB * b, min(VB * b + VB, TB)):
                        last = al.scalar_tensor_tensor(v_equal[:, k, :], rows16[:, h, k * P:(k + 1) * P], kk_stage[:, k:k + 1], bank[b][:, (k % VB) * P:(k % VB + 1) * P], ALU.is_equal, ALU.mult)
                    last.then_inc(eq_read, 1)
                dve.wait_ge(eq_read, n * VBANKS + VBANKS + START)
                mb.link(al.tensor_reduce(group_max[:, :], v_equal, AX, ALU.max))
                mb.link(al.tensor_tensor(masked[:, :, :], mask_stage[:, :, :], group_max[:, :].rearrange("p (k o) -> p k o", o=1).to_broadcast([P, TB, R2]), ALU.mult))
                thirds(mb, masked[:, :, :], ops16[:, :, 0:R2], ops16[:, :, R2:2 * R2], ops16[:, :, 2 * R2:3 * R2], rest[:, :, :])
                mb.did(al.tensor_copy(ops16[:, :, 3 * R2:SW], mask_stage[:, :, :]))
                al.tensor_copy(key_stage[:, :], row(key0, n)).then_inc(ops_ready, 1)
                first = dve.snap(n * S_)
                with dve.Fori(0, S_) as s:
                    c = first + s
                    dve.wait_ge(ops_ready, n + 1)
                    mr.begin(c)
                    mr.wait()
                    for k in range(TB):
                        last = al.tensor_scalar(hot16[:, k, :], iota16[:, :], key_stage[:, k:k + 1], None, ALU.is_equal)
                    last.then_inc(A2.hot, 1)
                    dve.wait_ge(A2.hot, c + 1)
                    next_window(mr, PAIR)
                    dve.wait_ge(maxed, c + 1)
                    both = psum[:, 6:8, 0:TB * SW].rearrange("p a (k w) -> p a k w", k=TB)
                    mr.did(al.tensor_scalar(cnt_u[:, :, :, :], both[:, :, :, 3 * R2:SW], 1.0, None, ALU.max))
                    for half in range(2):
                        last = al.tensor_reduce(val_u[:, half, :, :], both[:, half, :, 0:3 * R2].rearrange("p k (t r) -> p k r t", t=3), AX, ALU.add)
                    last.then_inc(max_read, 1)
                    mr.wait()
                    mr.did(al.reciprocal(cnt_u[:, :, :, :], cnt_u[:, :, :, :]))
                    dve.wait_ge(max_read, c + 1 + START)
                    mr.wait()
                    mr.link(al.tensor_tensor(val_u[:, :, :, :], val_u[:, :, :, :], cnt_u[:, :, :, :], ALU.mult))
                    mr.link(al.tensor_reduce(max_u[:, :, :], val_u[:, :, :, :].rearrange("p a k r -> p a r k"), AX, ALU.max))
                    sums = U[:, bass.ds(n + 2 * s, 2), :]
                    mr.did(al.tensor_tensor(sums, sums, max_u[:, :, :], ALU.max))
            blocks(dve, max_block)
            dve.wait_ge(m_round, S_ * (NB * 6) + START)

            ch = Chain(dve, n_chain)
            top, mx, _, ps_ = node
            s_n, d_n = scores[:, :, 0:R2], scores[:, :, R2:2 * R2]
            ch.link(al.tensor_tensor(top[:, :, :], U[:, 1:NB + 1, :], U[:, RING + 1:RING + NB + 1, :], ALU.max))
            ch.link(al.tensor_scalar(top[:, :, :], top[:, :, :], neg_low[:, :], None, ALU.subtract))
            ch.link(al.tensor_tensor(top[:, :, :], top[:, :, :], s_n, ALU.max))
            ch.link(al.tensor_tensor(top[:, :, :], top[:, :, :], d_n, ALU.add))
            ch.link(al.scalar_tensor_tensor(mx[:, :, :], top[:, :, :], SLOPE, top[:, :, :], ALU.mult, ALU.max))
            ch.link(al.memset(target[:, :, :], 0.0))
            for at in (1, RING + 1):
                ch.did(al.tensor_copy(target[:, at:at + NB, 0:R2], d_n))
                ch.link(al.tensor_copy(target[:, at:at + NB, R2:2 * R2], mx[:, :, :]))
            w = 2 * R2
            thirds(ch, target[:, :, :], target16[:, :, 0:w], target16[:, :, w:2 * w], target16[:, :, 2 * w:3 * w], target_rest[:, :, :])
            ch.link(al.tensor_tensor(ps_[:, :, :], s_n, d_n, ALU.add))
            ch.link(al.scalar_tensor_tensor(ps_[:, :, :], ps_[:, :, :], SLOPE, ps_[:, :, :], ALU.mult, ALU.max))
            assert ch.k == TARGET_STEPS, ch.k
            al.tensor_tensor(ps_[:, :, :], ps_[:, :, :], mx[:, :, :], ALU.subtract).then_inc(self_logit, 1)

            dm_pick.dve(dve, S_)
            dve.wait_ge(picked_all, 1)
            dve.wait_ge(kept_in[0], 16 * USES[0])
            dve.wait_ge(kept_in[1], 16 * USES[1])
            dve.wait_ge(extracted, NB)
            for g in range(2):
                dve.wait_ge(dm_pick.hot[g], S_ * NB)
            ec = Chain(dve, e_chain)
            ec.link(al.tensor_tensor(z_edge[:, :, :], s_edge[:, :, :], dm_edge[:, :, :, 0], ALU.add))
            ec.link(al.scalar_tensor_tensor(z_edge[:, :, :], z_edge[:, :, :], SLOPE, z_edge[:, :, :], ALU.mult, ALU.max))
            ec.link(al.tensor_tensor(z_edge[:, :, :], z_edge[:, :, :], dm_edge[:, :, :, 1], ALU.subtract))
            al.tensor_scalar(z_edge[:, :, :], z_edge[:, :, :], 1.0, None, ALU.min).then_inc(logits, 1)
            dve.wait_ge(exped, 1)
            ec.link(al.tensor_tensor(all_masked, rel_mask[:, :, :], p_edge[:, :, :].rearrange("p b (k o) -> p (b k) o", o=1).to_broadcast([P, SLOTS, R2]), ALU.mult))
            ec.link(al.tensor_copy(all16[:, :, 0:R2], all_masked))
            ec.link(al.tensor_tensor(all_rest, all_masked, all16[:, :, 0:R2], ALU.subtract))
            ec.link(al.tensor_copy(all16[:, :, R2:2 * R2], all_rest))
            al.tensor_tensor(all16[:, :, 2 * R2:3 * R2], all_rest, all16[:, :, R2:2 * R2], ALU.subtract).then_inc(p_ops, 1)

            db = Chain(dve, den_block, 1)
            dr = Chain(dve, den_round, 1)

            def den_block_(n, h, m):
                first = dve.snap(n * S_)
                dve.wait_ge(den_round, first + START)
                db.begin(n)
                db.did(al.tensor_copy(key_stage[:, :], row(key0, n)))
                with dve.Fori(0, S_) as s:
                    c = first + s
                    db.wait()
                    dr.begin(c)
                    dr.wait()
                    for g, (lo_, hi_) in enumerate(TILES):
                        dve.wait_ge(den_mm[g], c + START)
                        for k in range(lo_, hi_):
                            last = al.tensor_scalar(hot16[:, k, :], iota16[:, :], key_stage[:, k:k + 1], None, ALU.is_equal)
                        last.then_inc(den_hot[g], 1)
                    dve.wait_ge(den_hot[1], c + 1)
                    next_window(dr, PAIR)
            blocks(dve, den_block_)
            dve.wait_ge(den_done, S_ * NB + START)

            dve.wait_ge(self_exp, 1)
            ch.link(al.tensor_tensor(D_sum[:, :, :], D[:, :, 0, :], D[:, :, 1, :], ALU.add))
            ch.link(al.tensor_tensor(D_sum[:, :, :], D_sum[:, :, :], D[:, :, 2, :], ALU.add))
            ch.link(al.tensor_tensor(top[:, :, :], D_sum[:, 1:NB + 1, :], D_sum[:, RING + 1:RING + NB + 1, :], ALU.add))
            ch.link(al.tensor_tensor(top[:, :, :], top[:, :, :], ps_[:, :, :], ALU.add))
            ch.link(al.reciprocal(top[:, :, :], top[:, :, :]))
            ch.did(al.tensor_tensor(alpha_self[:, :, :], ps_[:, :, :], top[:, :, :], ALU.mult))
            share = target[:, :, 0:R2]
            ch.link(al.memset(target[:, :, :], 0.0))
            ch.did(al.tensor_copy(target[:, 1:NB + 1, 0:R2], top[:, :, :]))
            ch.link(al.tensor_copy(target[:, RING + 1:RING + NB + 1, 0:R2], top[:, :, :]))
            thirds(ch, share, share16[:, :, 0:R2], share16[:, :, R2:2 * R2], share16[:, :, 2 * R2:3 * R2], target_rest[:, :, 0:R2])
            assert ch.k == SHARE_STEPS + 1, ch.k

            share_pick.dve(dve, S_)
            dve.wait_ge(picked_all, 2)
            for g in range(2):
                dve.wait_ge(share_pick.hot[g], S_ * (2 * NB))
            ec.did(al.tensor_tensor(p_edge[:, :, :], p_edge[:, :, :], z_edge[:, :, :], ALU.mult))
            al.memset(acc[:, TB * P:2 * TB * P], 0.0).then_inc(acc_emptied, 1)
            ec.wait()

            wb = Chain(dve, w_block, 2)
            wr = Chain(dve, w_round, 1)

            def sum_block(n, h, m):
                first = dve.snap(n * T_)
                dve.wait_ge(w_round, first + START)
                for g in range(2):
                    dve.wait_ge(w_hot[g], first + START)
                wb.begin(n)
                wb.did(al.tensor_copy(key_stage[:, :], row(key_win, n)))
                wb.did(al.tensor_copy(v_stage[:, :], row(p_edge, n)))
                with dve.Fori(0, T_) as t:
                    c = first + t
                    wb.wait()
                    wr.begin(c)
                    wr.wait()
                    for g, (lo_, hi_) in enumerate(TILES):
                        dve.wait_ge(w_used if g == 0 else A2.summed, c + START)
                        for k in range(lo_, hi_):
                            last = al.tensor_scalar(onehot[:, k, :], iota[:, 0:P], key_stage[:, k:k + 1], v_stage[:, k:k + 1], ALU.is_equal, ALU.mult)
                        last.then_inc(w_hot[g], 1)
                    dve.wait_ge(w_hot[1], c + 1 + START)
                    next_window(wr, P)
            blocks(dve, sum_block)
            fold(dve, A2, tails[2], T_)

        picked_all = sem("picked_all")

        def attend_pool(pool, S_, T_):
            al = nc.gpsimd
            al.memset(D[:, :, :, :], 0.0).then_inc(d_zero, 1)
            dm_pick.add(pool, al, S_)
            pool.sem_inc(picked_all, 1)
            pool.wait_ge(d_zero, 1)

            def den_block_(n, h, m):
                first = pool.snap(n * S_)
                with pool.Fori(0, S_) as s:
                    c = first + s
                    pool.wait_ge(den_out, c + 1 + START)
                    pool.wait_ge(den_done, c + START)
                    sums = D[:, bass.ds(n + 2 * s, 2), :, :].rearrange("p a t r -> p (a t r)")
                    al.tensor_tensor(sums, sums, den_u[:, :, :, :].rearrange("p a t r -> p (a t r)"), ALU.add).then_inc(den_done, 1)
            blocks(pool, den_block_)
            share_pick.add(pool, al, S_)
            pool.sem_inc(picked_all, 1)
            pool.wait_ge(acc_emptied, 2)

            def sum_block(n, h, m):
                first = pool.snap(n * T_)
                with pool.Fori(0, T_) as t:
                    c = first + t
                    pool.wait_ge(w_out, c + 1 + START)
                    pool.wait_ge(A2.acc_done, c + START)
                    sums = acc[:, bass.ds((n + t) * P, PAIR)]
                    al.tensor_tensor(sums, sums, sum_u[:, :], ALU.add).then_inc(A2.acc_done, 1)
            blocks(pool, sum_block)

        block = ctx.enter_context(nc.Block())
        PS = passes

        @block.sync
        def _(sp):
            edge_arrays = ["src", "dst", "edge_type_2", "edge_type_4", "edge_type_8"]
            sp.wait_ge(pads_set, 1)
            full, part = (NCH - 1) * RC * P, (ROWS - 1 - (NCH - 1) * RC)
            for i, name in enumerate(edge_arrays):
                sp.dma_start(edge_rows[:, i, 0:NCH - 1, :], a[name][0:full].rearrange("(q p e) -> p q e", p=RC, e=P)).then_inc(edges_in, 16)
                sp.dma_start(edge_rows[0:part, i, NCH - 1, :], a[name][full:full + part * P].rearrange("(p e) -> p e", e=P)).then_inc(edges_in, 16)
                sp.dma_start(edge_rows[part:part + 1, i, NCH - 1, 0:REST], a[name][full + part * P:E].rearrange("(p e) -> p e", p=1)).then_inc(edges_in, 16)
            for t in range(NB):
                here = min(P, N - t * P)
                sp.dma_start(X[0:here, t, :], a["x"][t * P:t * P + here, :]).then_inc(x_in, 16)
            sp.wait_ge(rows16_set, 1)
            for i, rows in enumerate((dst_rows, pair_rows)):
                sp.dma_start(rows[LEAD:LEAD + ROWS, :].rearrange("(q p) e -> p q e", p=RC), row16[:, i, :, :]).then_inc(rows16_kept, 16)
                sp.dma_start(rows[0:LEAD, :], fill16[0:LEAD, :]).then_inc(rows16_kept, 16)
                if TRAIL:
                    sp.dma_start(rows[LEAD + ROWS:SLOTS, :], fill16[0:TRAIL, :]).then_inc(rows16_kept, 16)
            sp.wait_ge(rows16_kept, 16 * 2 * (3 if TRAIL else 2))
            for l in range(upto + 1):
                if l == 2:
                    attend_sp(sp)
                if l < 3:
                    tail_sp(sp, tails[l])
            if upto == 3:
                store_out(sp, tails[3])
            else:
                tl = tails[upto]
                sp.wait_ge(tl.x_kept, NBATCH + START)
                for t in range(NB):
                    here = min(P, N - t * P)
                    sp.dma_start(out[t * P:t * P + here, :], X[0:here, t, :]).then_inc(out_stored, 16)
                sp.wait_ge(out_stored, NB * 16 + START)

        @block.gpsimd
        def _(pool):
            nc.gpsimd.iota(iota[:, :], [[1, PAIR]], base=0, channel_multiplier=0, allow_small_or_imprecise_dtypes=True).then_inc(iota_set, 1)
            nc.gpsimd.iota(prow[:, :], [[1, 1]], base=0, channel_multiplier=1, allow_small_or_imprecise_dtypes=True).then_inc(iota_set, 1)
            nc.gpsimd.iota(block_base[:, :], [[P, NB]], base=-P, channel_multiplier=0, allow_small_or_imprecise_dtypes=True).then_inc(iota_set, 1)
            nc.gpsimd.iota(node_of[:, :], [[0, 2], [P, RING]], base=-P, channel_multiplier=1, allow_small_or_imprecise_dtypes=True).then_inc(iota_set, 1)
            for started in counters:
                pool.sem_inc(started, START)
            for l in range(upto + 1):
                if l:
                    pool.wait_ge(PS[l].ready, NB * 16 + START)
                gather_pass(pool, PS[l])
                if l == 2:
                    S_ = pool.value_load(shifts[0:1, 0:1], min_val=1, max_val=SHIFTS)
                    T_ = pool.value_load(shifts[0:1, 1:2], min_val=1, max_val=2 * SHIFTS)
                    attend_pool(pool, S_, T_)

        @block.scalar
        def _(act):
            mats = ["L0_gnn_W1", "L0_gnn_W2", "L1_gnn_W_data", "L1_gnn_W_control", "L1_gnn_W_self", "L2_gnn_W_self", "L3_gnn_root_weight"]
            for i, name in enumerate(mats):
                act.dma_start(wraw[:, i, :], a[name]).then_inc(weights_in, 16)
            act.dma_start(wraw[:, 7:7 + R2, :], a["L2_gnn_W_rel"].rearrange("r i o -> i r o")).then_inc(weights_in, 16)
            act.dma_start(wraw[:, 7 + R2:7 + R2 + NBASE, :], a["L3_gnn_weight"].rearrange("r i o -> i r o")).then_inc(weights_in, 16)
            for i, name in enumerate(["L0_gnn_b1", "L0_gnn_gamma", "L0_gnn_beta"]):
                act.dma_start(small[i:i + 1, :], a[name].rearrange("(p n) -> p n", p=1)).then_inc(weights_in, 16)
            act.dma_start(small[3:3 + R2, :], a["L2_gnn_att_src"]).then_inc(weights_in, 16)
            act.dma_start(small[3 + R2:3 + 2 * R2, :], a["L2_gnn_att_dst"]).then_inc(weights_in, 16)
            for i, name in enumerate(["L0_gnn_b2", "L1_gnn_b_data", "L1_gnn_b_control", "L1_gnn_b_self", "L2_gnn_b_self", "L3_gnn_bias"]):
                act.dma_start(rows_b[:, i, :], a[name].rearrange("(p n) -> p n", p=1).to_broadcast([P, F])).then_inc(weights_in, 16)
            act.dma_start(rows_b[:, 6:6 + R2, :].rearrange("p a f -> p (a f)"), a["L2_gnn_b_rel"].rearrange("(p r) n -> p (r n)", p=1).to_broadcast([P, R2 * F])).then_inc(weights_in, 16)
            act.dma_start(wcomp[:, :], a["L3_gnn_w_comp"].rearrange("(p r) n -> p (r n)", p=1).to_broadcast([P, R3 * NBASE])).then_inc(weights_in, 16)

            act.wait_ge(idx_ready, 1)
            stage(PS[0], 0, 0)
            stage(PS[0], 1, 1)
            act.wait_ge(acc_zero, 1)
            for g in range(-(-NB // 4)):
                act.wait_ge(x_tr, g + 1)
                n = min(4, NB - 4 * g)
                nc.scalar.copy(featT[:, 4 * g * P:(4 * g + n) * P], bank[1 + g % 2][:, 0:n * P]).then_inc(x_ev, 1)
            act.wait_ge(shifts_ready, 1)
            S_ = act.value_load(shifts[0:1, 0:1], min_val=1, max_val=SHIFTS)
            T_ = act.value_load(shifts[0:1, 1:2], min_val=1, max_val=2 * SHIFTS)
            for l in range(upto + 1):
                ps = PS[l]
                if l in (1, 3):
                    stage(ps, 0, 0)
                    stage(ps, 1, 1)
                if l != 2:
                    stage_indices(act, ps, T_, power_steps_act(act) if l == 0 else None)
                if l == 0:
                    gin_act(act)
                if l == 2:
                    attend_act(act, S_, T_)
                tail_act(act, tails[l])

        @block.tensor
        def _(pe):
            prepare_pe(pe)
            pe.wait_ge(shifts_ready, 1)
            S_ = pe.value_load(shifts[0:1, 0:1], min_val=1, max_val=SHIFTS)
            T_ = pe.value_load(shifts[0:1, 1:2], min_val=1, max_val=2 * SHIFTS)
            for l in range(upto + 1):
                if l != 2:
                    sum_pass_pe(pe, PS[l], T_, power_steps_pe(pe) if l == 0 else None)
                if l == 0:
                    gin_pe(pe)
                if l == 2:
                    attend_pe(pe, S_, T_)
                tail_pe(pe, tails[l])

        @block.vector
        def _(dve):
            prepare_dve(dve)
            S_ = dve.value_load(shifts[0:1, 0:1], min_val=1, max_val=SHIFTS)
            T_ = dve.value_load(shifts[0:1, 1:2], min_val=1, max_val=2 * SHIFTS)
            for l in range(upto + 1):
                if l != 2:
                    sum_pass_dve(dve, PS[l], T_, power_steps_dve(dve) if l == 0 else None)
                    fold(dve, PS[l], tails[l], T_)
                if l == 0:
                    gin_dve(dve)
                if l == 2:
                    attend_dve(dve, S_, T_)
                tail_dve(dve, tails[l])


_INS = ["x", "src", "dst", "edge_type_2", "edge_type_4", "edge_type_8",
        "L0_gnn_W1", "L0_gnn_b1", "L0_gnn_gamma", "L0_gnn_beta", "L0_gnn_W2", "L0_gnn_b2",
        "L1_gnn_W_data", "L1_gnn_b_data", "L1_gnn_W_control", "L1_gnn_b_control", "L1_gnn_W_self", "L1_gnn_b_self",
        "L2_gnn_W_self", "L2_gnn_b_self", "L2_gnn_W_rel", "L2_gnn_b_rel", "L2_gnn_att_src", "L2_gnn_att_dst",
        "L3_gnn_weight", "L3_gnn_w_comp", "L3_gnn_root_weight", "L3_gnn_bias"]


def kernel(**inputs):
    import numpy as _np
    import concourse.bacc as _bacc
    from concourse import mybir as _mybir
    from concourse.bass_utils import run_bass_kernel_spmd as _run

    nc = _bacc.Bacc("TRN2", target_bir_lowering=False, num_devices=1)
    arrays, aps = {}, {}
    for name in _INS:
        value = _np.ascontiguousarray(inputs[name])
        arrays[f"in_{name}"] = value
        aps[name] = nc.dram_tensor(f"in_{name}", value.shape, _mybir.dt.from_np(value.dtype), kind="ExternalInput").ap()
    out = nc.dram_tensor("out_x", inputs["x"].shape, _mybir.dt.float32, kind="ExternalOutput").ap()
    build_gnn(nc, aps, out)
    r = _run(nc, [arrays], core_ids=[0])
    return r.results[0]["out_x"]
```
